# Optimizing a Trainium2 kernel written in Bass

```python
import numpy as np
import jax
import jax.numpy as jnp

def _softmax(x, axis=-1):
    return jax.nn.softmax(x, axis=axis)

def _gelu(x):
    return jax.nn.gelu(x, approximate=True)

def _silu(x):
    return jax.nn.silu(x)

def _sigmoid(x):
    return jax.nn.sigmoid(x)

def _layernorm(x, axis=-1, eps=1e-05):
    m = jnp.mean(x, axis=axis, keepdims=True)
    v = jnp.var(x, axis=axis, keepdims=True)
    return (x - m) / jnp.sqrt(v + eps)

def _scatter_add(tgt, idx, src, axis=0):
    return tgt.at[idx].add(src)

def _segment_sum(src, seg, n):
    return jax.ops.segment_sum(src, seg, n)
kernel_name = 'mk_xattn_ffn_d2_seqx_r4_2618ff'

def setup_inputs(seed: int=0):
    np.random.seed(seed)
    _w = jnp.asarray

    def _rec_inputs():
        import jax
        import jax.numpy as jnp
        _rk = jax.random.key(seed)
        x = 0.01048 + 0.1018 * jax.random.normal(jax.random.fold_in(_rk, 1), (4, 512, 512), jnp.float32)
        _lenS = 512 - jax.random.randint(jax.random.fold_in(_rk, 7), (4,), 0, max(1, 512 // 4) + 1, jnp.int32)
        _lenS2 = 512 - jax.random.randint(jax.random.fold_in(_rk, 8), (4,), 0, max(1, 512 // 4) + 1, jnp.int32)
        _ctx_512P = jax.random.normal(jax.random.fold_in(_rk, 11), (4, 16, 128), jnp.float32)
        _ctx_512c = jax.random.dirichlet(jax.random.fold_in(_rk, 511), 0.3 * jnp.ones((16,), jnp.float32), (4, 512))
        _ctx_512t = jnp.einsum('bsk,bkd->bsd', _ctx_512c, _ctx_512P)
        _ctx_512t = _ctx_512t * jax.lax.rsqrt(jnp.mean(jnp.square(_ctx_512t)) + 1e-12) * 0.953939
        ctx_512 = -0.000292821 + 1.00034 * (_ctx_512t + 0.3 * jax.random.normal(jax.random.fold_in(_rk, 611), (4, 512, 128), jnp.float32))
        return (x, ctx_512)
    x, ctx_512 = _rec_inputs()

    def _L0_xattn_setup():
        import jax, jax.numpy as jnp
        import numpy as np
        LRELU_ALPHA = 0.2
        MASK_VAL = -10000000000.0
        B, N, F_IN = (4, 512, 128)
        H, F_OUT = (8, 64)
        F_HID = H * F_OUT

        def gat_layer(x, adj, W, a_self, a_neigh, b):
            feat = jnp.einsum('nf,hfo->hno', x, W)
            attn_self = jnp.einsum('hno,ho->hn', feat, a_self)
            attn_neigh = jnp.einsum('hno,ho->hn', feat, a_neigh)
            e = attn_self[:, :, None] + attn_neigh[:, None, :]
            e = jax.nn.leaky_relu(e, LRELU_ALPHA)
            e = e + MASK_VAL * (1.0 - adj)[None, :, :]
            alpha = jax.nn.softmax(e, axis=-1)
            out = jnp.einsum('hnm,hmo->hno', alpha, feat) + b[:, None, :]
            out = jnp.transpose(out, (1, 0, 2)).reshape(out.shape[1], -1)
            return jax.nn.elu(out)
        key = jax.random.key(seed)
        ks = jax.random.split(key, 10)
        feats = jax.random.normal(ks[0], (B, N, F_IN), dtype=jnp.float32)
        a = (jax.random.uniform(ks[1], (B, N, N)) < 0.01).astype(jnp.float32)
        adj = jnp.maximum(a, jnp.eye(N, dtype=jnp.float32)[None])
        s0 = 1.0 / np.sqrt(F_IN)
        s1 = 1.0 / np.sqrt(F_HID)
        return {'feats': feats, 'adj': adj, 'W0': jax.random.normal(ks[2], (H, F_IN, F_OUT), dtype=jnp.float32) * s0, 'a_self0': jax.random.normal(ks[3], (H, F_OUT), dtype=jnp.float32) * 0.1, 'a_neigh0': jax.random.normal(ks[4], (H, F_OUT), dtype=jnp.float32) * 0.1, 'b0': jnp.zeros((H, F_OUT), dtype=jnp.float32), 'W1': jax.random.normal(ks[5], (H, F_HID, F_OUT), dtype=jnp.float32) * s1, 'a_self1': jax.random.normal(ks[6], (H, F_OUT), dtype=jnp.float32) * 0.1, 'a_neigh1': jax.random.normal(ks[7], (H, F_OUT), dtype=jnp.float32) * 0.1, 'b1': jnp.zeros((H, F_OUT), dtype=jnp.float32)}
    _L0_xattn_all = _L0_xattn_setup()
    _L0_xattn_in = {k: v for k, v in _L0_xattn_all.items() if k in ('W0', 'a_self0', 'a_neigh0', 'b0', 'W1', 'a_self1', 'a_neigh1', 'b1')}
    del _L0_xattn_all

    def _L0_ffn_setup():
        import jax, jax.numpy as jnp
        import numpy as np
        B, S, D = (4, 1024, 512)
        DFF = 4 * D
        SKIP = 0.125
        key = jax.random.key(seed)
        ks = jax.random.split(key, 4)
        s_in = 1.0 / np.sqrt(D).astype(np.float32)
        s_ff = 1.0 / np.sqrt(DFF).astype(np.float32)
        return {'x': jax.random.normal(ks[0], (B, S, D), jnp.float32), 'Wr': jax.random.normal(ks[1], (D, 1), jnp.float32) * s_in, 'br': jnp.zeros((1,), jnp.float32), 'W1': jax.random.normal(ks[2], (D, DFF), jnp.float32) * s_in, 'b1': jnp.zeros((DFF,), jnp.float32), 'W2': jax.random.normal(ks[3], (DFF, D), jnp.float32) * s_ff, 'b2': jnp.zeros((D,), jnp.float32)}
    _L0_ffn_all = _L0_ffn_setup()
    _L0_ffn_in = {k: v for k, v in _L0_ffn_all.items() if k in ('Wr', 'br', 'W1', 'b1', 'W2', 'b2')}
    del _L0_ffn_all

    def _L1_xattn_setup():
        import jax, jax.numpy as jnp
        import numpy as np
        B, S, L = (2, 256, 256)
        DIM_Q, H, K, D_C, D_CQ, R = (512, 16, 128, 128, 384, 64)

        def _rope_tables(seq_len, dim, dtype):
            inv_freq = 1.0 / 10000.0 ** (jnp.arange(0, dim, 2, dtype=dtype) / dim)
            t = jnp.arange(seq_len, dtype=dtype)
            freqs = t[:, None] * inv_freq[None, :]
            sin = jnp.repeat(jnp.sin(freqs), 2, axis=-1)
            cos = jnp.repeat(jnp.cos(freqs), 2, axis=-1)
            return (sin, cos)

        def _rotate_half(x):
            h = x.shape[-1] // 2
            return jnp.concatenate([-x[..., h:], x[..., :h]], axis=-1)
        key = jax.random.key(seed)
        ks = jax.random.split(key, 8)
        s_in = 1.0 / np.sqrt(DIM_Q)
        s_k = 1.0 / np.sqrt(K)
        s_cq = 1.0 / np.sqrt(D_CQ)
        s_c = 1.0 / np.sqrt(D_C)
        return {'hidden_q': jax.random.normal(ks[0], (B, S, DIM_Q), jnp.float32), 'kv_c': jax.random.normal(ks[1], (B, L, D_C), jnp.float32), 'Wq': jax.random.normal(ks[2], (H * K, DIM_Q), jnp.float32) * s_in, 'w_kc_q': jax.random.normal(ks[3], (H, K, D_CQ), jnp.float32) * s_k, 'w_kc_kv': jax.random.normal(ks[4], (H, K, D_C), jnp.float32) * s_k, 'W_qr': jax.random.normal(ks[5], (H, D_CQ, R), jnp.float32) * s_cq / np.sqrt(R), 'W_kr': jax.random.normal(ks[6], (H, D_C, R), jnp.float32) * s_c, 'Wo': jax.random.normal(ks[7], (DIM_Q, H * K), jnp.float32) * s_k}
    _L1_xattn_all = _L1_xattn_setup()
    _L1_xattn_in = {k: v for k, v in _L1_xattn_all.items() if k in ('Wq', 'w_kc_q', 'w_kc_kv', 'W_qr', 'W_kr', 'Wo')}
    del _L1_xattn_all

    def _L1_ffn_setup():
        import jax, jax.numpy as jnp
        import numpy as np
        HIDDEN = 512
        INTER = 2048
        SCALE = 64.0

        def fwht(x):
            orig_shape = x.shape
            n = orig_shape[-1]
            x = x.reshape(-1, n)
            h = 1
            while h < n:
                x = x.reshape(-1, n // (2 * h), 2, h)
                a, b = (x[:, :, 0, :], x[:, :, 1, :])
                x = jnp.stack([a + b, a - b], axis=2).reshape(-1, n)
                h *= 2
            return (x / jnp.sqrt(jnp.asarray(n, x.dtype))).reshape(orig_shape)
        key = jax.random.key(seed)
        ks = jax.random.split(key, 8)
        inp = jax.random.normal(ks[0], (4, 512, HIDDEN), dtype=jnp.float32)
        SU_ug = jnp.where(jax.random.bernoulli(ks[1], 0.5, (HIDDEN,)), 1.0, -1.0).astype(jnp.float32)
        SU_dp = jnp.where(jax.random.bernoulli(ks[2], 0.5, (INTER,)), 1.0, -1.0).astype(jnp.float32)
        Wscale_ug = jax.random.uniform(ks[3], (2 * INTER,), jnp.float32, 0.5, 1.5)
        Wscale_dp = jax.random.uniform(ks[4], (HIDDEN,), jnp.float32, 0.5, 1.5)
        W_up = jax.random.normal(ks[5], (INTER, HIDDEN), dtype=jnp.float32) * 0.02
        W_gate = jax.random.normal(ks[6], (INTER, HIDDEN), dtype=jnp.float32) * 0.02
        W_down = jax.random.normal(ks[7], (HIDDEN, INTER), dtype=jnp.float32) * 0.02
        return {'input': inp, 'SU_ug': SU_ug, 'SU_dp': SU_dp, 'Wscale_ug': Wscale_ug, 'Wscale_dp': Wscale_dp, 'W_up': W_up, 'W_gate': W_gate, 'W_down': W_down}
    _L1_ffn_all = _L1_ffn_setup()
    _L1_ffn_in = {k: v for k, v in _L1_ffn_all.items() if k in ('SU_ug', 'SU_dp', 'Wscale_ug', 'Wscale_dp', 'W_up', 'W_gate', 'W_down')}
    del _L1_ffn_all
    return {'x': x, 'ctx_512': ctx_512, 'L0_xattn_W0': _L0_xattn_in['W0'], 'L0_xattn_a_self0': _L0_xattn_in['a_self0'], 'L0_xattn_a_neigh0': _L0_xattn_in['a_neigh0'], 'L0_xattn_b0': _L0_xattn_in['b0'], 'L0_xattn_W1': _L0_xattn_in['W1'], 'L0_xattn_a_self1': _L0_xattn_in['a_self1'], 'L0_xattn_a_neigh1': _L0_xattn_in['a_neigh1'], 'L0_xattn_b1': _L0_xattn_in['b1'], 'L0_ffn_Wr': _L0_ffn_in['Wr'], 'L0_ffn_br': _L0_ffn_in['br'], 'L0_ffn_W1': _L0_ffn_in['W1'], 'L0_ffn_b1': _L0_ffn_in['b1'], 'L0_ffn_W2': _L0_ffn_in['W2'], 'L0_ffn_b2': _L0_ffn_in['b2'], 'L1_xattn_Wq': _L1_xattn_in['Wq'], 'L1_xattn_w_kc_q': _L1_xattn_in['w_kc_q'], 'L1_xattn_w_kc_kv': _L1_xattn_in['w_kc_kv'], 'L1_xattn_W_qr': _L1_xattn_in['W_qr'], 'L1_xattn_W_kr': _L1_xattn_in['W_kr'], 'L1_xattn_Wo': _L1_xattn_in['Wo'], 'L1_ffn_SU_ug': _L1_ffn_in['SU_ug'], 'L1_ffn_SU_dp': _L1_ffn_in['SU_dp'], 'L1_ffn_Wscale_ug': _L1_ffn_in['Wscale_ug'], 'L1_ffn_Wscale_dp': _L1_ffn_in['Wscale_dp'], 'L1_ffn_W_up': _L1_ffn_in['W_up'], 'L1_ffn_W_gate': _L1_ffn_in['W_gate'], 'L1_ffn_W_down': _L1_ffn_in['W_down']}

def reference(x, ctx_512, L0_xattn_W0, L0_xattn_a_self0, L0_xattn_a_neigh0, L0_xattn_b0, L0_xattn_W1, L0_xattn_a_self1, L0_xattn_a_neigh1, L0_xattn_b1, L0_ffn_Wr, L0_ffn_br, L0_ffn_W1, L0_ffn_b1, L0_ffn_W2, L0_ffn_b2, L1_xattn_Wq, L1_xattn_w_kc_q, L1_xattn_w_kc_kv, L1_xattn_W_qr, L1_xattn_W_kr, L1_xattn_Wo, L1_ffn_SU_ug, L1_ffn_SU_dp, L1_ffn_Wscale_ug, L1_ffn_Wscale_dp, L1_ffn_W_up, L1_ffn_W_gate, L1_ffn_W_down):
    import jax
    import jax.numpy as jnp

    def _L0_xattn_ref(feats, adj, W0, a_self0, a_neigh0, b0, W1, a_self1, a_neigh1, b1):
        import jax, jax.numpy as jnp
        import numpy as np
        LRELU_ALPHA = 0.2
        MASK_VAL = -10000000000.0
        B, N, F_IN = (4, 512, 128)
        H, F_OUT = (8, 64)
        F_HID = H * F_OUT

        def gat_layer(x, adj, W, a_self, a_neigh, b):
            feat = jnp.einsum('nf,hfo->hno', x, W)
            attn_self = jnp.einsum('hno,ho->hn', feat, a_self)
            attn_neigh = jnp.einsum('hno,ho->hn', feat, a_neigh)
            e = attn_self[:, :, None] + attn_neigh[:, None, :]
            e = jax.nn.leaky_relu(e, LRELU_ALPHA)
            e = e + MASK_VAL * (1.0 - adj)[None, :, :]
            alpha = jax.nn.softmax(e, axis=-1)
            out = jnp.einsum('hnm,hmo->hno', alpha, feat) + b[:, None, :]
            out = jnp.transpose(out, (1, 0, 2)).reshape(out.shape[1], -1)
            return jax.nn.elu(out)

        def per_graph(x, a):
            h = gat_layer(x, a, W0, a_self0, a_neigh0, b0)
            return gat_layer(h, a, W1, a_self1, a_neigh1, b1)
        return jax.vmap(per_graph)(feats, adj)

    def _L0_ffn_ref(x, Wr, br, W1, b1, W2, b2):
        import jax, jax.numpy as jnp
        import numpy as np
        B, S, D = (4, 1024, 512)
        DFF = 4 * D
        SKIP = 0.125
        Bs, Ss, Ds = x.shape
        k = max(int(Ss * SKIP), 1)
        logits = (x @ Wr + br)[..., 0]
        weights, idx = jax.lax.top_k(logits, k)
        perm = jnp.argsort(idx, axis=1)
        tokens = jnp.take_along_axis(idx, perm, axis=1)
        fx = jnp.take_along_axis(x, tokens[..., None], axis=1)
        h = jax.nn.gelu(fx @ W1 + b1, approximate=False)
        out_l = h @ W2 + b2
        tw = jax.nn.softmax(weights, axis=1)
        rw = jnp.take_along_axis(tw, perm, axis=1)
        xw = rw[..., None] * out_l
        bidx = jnp.arange(Bs)[:, None]
        return x.at[bidx, tokens].add(xw)

    def _L1_xattn_ref(hidden_q, kv_c, Wq, w_kc_q, w_kc_kv, W_qr, W_kr, Wo):
        import jax, jax.numpy as jnp
        import numpy as np
        B, S, L = (2, 256, 256)
        DIM_Q, H, K, D_C, D_CQ, R = (512, 16, 128, 128, 384, 64)

        def _rope_tables(seq_len, dim, dtype):
            inv_freq = 1.0 / 10000.0 ** (jnp.arange(0, dim, 2, dtype=dtype) / dim)
            t = jnp.arange(seq_len, dtype=dtype)
            freqs = t[:, None] * inv_freq[None, :]
            sin = jnp.repeat(jnp.sin(freqs), 2, axis=-1)
            cos = jnp.repeat(jnp.cos(freqs), 2, axis=-1)
            return (sin, cos)

        def _rotate_half(x):
            h = x.shape[-1] // 2
            return jnp.concatenate([-x[..., h:], x[..., :h]], axis=-1)
        b, s, _ = hidden_q.shape
        l = kv_c.shape[1]
        q_hk = (hidden_q @ Wq.T).reshape(b, s, H, K)
        q_big = jnp.einsum('bshk,hkq->bshq', q_hk, w_kc_q)
        sin, cos = _rope_tables(l, D_C, kv_c.dtype)
        kv_rope = kv_c * cos[None] + _rotate_half(kv_c) * sin[None]
        q_r = jnp.einsum('bshq,hqr->bhsr', q_big, W_qr)
        k_r = jnp.einsum('bld,hdr->bhlr', kv_rope, W_kr)
        scores = jnp.einsum('bhsr,bhlr->bhsl', q_r, k_r)
        attn = jax.nn.softmax(scores, axis=-1)
        ctx_c = jnp.einsum('bhsl,bld->bhsd', attn, kv_rope)
        ctx_lat = jnp.einsum('bhsd,hkd->bshk', ctx_c, w_kc_kv)
        out = ctx_lat.reshape(b, s, H * K) @ Wo.T
        return out

    def _L1_ffn_ref(input, SU_ug, SU_dp, Wscale_ug, Wscale_dp, W_up, W_gate, W_down):
        import jax, jax.numpy as jnp
        import numpy as np
        HIDDEN = 512
        INTER = 2048
        SCALE = 64.0

        def fwht(x):
            orig_shape = x.shape
            n = orig_shape[-1]
            x = x.reshape(-1, n)
            h = 1
            while h < n:
                x = x.reshape(-1, n // (2 * h), 2, h)
                a, b = (x[:, :, 0, :], x[:, :, 1, :])
                x = jnp.stack([a + b, a - b], axis=2).reshape(-1, n)
                h *= 2
            return (x / jnp.sqrt(jnp.asarray(n, x.dtype))).reshape(orig_shape)
        n = SU_ug.shape[0]
        x = input.reshape(-1, n)
        x = fwht(x * SU_ug) / SCALE
        x_up = x @ W_up.T * (Wscale_ug[:INTER] * SCALE)
        x_gate = x @ W_gate.T * (Wscale_ug[INTER:] * SCALE)
        x = jax.nn.silu(x_gate) * x_up
        x = fwht(x * SU_dp) / SCALE
        x = x @ W_down.T * (Wscale_dp * SCALE)
        return x.reshape(input.shape)
    x = x + _L0_xattn_ref(ctx_512, _layernorm(x, axis=-1), L0_xattn_W0, L0_xattn_a_self0, L0_xattn_a_neigh0, L0_xattn_b0, L0_xattn_W1, L0_xattn_a_self1, L0_xattn_a_neigh1, L0_xattn_b1)
    x = x + _L0_ffn_ref(_layernorm(x, axis=-1), L0_ffn_Wr, L0_ffn_br, L0_ffn_W1, L0_ffn_b1, L0_ffn_W2, L0_ffn_b2)
    x = x + _L1_xattn_ref(_layernorm(x, axis=-1), ctx_512, L1_xattn_Wq, L1_xattn_w_kc_q, L1_xattn_w_kc_kv, L1_xattn_W_qr, L1_xattn_W_kr, L1_xattn_Wo)
    x = x + _L1_ffn_ref(_layernorm(x, axis=-1), L1_ffn_SU_ug, L1_ffn_SU_dp, L1_ffn_Wscale_ug, L1_ffn_Wscale_dp, L1_ffn_W_up, L1_ffn_W_gate, L1_ffn_W_down)
    return x

_drawn_inputs = setup_inputs


def setup_inputs(seed=0):
    import zlib

    import numpy as np

    out = dict(_drawn_inputs(seed))
    spreads = {'L0_xattn_b0': (0.0, 0.1),
     'L0_xattn_b1': (0.0, 0.1),
     'L0_ffn_b1': (0.0, 0.8),
     'L0_ffn_b2': (0.0, 0.8)}
    factors = {'L0_ffn_Wr': 8.0,
     'L0_ffn_W1': 8.0,
     'L0_ffn_W2': 8.0,
     'L1_ffn_Wscale_ug': 2.689,
     'L1_ffn_Wscale_dp': 3.946}
    for name, (base, spread) in spreads.items():
        noise = np.random.default_rng([zlib.crc32(name.encode()), seed]).standard_normal(out[name].shape)
        drawn = base * np.exp(spread * noise) if base else spread * noise
        out[name] = jnp.asarray(drawn.astype(out[name].dtype))
    for name, factor in factors.items():
        out[name] = (out[name] * factor).astype(out[name].dtype)
    return out
```

```python
from contextlib import ExitStack

import concourse.bass as bass
from concourse import mybir

ALU = mybir.AluOpType
ACT = mybir.ActivationFunctionType
AX = mybir.AxisListType
F32 = mybir.dt.float32

P = 128
B, N, D = 4, 512, 512
NT = N // P
T = B * NT
KD = D // P
F_IN = 128
GH, GO = 8, 64
GP = GH // 2
TOPK = N // 8
DFF = 4 * D
KF = DFF // P
XH, XR = 16, 64
DCQ = 384
LN_EPS = 1e-5
MASK_VAL = -1.0e10
SLOPE = 0.2
BIG = 3.0e38


def layernorm_stats(dve, act, x_res, stats, mean_var, std, rstd, sems):
    stats_done, var_done, std_done, rstd_done = sems

    def on_vector(before=lambda t: None):
        for t in range(T):
            before(t)
            dve.bn_stats(stats[:, t, :], x_res[:, t, :]).then_inc(stats_done, 1)
        dve.wait_ge(stats_done, T)
        for t in range(T):
            dve.bn_aggr(mean_var[:, t, :], stats[:, t, :]).then_inc(stats_done, 1)
        dve.wait_ge(stats_done, 2 * T)
        dve.tensor_scalar(std[:, :], mean_var[:, :, 1], LN_EPS, None, ALU.add).then_inc(var_done, 1)
        dve.wait_ge(std_done, 1)
        dve.reciprocal(rstd[:, :], std[:, :]).then_inc(rstd_done, 1)
        dve.wait_ge(rstd_done, 1)

    def on_scalar():
        act.wait_ge(var_done, 1)
        act.activation(std[:, :], std[:, :], ACT.Sqrt).then_inc(std_done, 1)

    return on_vector, on_scalar


def gat_step(nc, sem, d, x_res, ident, ident_ready, ffn_w1, ffn_w2, ffn_loaded):
    with ExitStack() as ctx:
        sb = lambda name, shape: ctx.enter_context(nc.sbuf_tensor(name, shape, F32))
        ps = lambda name, shape: ctx.enter_context(nc.psum_tensor(name, shape, F32))

        stats, mean_var = sb("g_stats", [P, T, 6]), sb("g_mean_var", [P, T, 2])
        std, rstd = sb("g_std", [P, T]), sb("g_rstd", [P, T])
        weights = [sb("g_w0", [P, 1, GH * GO]), sb("g_w1", [P, KD, GH * GO])]
        vectors = [sb("g_v0", [P, 1, 2 * GH]), sb("g_v1", [P, KD, 2 * GH])]
        a_rows = sb("g_a_rows", [P, 4, GH * GO])
        bias = sb("g_bias", [P, 2, GP])
        product = sb("g_product", [P, GH * GO])
        ctx_in = sb("g_ctx_in", [P, B, N])
        ctx_t = sb("g_ctx_t", [P, 1, N])
        hidden_t = sb("g_hidden_t", [P, GP, N])
        last_t = sb("g_last_t", [P, GP, N])
        mask = sb("g_mask", [P, NT, N])
        row_min, mask_max = sb("g_row_min", [P, NT]), sb("g_mask_max", [P, NT])
        feat = sb("g_feat", [P, NT, GH * GO])
        self_neigh = sb("g_self_neigh", [P, NT, 2 * GH])
        self_part = sb("g_self_part", [P, NT, GH])
        neigh_row = sb("g_neigh_row", [P, 2, N])
        NA, NE = 4, 5
        base = sb("g_base", [P, NA, N])
        expo = sb("g_expo", [P, NE, N])
        neg_max, sums, rsums = sb("g_neg_max", [P, 8]), sb("g_sums", [P, 8]), sb("g_rsums", [P, 8])
        probs_t = sb("g_probs_t", [P, 2, NT, N])
        low, high = sb("g_low", [P, N]), sb("g_high", [P, N])

        neigh_ps = [ps(f"g_neigh_ps{i}", [P, N]) for i in range(2)]
        relu_ps = [ps(f"g_relu_ps{i}", [P, N]) for i in range(2)]
        turn_ps = [ps(f"g_turn_ps{i}", [P, N]) for i in range(2)]
        out_ps = [ps(f"g_out_ps{i}", [P, N]) for i in range(2)]

        x_loaded, w_loaded = sem("g_x_loaded"), sem("g_w_loaded")
        ctx_loaded, ctx_ready = sem("g_ctx_loaded"), sem("g_ctx_ready")
        ln_sems = [sem("g_stats_done"), sem("g_var_done"), sem("g_std_done"), sem("g_rstd_done")]
        product_done, vectors_ready = sem("g_product_done"), sem("g_vectors_ready")
        mask_step, parts_ready = sem("g_mask_step"), sem("g_parts_ready")
        neigh_filled, row_ready, base_ready = sem("g_neigh_filled"), sem("g_row_ready"), sem("g_base_ready")
        relu_ready, expo_ready, exp_done = sem("g_relu_ready"), sem("g_expo_ready"), sem("g_exp_done")
        rsum_ready, probs_ready = sem("g_rsum_ready"), sem("g_probs_ready")
        turned, turn_free = sem("g_turned"), sem("g_turn_free")
        attn_done, out_free = sem("g_attn_done"), sem("g_out_free")
        low_ready, low_exp, hidden_ready = sem("g_low_ready"), sem("g_low_exp"), sem("g_hidden_ready")
        high_ready = sem("g_high_ready")
        row_store = sem("g_row_store")

        TILES = GH * NT
        L_USES = 1 + NT + TILES
        USES = 2 * L_USES + NT
        assert USES % 2 == 0
        LAG = 4

        def use_of(layer, k):
            return layer * L_USES + k

        block = ctx.enter_context(nc.Block())

        @block.sync
        def _(sp):
            for b in range(B):
                sp.dma_start(x_res[:, b * NT:(b + 1) * NT, :],
                             d["x"][b].rearrange("(t p) c -> p t c", p=P)).then_inc(x_loaded, 16)
                sp.dma_start(ctx_in[:, b, :], d["ctx_t"][b]).then_inc(ctx_loaded, 16)
            sp.wait_ge(w_loaded, 16 * 8)
            sp.dma_start(ffn_w1[:, :, :], d["ffn_w1"]).then_inc(ffn_loaded, 16)
            sp.dma_start(ffn_w2[:, :, :], d["ffn_w2"]).then_inc(ffn_loaded, 16)

        @block.gpsimd
        def _(pool):
            pool.sem_inc(base_ready, 8)
            with pool.Fori(0, B) as b:
                for layer in range(2):
                    for h in range(GH):
                        for t in range(NT):
                            j = (layer * GH + h) * NT + t
                            pool.wait_ge(row_ready, b * 2 * GH + layer * GH + h + 1)
                            pool.wait_ge(expo_ready, b * 2 * TILES + j + 1)
                            pool.tensor_tensor(base[:, j % NA, :], mask[:, t, :], neigh_row[:, h % 2, :],
                                               ALU.add).then_inc(base_ready, 1)

        @block.tensor
        def _(pe):
            pe.sem_inc(attn_done, 2)
            pe.wait_ge(ident_ready, 16)
            pe.wait_ge(vectors_ready, 2 + 2 * KD)
            with pe.Fori(0, B) as b:
                def turn(u, pieces, source_ready=None):
                    pe.wait_ge(turn_free, b * USES + u + 1)
                    if source_ready:
                        pe.wait_ge(*source_ready)
                    for c, piece in enumerate(pieces):
                        last = pe.transpose(turn_ps[u % 2][:, c * P:(c + 1) * P], piece, ident[:, :])
                    last.then_inc(turned, 1)

                for layer in range(2):
                    source = [ctx_t, hidden_t][layer]
                    chunks = [1, KD][layer]
                    if layer == 0:
                        pe.wait_ge(ctx_ready, b + 1)
                    else:
                        pe.wait_ge(hidden_ready, b * 2 * GP + GP)
                    u = use_of(layer, 0)
                    pe.wait_ge(turn_free, b * USES + u + 1)
                    for t in range(NT):
                        for c in range(chunks):
                            last = pe.matmul(turn_ps[u % 2][:, t * 2 * GH:(t + 1) * 2 * GH],
                                             source[:, c, t * P:(t + 1) * P], vectors[layer][:, c, :],
                                             start=(c == 0), stop=(c == chunks - 1))
                    last.then_inc(turned, 1)

                    def feature(t):
                        u = use_of(layer, 1 + t)
                        pe.wait_ge(turn_free, b * USES + u + 1)
                        for c in range(chunks):
                            last = pe.matmul(turn_ps[u % 2][:, :], source[:, c, t * P:(t + 1) * P],
                                             weights[layer][:, c, :], start=(c == 0), stop=(c == chunks - 1))
                        last.then_inc(turned, 1)

                    def neighbour(h):
                        g = layer * GH + h
                        if h == 0:
                            pe.wait_ge(turn_free, b * USES + use_of(layer, 0) + 1 + 2)
                        pe.wait_ge(relu_ready, b * 2 * TILES + 4 * g + 4)
                        for t in range(NT):
                            last = pe.transpose(neigh_ps[g % 2][:, t * P:(t + 1) * P],
                                                self_neigh[:, t, GH + h:GH + h + 1].to_broadcast([P, P]),
                                                ident[:, :])
                        last.then_inc(neigh_filled, 1)

                    def attend(h, ks):
                        g = layer * GH + h
                        q = layer * GP + h // 2
                        if ks[0] == 0:
                            pe.wait_ge(turn_free, b * USES + use_of(layer, 1 + NT + h * NT + NT - 1) + 1 + 2)
                            if h % 2 == 0:
                                pe.wait_ge(out_free, b * 2 * GP + q + 1)
                        half = (h % 2) * GO
                        for k in ks:
                            last = pe.matmul(out_ps[q % 2][half:half + GO, :], feat[:, k, h * GO:(h + 1) * GO],
                                             probs_t[:, g % 2, k, :], start=(k == 0), stop=(k == NT - 1))
                        if ks[-1] == NT - 1:
                            last.then_inc(attn_done, 1)

                    neighbour(0)
                    feature(0)
                    neighbour(1)
                    for t in range(1, NT):
                        feature(t)
                    for h in range(GH):
                        for t in range(NT):
                            j = layer * TILES + h * NT + t
                            turn(use_of(layer, 1 + NT + h * NT + t),
                                 [expo[:, j % NE, c * P:(c + 1) * P] for c in range(NT)],
                                 (probs_ready, b * 2 * TILES + j + 1))
                            if h and t == 2:
                                attend(h - 1, [0, 1])
                            if t == 3 and h + 2 < GH:
                                neighbour(h + 2)
                            if h and t == 3:
                                attend(h - 1, [2, 3])
                    attend(GH - 1, [0, 1, 2, 3])
                pe.wait_ge(hidden_ready, b * 2 * GP + 2 * GP)
                for t in range(NT):
                    turn(use_of(2, t), [last_t[:, c, t * P:(t + 1) * P] for c in range(GP)])

        @block.scalar
        def _(act):
            act.sem_inc(relu_ready, 8)
            for i, name in enumerate(("a_self0", "a_neigh0", "a_self1", "a_neigh1")):
                act.dma_start(a_rows[:, i, :], d[name].rearrange("h o -> (h o)").partition_broadcast(P)
                              ).then_inc(w_loaded, 16)
            act.dma_start(weights[0][:, 0, :], d["W0"]).then_inc(w_loaded, 16)
            act.dma_start(weights[1][:, :, :], d["W1"]).then_inc(w_loaded, 16)
            for i, name in enumerate(("b0", "b1")):
                act.dma_start(bias[:, i, :], d[name]).then_inc(w_loaded, 16)
            layernorm_stats(None, act, x_res, stats, mean_var, std, rstd, ln_sems)[1]()
            with act.Fori(0, B) as b:
                for layer in range(2):
                    def elu_exp(q):
                        act.wait_ge(low_ready, b * 2 * GP + layer * GP + q + 1)
                        act.activation(low[:, :], low[:, :], ACT.Exp).then_inc(low_exp, 1)

                    def neighbour_row(h):
                        g = layer * GH + h
                        act.wait_ge(neigh_filled, b * 2 * GH + g + 1)
                        act.wait_ge(base_ready, b * 2 * TILES + 4 * g + 4)
                        act.activation(neigh_row[:, g % 2, :], neigh_ps[g % 2][:, :], ACT.Copy, scale=SLOPE
                                       ).then_inc(row_ready, 1)

                    neighbour_row(0)
                    for i in range(TILES + 1):
                        if i < TILES:
                            h, t = i // NT, i % NT
                            g = layer * GH + h
                            j = layer * TILES + i
                            if i == 0:
                                act.wait_ge(parts_ready, b * 2 + layer + 1)
                            act.wait_ge(expo_ready, b * 2 * TILES + j - 2 + 1 + NA)
                            act.activation(relu_ps[j % 2][:, :], neigh_ps[g % 2][:, :], ACT.Relu,
                                           bias=self_part[:, t, h:h + 1], scale=1.0 - SLOPE
                                           ).then_inc(relu_ready, 1)
                        if i:
                            j = layer * TILES + i - 1
                            act.wait_ge(expo_ready, b * 2 * TILES + j + 1 + NA)
                            act.activation(expo[:, j % NE, :], expo[:, j % NE, :], ACT.Exp,
                                           bias=neg_max[:, j % 8:j % 8 + 1], scale=-1.0,
                                           accum_out=sums[:, j % 8:j % 8 + 1]).then_inc(exp_done, 1)
                        if i % NT == 2 and i // NT + 1 < GH:
                            neighbour_row(i // NT + 1)
                        if i in (17, 25):
                            elu_exp((i - 17) // 8)
                    elu_exp(2)
                    elu_exp(3)

        @block.vector
        def _(dve):
            dve.sem_inc(expo_ready, NA)
            dve.sem_inc(turn_free, 2)
            dve.sem_inc(out_free, 2)
            dve.wait_ge(w_loaded, 16 * 8)
            dve.wait_ge(ctx_loaded, 16 * B)
            n_products = 0
            for layer in range(2):
                for c in range([1, KD][layer]):
                    for side in range(2):
                        if n_products:
                            dve.wait_ge(vectors_ready, n_products)
                        dve.tensor_tensor(product[:, :], weights[layer][:, c, :], a_rows[:, 2 * layer + side, :],
                                          ALU.mult).then_inc(product_done, 1)
                        n_products += 1
                        dve.wait_ge(product_done, n_products)
                        dve.tensor_reduce(vectors[layer][:, c, side * GH:(side + 1) * GH],
                                          product[:, :].rearrange("p (h o) -> p h o", h=GH), AX.X, ALU.add
                                          ).then_inc(vectors_ready, 1)
            layernorm_stats(dve, None, x_res, stats, mean_var, std, rstd, ln_sems)[0](
                lambda t: dve.wait_ge(x_loaded, 16 * (t // NT + 1)) if t % NT == 0 else None)
            with dve.Fori(0, B) as b:
                M_STEPS = 2 * NT + NT + 1 + NT
                for t in range(NT):
                    dve.tensor_scalar(mask[:, t, :], x_res[:, bass.ds(b * NT + t, 1), :].rearrange("p a c -> p (a c)"),
                                      mean_var[:, bass.ds(b * NT + t, 1), 0], rstd[:, bass.ds(b * NT + t, 1)],
                                      ALU.subtract, ALU.mult).then_inc(mask_step, 1)
                dve.wait_ge(mask_step, b * M_STEPS + NT)
                for t in range(NT):
                    dve.tensor_scalar(mask[:, t, :], mask[:, t, :], -1.0, 1.0, ALU.mult, ALU.add
                                      ).then_inc(mask_step, 1)
                dve.wait_ge(mask_step, b * M_STEPS + 2 * NT)
                for t in range(NT):
                    dve.tensor_reduce(row_min[:, t:t + 1], mask[:, t, :], AX.X, ALU.min).then_inc(mask_step, 1)
                dve.wait_ge(mask_step, b * M_STEPS + 3 * NT)
                dve.tensor_scalar(mask_max[:, :], row_min[:, :], MASK_VAL, None, ALU.mult).then_inc(mask_step, 1)
                dve.wait_ge(mask_step, b * M_STEPS + 3 * NT + 1)
                for t in range(NT):
                    dve.tensor_scalar(mask[:, t, :], mask[:, t, :], MASK_VAL, mask_max[:, t:t + 1],
                                      ALU.mult, ALU.subtract).then_inc(mask_step, 1)

                dve.tensor_copy(ctx_t[:, :, :], ctx_in[:, bass.ds(b, 1), :]).then_inc(ctx_ready, 1)

                for layer in range(2):
                    target = [hidden_t, last_t][layer]
                    u = use_of(layer, 0)
                    dve.wait_ge(turned, b * USES + u + 1)
                    columns = turn_ps[u % 2][:, 0:NT * 2 * GH].rearrange("p (t h) -> p t h", t=NT)
                    dve.tensor_scalar(self_part[:, :, :], columns[:, :, 0:GH], 1.0 - SLOPE, None, ALU.mult
                                      ).then_inc(parts_ready, 1)
                    dve.tensor_copy(self_neigh[:, :, :], columns).then_inc(turn_free, 1)

                    def copy(k):
                        u = use_of(layer, 1 + k)
                        dve.wait_ge(turned, b * USES + u + 1)
                        if k < NT:
                            dve.tensor_copy(feat[:, k, :], turn_ps[u % 2][:, :]).then_inc(turn_free, 1)
                            return
                        h, t = (k - NT) // NT, (k - NT) % NT
                        g = layer * GH + h
                        if t == 0:
                            dve.wait_ge(attn_done, b * 2 * GH + g + 1)
                        dve.tensor_copy(probs_t[:, g % 2, :, t * P:(t + 1) * P],
                                        turn_ps[u % 2][:, :].rearrange("p (k n) -> p k n", k=NT)
                                        ).then_inc(turn_free, 1)

                    def elu_parts(q):
                        gq = layer * GP + q
                        dve.wait_ge(attn_done, b * 2 * GH + 2 * gq + 2 + 2)
                        dve.tensor_scalar(low[:, :], out_ps[gq % 2][:, :], bias[:, layer, q:q + 1], 0.0,
                                          ALU.add, ALU.min).then_inc(low_ready, 1)
                        dve.tensor_scalar(high[:, :], out_ps[gq % 2][:, :], bias[:, layer, q:q + 1], 0.0,
                                          ALU.add, ALU.max).then_inc(out_free, 1)

                    def elu_sum(q):
                        gq = layer * GP + q
                        dve.wait_ge(low_exp, b * 2 * GP + gq + 1)
                        dve.wait_ge(out_free, b * 2 * GP + gq + 1 + 2)
                        dve.scalar_tensor_tensor(target[:, q, :], low[:, :], -1.0, high[:, :], ALU.add, ALU.add
                                                 ).then_inc(hidden_ready, 1)

                    for i in range(TILES + NT + LAG):
                        if i < TILES:
                            j = layer * TILES + i
                            dve.wait_ge(relu_ready, b * 2 * TILES + j + 1 + 8)
                            dve.wait_ge(base_ready, b * 2 * TILES + j + 1 + 8)
                        if i < TILES + LAG:
                            copy(i)
                        if i < TILES:
                            dve.tensor_tensor_reduce(expo[:, j % NE, :], relu_ps[j % 2][:, :], base[:, j % NA, :],
                                                     -1.0, BIG, ALU.add, ALU.min, neg_max[:, j % 8:j % 8 + 1]
                                                     ).then_inc(expo_ready, 1)
                        if 1 <= i <= TILES:
                            j = layer * TILES + i - 1
                            dve.wait_ge(exp_done, b * 2 * TILES + j + 1)
                            dve.reciprocal(rsums[:, j % 8:j % 8 + 1], sums[:, j % 8:j % 8 + 1]).then_inc(rsum_ready, 1)
                            dve.wait_ge(rsum_ready, b * 2 * TILES + j + 1)
                            dve.tensor_scalar(expo[:, j % NE, :], expo[:, j % NE, :], rsums[:, j % 8:j % 8 + 1], None,
                                              ALU.mult).then_inc(probs_ready, 1)
                        if i in (16, 24, 32):
                            elu_parts((i - 16) // 8)
                        if i in (18, 26, 34):
                            elu_sum((i - 18) // 8)
                    elu_parts(3)
                    elu_sum(3)

                for t in range(NT):
                    u = use_of(2, t)
                    dve.wait_ge(turned, b * USES + u + 1)
                    x_tile = x_res[:, bass.ds(b * NT + t, 1), :].rearrange("p a c -> p (a c)")
                    dve.tensor_tensor(x_tile, x_tile, turn_ps[u % 2][:, :], ALU.add).then_inc(turn_free, 1)


def routed_ffn_step(nc, sem, d, x_res, ident, ffn_w1, ffn_w2, ffn_loaded):
    with ExitStack() as ctx:
        sb = lambda name, shape: ctx.enter_context(nc.sbuf_tensor(name, shape, F32))
        ps = lambda name, shape: ctx.enter_context(nc.psum_tensor(name, shape, F32))
        PT = 2 * NT
        KH = DFF // P
        stats, mean_var = sb("r_stats", [P, T, 6]), sb("r_mean_var", [P, T, 2])
        std, rstd = sb("r_std", [P, T]), sb("r_rstd", [P, T])
        wr_row, b2_row = sb("r_wr_row", [P, D]), sb("r_b2_row", [P, D])
        br, b1 = sb("r_br", [P, 1]), sb("r_b1", [P, KH])
        before, not_before = sb("r_before", [P, NT, N]), sb("r_not_before", [P, NT, N])
        slots = sb("r_slots", [P, 2, P])
        ones = sb("r_ones", [P, P])
        y = sb("r_y", [P, PT, D])
        scratch = sb("r_scratch", [P, 2, D])
        dots, logit = sb("r_dots", [P, PT]), sb("r_logit", [P, PT])
        logit_row = sb("r_logit_row", [P, 2, N])
        neg_max = sb("r_neg_max", [P, 2])
        above = sb("r_above", [P, 2, PT])
        rank, picked = sb("r_rank", [P, PT]), sb("r_picked", [P, PT])
        expo, weight = sb("r_expo", [P, PT]), sb("r_weight", [P, T])
        total, rtotal = sb("r_total", [P, 2]), sb("r_rtotal", [P, 2])
        onehot, onehot_t = sb("r_onehot", [P, PT, P]), sb("r_onehot_t", [P, T, P])
        fx_t = sb("r_fx_t", [P, KD, 4 * TOPK])
        hidden_t = sb("r_hidden_t", [P, KH, 4 * TOPK])
        picks_out = sb("r_picks_out", [P, 2, D])

        row_ps = [ps(f"r_row_ps{i}", [P, N]) for i in range(2)]
        total_ps = ps("r_total_ps", [P, N])
        fx_ps = ps("r_fx_ps", [P, N])
        turn_ps = [ps(f"r_turn_ps{i}", [P, N]) for i in range(2)]
        hidden_ps = [ps(f"r_hidden_ps{i}", [P, N]) for i in range(2)]

        loaded = sem("r_loaded")
        ln_sems = [sem("r_stats_done"), sem("r_var_done"), sem("r_std_done"), sem("r_rstd_done")]
        y_ready, dot_done, logit_ready = sem("r_y_ready"), sem("r_dot_done"), sem("r_logit_ready")
        row_filled, row_copied, max_ready = sem("r_row_filled"), sem("r_row_copied"), sem("r_max_ready")
        exp_done, count_done, rank_ready = sem("r_exp_done"), sem("r_count_done"), sem("r_rank_ready")
        chosen, total_filled, total_step = sem("r_chosen"), sem("r_total_filled"), sem("r_total_step")
        onehot_ready, gathered, fx_copied = sem("r_onehot_ready"), sem("r_gathered"), sem("r_fx_copied")
        turned, turn_copied, y_added = sem("r_turned"), sem("r_turn_copied"), sem("r_y_added")
        hidden_filled, hidden_ready = sem("r_hidden_filled"), sem("r_hidden_ready")
        out_filled, out_ready = sem("r_out_filled"), sem("r_out_ready")
        scattered, x_updated = sem("r_scattered"), sem("r_x_updated")
        LOADS = 8
        block = ctx.enter_context(nc.Block())

        @block.sync
        def _(sp):
            for dst, src in ((wr_row[:, :], d["Wr"].rearrange("d a -> (d a)").partition_broadcast(P)),
                             (b2_row[:, :], d["b2"].partition_broadcast(P)),
                             (br[:, :], d["br"].partition_broadcast(P)), (b1[:, :], d["b1"]),
                             (before[:, :, :], d["before"]), (not_before[:, :, :], d["not_before"]),
                             (slots[:, :, :], d["slots"]), (ones[:, :], d["ones"])):
                sp.dma_start(dst, src).then_inc(loaded, 16)

        @block.gpsimd
        def _(pool):
            for pair in range(2):
                for i in range(PT):
                    pool.wait_ge(y_ready, pair * PT + i + 1)
                    tile = pair * PT + i
                    pool.tensor_tensor(x_res[:, tile, :], x_res[:, tile, :], y[:, i, :], ALU.add
                                       ).then_inc(y_added, 1)

        @block.tensor
        def _(pe):
            pe.wait_ge(loaded, 16 * LOADS)
            for pair in range(2):
                pe.wait_ge(logit_ready, pair + 1)
                for g in range(2):
                    if pair:
                        pe.wait_ge(row_copied, 2 * (pair - 1) + g + 1)
                    for t in range(NT):
                        last = pe.transpose(row_ps[g][:, t * P:(t + 1) * P],
                                            logit[:, g * NT + t:g * NT + t + 1].to_broadcast([P, P]), ident[:, :])
                    last.then_inc(row_filled, 1)
                pe.wait_ge(chosen, pair + 1)
                pe.matmul(total_ps[:, 0:PT], ones[:, :], expo[:, :], start=True, stop=True).then_inc(total_filled, 1)
                pe.wait_ge(onehot_ready, PT * (pair + 1))
                if pair:
                    pe.wait_ge(fx_copied, pair)
                for c in range(KD):
                    for i in range(PT):
                        last = pe.matmul(fx_ps[:, c * P:(c + 1) * P], y[:, i, c * P:(c + 1) * P], onehot[:, i, :],
                                         start=(i == 0), stop=(i == PT - 1))
                last.then_inc(gathered, 1)
                for half in range(2):
                    if pair:
                        pe.wait_ge(turn_copied, 2 * (pair - 1) + half + 1)
                    for i in range(NT):
                        last = pe.transpose(turn_ps[half][:, i * P:(i + 1) * P], onehot[:, half * NT + i, :],
                                            ident[:, :])
                    last.then_inc(turned, 1)
            pe.wait_ge(fx_copied, 2)
            pe.wait_ge(ffn_loaded, 32)
            for f in range(KH):
                if f >= 2:
                    pe.wait_ge(hidden_ready, f - 1)
                for c in range(KD):
                    last = pe.matmul(hidden_ps[f % 2][:, 0:4 * TOPK], ffn_w1[:, c, f * P:(f + 1) * P], fx_t[:, c, :],
                                     start=(c == 0), stop=(c == KD - 1))
                last.then_inc(hidden_filled, 1)
            for r in range(2):
                for f in range(KH):
                    if r == 0:
                        pe.wait_ge(hidden_ready, f + 1)
                    last = pe.matmul(row_ps[r][:, :], hidden_t[:, f, r * P:(r + 1) * P], ffn_w2[:, f, :],
                                     start=(f == 0), stop=(f == KH - 1))
                last.then_inc(out_filled, 1)
            pe.wait_ge(turn_copied, 4)
            for tile in range(T):
                pe.wait_ge(out_ready, tile // PT + 1)
                if tile >= 2:
                    pe.wait_ge(x_updated, tile - 1)
                pe.matmul(turn_ps[tile % 2][:, :], onehot_t[:, tile, :], picks_out[:, tile // PT, :],
                          start=True, stop=True).then_inc(scattered, 1)

        @block.scalar
        def _(act):
            layernorm_stats(None, act, x_res, stats, mean_var, std, rstd, ln_sems)[1]()
            for pair in range(2):
                act.wait_ge(max_ready, pair + 1)
                act.wait_ge(logit_ready, pair + 1)
                for g in range(2):
                    act.activation(expo[:, g * NT:(g + 1) * NT], logit[:, g * NT:(g + 1) * NT], ACT.Exp,
                                   bias=neg_max[:, g:g + 1]).then_inc(exp_done, 1)
            act.wait_ge(loaded, 16 * LOADS)
            for f in range(KH):
                act.wait_ge(hidden_filled, f + 1)
                act.activation(hidden_t[:, f, :], hidden_ps[f % 2][:, 0:4 * TOPK], ACT.Gelu, bias=b1[:, f:f + 1]
                               ).then_inc(hidden_ready, 1)

        @block.vector
        def _(dve):
            layernorm_stats(dve, None, x_res, stats, mean_var, std, rstd, ln_sems)[0]()
            dve.wait_ge(loaded, 16 * LOADS)
            for pair in range(2):
                if pair:
                    dve.wait_ge(gathered, pair)
                    dve.wait_ge(y_added, pair * PT)
                for i in range(PT):
                    tile = pair * PT + i
                    dve.tensor_scalar(y[:, i, :], x_res[:, tile, :], mean_var[:, tile, 0:1], rstd[:, tile:tile + 1],
                                      ALU.subtract, ALU.mult).then_inc(y_ready, 1)
                for i in range(PT):
                    n = pair * PT + i
                    dve.wait_ge(y_ready, n + 1)
                    if i == 0 and pair:
                        dve.wait_ge(count_done, 2 * PT * pair)
                    if i >= 2:
                        dve.wait_ge(dot_done, n - 1)
                    dve.tensor_tensor_reduce(scratch[:, i % 2, :], y[:, i, :], wr_row[:, :], 1.0, 0.0,
                                             ALU.mult, ALU.add, dots[:, i:i + 1]).then_inc(dot_done, 1)
                dve.wait_ge(dot_done, PT * (pair + 1))
                if pair:
                    dve.wait_ge(exp_done, 2 * pair)
                    dve.wait_ge(row_filled, 2 * pair)
                    dve.wait_ge(onehot_ready, PT * pair)
                dve.tensor_scalar(logit[:, :], dots[:, :], br[:, 0:1], None, ALU.add).then_inc(logit_ready, 1)
                for g in range(2):
                    dve.wait_ge(row_filled, 2 * pair + g + 1)
                    dve.tensor_copy(logit_row[:, g, :], row_ps[g][:, :]).then_inc(row_copied, 1)
                    dve.wait_ge(row_copied, 2 * pair + g + 1)
                dve.tensor_reduce(neg_max[:, :], logit_row[:, :, :], AX.X, ALU.max, negate=True
                                  ).then_inc(max_ready, 1)
                dve.wait_ge(logit_ready, pair + 1)
                for i in range(PT):
                    for side, (mask, op) in enumerate(((before, ALU.is_ge), (not_before, ALU.is_gt))):
                        n = (pair * PT + i) * 2 + side
                        if n % (2 * PT) >= 2:
                            dve.wait_ge(count_done, n - 1)
                        dve.scalar_tensor_tensor(scratch[:, side, :], logit_row[:, i // NT, :], logit[:, i:i + 1],
                                                 mask[:, i % NT, :], op, ALU.mult,
                                                 accum_out=above[:, side, i:i + 1]).then_inc(count_done, 1)
                dve.wait_ge(count_done, 2 * PT * (pair + 1))
                dve.tensor_tensor(rank[:, :], above[:, 0, :], above[:, 1, :], ALU.add).then_inc(rank_ready, 1)
                dve.wait_ge(rank_ready, pair + 1)
                if pair:
                    dve.wait_ge(turned, 2 * pair)
                for i in range(PT):
                    dve.tensor_scalar(onehot[:, i, :], slots[:, i // NT, :], rank[:, i:i + 1], None, ALU.is_equal
                                      ).then_inc(onehot_ready, 1)
                dve.tensor_scalar(picked[:, :], rank[:, :], float(TOPK), None, ALU.is_lt).then_inc(total_step, 1)
                dve.wait_ge(total_step, pair * 4 + 1)
                dve.wait_ge(exp_done, 2 * pair + 2)
                dve.tensor_tensor(expo[:, :], expo[:, :], picked[:, :], ALU.mult).then_inc(chosen, 1)
                dve.wait_ge(total_filled, pair + 1)
                dve.tensor_reduce(total[:, :], total_ps[:, 0:PT].rearrange("p (g t) -> p g t", g=2), AX.X, ALU.add
                                  ).then_inc(total_step, 1)
                dve.wait_ge(total_step, pair * 4 + 2)
                dve.reciprocal(rtotal[:, :], total[:, :]).then_inc(total_step, 1)
                dve.wait_ge(total_step, pair * 4 + 3)
                for g in range(2):
                    at = (2 * pair + g) * NT
                    w = dve.tensor_scalar(weight[:, at:at + NT], expo[:, g * NT:(g + 1) * NT], rtotal[:, g:g + 1],
                                          None, ALU.mult)
                w.then_inc(total_step, 1)
                dve.wait_ge(gathered, pair + 1)
                dve.tensor_copy(fx_t[:, :, pair * P:(pair + 1) * P],
                                fx_ps[:, :].rearrange("p (c r) -> p c r", c=KD)).then_inc(fx_copied, 1)
                for half in range(2):
                    dve.wait_ge(turned, 2 * pair + half + 1)
                    at = pair * PT + half * NT
                    dve.tensor_copy(onehot_t[:, at:at + NT, :], turn_ps[half][:, :].rearrange(
                        "p (t n) -> p t n", t=NT)).then_inc(turn_copied, 1)
            for r in range(2):
                dve.wait_ge(out_filled, r + 1)
                dve.tensor_tensor(picks_out[:, r, :], row_ps[r][:, :], b2_row[:, :], ALU.add).then_inc(out_ready, 1)
            dve.wait_ge(total_step, 8)
            dve.wait_ge(y_added, T)
            for tile in range(T):
                dve.wait_ge(scattered, tile + 1)
                dve.scalar_tensor_tensor(x_res[:, tile, :], turn_ps[tile % 2][:, :], weight[:, tile:tile + 1],
                                         x_res[:, tile, :], ALU.mult, ALU.add).then_inc(x_updated, 1)


def cross_attention_step(nc, sem, d, x_res, ident):
    with ExitStack() as outer:
        keep = lambda name, shape: outer.enter_context(nc.sbuf_tensor(name, shape, F32))
        XP = XH // 2
        q_w = keep("x_q_w", [P, KD, XH * XR])
        o_w = keep("x_o_w", [P, XH, D])
        kr_w = keep("x_kr_w", [P, XH * XR])
        kv = keep("x_kv", [P, T, F_IN])
        kv_t = keep("x_kv_t", [P, B, N])

        with ExitStack() as ctx:
            sb = lambda name, shape: ctx.enter_context(nc.sbuf_tensor(name, shape, F32))
            ps = lambda name, shape: ctx.enter_context(nc.psum_tensor(name, shape, F32))
            KC = DCQ // P
            wq, kcq_t = sb("x_wq", [P, XH, D]), sb("x_kcq_t", [P, KC, XH, P])
            wqr, latent = sb("x_wqr", [P, KC, XH, XR]), sb("x_latent", [P, XH, XR])
            wo_t, kckv = sb("x_wo_t", [P, 4, D]), sb("x_kckv", [P, XH, P])
            swapped, cos, sin = sb("x_swapped", [P, T, F_IN]), sb("x_cos", [P, NT, F_IN]), sb("x_sin", [P, NT, F_IN])
            cos_t, sin_t = sb("x_cos_t", [P, N]), sb("x_sin_t", [P, N])
            swapped_t = swapped[:, :, :].rearrange("p (b t) f -> p b (t f)", b=B)
            mm_ps = [ps(f"x_mm_ps{i}", [P, N]) for i in range(4)]
            ctx_loaded, rope_step = sem("x_ctx_loaded"), sem("x_rope_step")
            a_loaded, q_loaded, tables_loaded = sem("x_a_loaded"), sem("x_q_loaded"), sem("x_tables_loaded")
            o_loaded = [sem(f"x_o_loaded{i}") for i in range(2)]
            filled, copied = sem("x_filled"), sem("x_copied")
            block = ctx.enter_context(nc.Block())
            AP_, QP, OP = 2, KD * 2, XH
            wo_v = d["wo"]

            @block.sync
            def _(sp):
                sp.dma_start(kcq_t[:, :, :, :], d["kcq"]).then_inc(a_loaded, 16)
                sp.dma_start(wqr[:, :, :, :], d["wqr"]).then_inc(a_loaded, 16)
                sp.dma_start(wq[:, :, :], d["wq"]).then_inc(q_loaded, 16)
                for n in range(XH // 2):
                    if n >= 2:
                        sp.wait_ge(filled, AP_ + QP + 2 * n - 2)
                    at = 2 * (n % 2)
                    sp.dma_start(wo_t[:, at:at + 2, :], wo_v[:, 2 * n:2 * n + 2, :]).then_inc(o_loaded[n % 2], 16)

            @block.gpsimd
            def _(pool):
                steps = 0

                def step(ins):
                    nonlocal steps
                    steps += 1
                    ins.then_inc(rope_step, 1)
                    pool.wait_ge(rope_step, steps)

                pool.wait_ge(ctx_loaded, 16 * 8)
                for b in range(B):
                    at = slice(b * NT, (b + 1) * NT)
                    step(pool.tensor_tensor(kv[:, at, :], kv[:, at, :], cos[:, :, :], ALU.mult))
                    step(pool.tensor_tensor(swapped[:, at, :], swapped[:, at, :], sin[:, :, :], ALU.mult))
                    step(pool.tensor_tensor(kv[:, at, :], kv[:, at, :], swapped[:, at, :], ALU.add))
                pool.wait_ge(ctx_loaded, 16 * 10)
                pool.wait_ge(tables_loaded, 32)
                for b in range(B):
                    step(pool.tensor_tensor(kv_t[:, b, :], kv_t[:, b, :], cos_t[:, :], ALU.mult))
                    step(pool.tensor_tensor(swapped_t[:, b, :], swapped_t[:, b, :], sin_t[:, :], ALU.mult))
                    step(pool.tensor_tensor(kv_t[:, b, :], kv_t[:, b, :], swapped_t[:, b, :], ALU.add))

            @block.tensor
            def _(pe):
                use = 0

                def begin():
                    if use >= 4:
                        pe.wait_ge(copied, use - 3)
                    return mm_ps[use % 4]

                pe.wait_ge(a_loaded, 32)
                for half in range(AP_):
                    out = begin()
                    for i in range(8):
                        h = half * 8 + i
                        for c in range(KC):
                            last = pe.matmul(out[:, i * XR:(i + 1) * XR], kcq_t[:, c, h, :], wqr[:, c, h, :],
                                             start=(c == 0), stop=(c == KC - 1))
                    last.then_inc(filled, 1)
                    use += 1
                pe.wait_ge(q_loaded, 16)
                pe.wait_ge(copied, AP_)
                for c in range(KD):
                    for half in range(2):
                        out = begin()
                        for i in range(8):
                            h = half * 8 + i
                            last = pe.matmul(out[:, i * XR:(i + 1) * XR], wq[:, h, c * P:(c + 1) * P],
                                             latent[:, h, :], start=True, stop=True)
                        last.then_inc(filled, 1)
                        use += 1
                pe.wait_ge(ctx_loaded, 16 * 8)
                for h in range(XH):
                    out = begin()
                    pe.wait_ge(o_loaded[h // 2 % 2], 16 * (h // 4 + 1))
                    pe.matmul(out[:, :], kckv[:, h, :], wo_t[:, h % 4, :], start=True, stop=True).then_inc(filled, 1)
                    use += 1

            @block.scalar
            def _(act):
                ctx_v = d["ctx"].rearrange("b (t p) f -> p (b t) f", p=P)
                H = F_IN // 2
                ctx_t_v = d["ctx_t"].rearrange("b f n -> f b n")
                for dst, src in ((kv[:, :, :], ctx_v), (swapped[:, :, 0:H], ctx_v[:, :, H:F_IN]),
                                 (swapped[:, :, H:F_IN], ctx_v[:, :, 0:H]), (cos[:, :, :], d["cos"]),
                                 (sin[:, :, :], d["sin"]), (kr_w[:, :].rearrange("p (h r) -> p h r", h=XH),
                                                            d["wkr"]),
                                 (kv_t[:, :, :], ctx_t_v),
                                 (kckv[:, :, :], d["kckv"])):
                    act.dma_start(dst, src).then_inc(ctx_loaded, 16)
                act.dma_start(cos_t[:, :], d["cos_t"]).then_inc(tables_loaded, 16)
                act.dma_start(sin_t[:, :], d["sin_t"]).then_inc(tables_loaded, 16)
                act.wait_ge(rope_step, 3 * B)
                act.dma_start(swapped_t[0:H, :, :], ctx_t_v[H:F_IN]).then_inc(ctx_loaded, 16)
                act.dma_start(swapped_t[H:F_IN, :, :], ctx_t_v[0:H]).then_inc(ctx_loaded, 16)

            @block.vector
            def _(dve):
                use = 0
                for half in range(AP_):
                    dve.wait_ge(filled, use + 1)
                    dve.tensor_copy(latent[:, half * 8:(half + 1) * 8, :], mm_ps[use % 4][:, :].rearrange(
                        "p (h r) -> p h r", h=8)).then_inc(copied, 1)
                    use += 1
                for c in range(KD):
                    for half in range(2):
                        dve.wait_ge(filled, use + 1)
                        dve.tensor_copy(q_w[:, c, half * N:(half + 1) * N], mm_ps[use % 4][:, :]).then_inc(copied, 1)
                        use += 1
                for h in range(XH):
                    dve.wait_ge(filled, use + 1)
                    dve.tensor_copy(o_w[:, h, :], mm_ps[use % 4][:, :]).then_inc(copied, 1)
                    use += 1

        with ExitStack() as ctx:
            sb = lambda name, shape: ctx.enter_context(nc.sbuf_tensor(name, shape, F32))
            ps = lambda name, shape: ctx.enter_context(nc.psum_tensor(name, shape, F32))
            stats, mean_var = sb("x_stats", [P, T, 6]), sb("x_mean_var", [P, T, 2])
            std, rstd = sb("x_std", [P, T]), sb("x_rstd", [P, T])
            NE = 4
            expo = sb("x_expo", [P, NE, N])
            y_t = sb("x_y_t", [P, KD, N])
            kv_now = sb("x_kv_now", [P, NT, F_IN])
            k_t, q_t = sb("x_k_t", [P, XP, N]), sb("x_q_t", [P, XP, N])
            neg_max, sums, rsums = sb("x_neg_max", [P, 8]), sb("x_sums", [P, 8]), sb("x_rsums", [P, 8])
            probs_t = sb("x_probs_t", [P, 2, NT, N])
            latent_t = sb("x_latent_t", [P, XH, N])
            score_ps = [ps(f"x_score_ps{i}", [P, N]) for i in range(2)]
            turn_ps = [ps(f"x_turn_ps{i}", [P, N]) for i in range(2)]
            latent_ps = [ps(f"x_latent_ps{i}", [P, N]) for i in range(2)]
            project_ps = [ps(f"x_project_ps{i}", [P, N]) for i in range(2)]

            ln_sems = [sem("x_stats_done"), sem("x_var_done"), sem("x_std_done"), sem("x_rstd_done")]
            y_ready, kv_ready = sem("x_y_ready"), sem("x_kv_ready")
            turned, turn_free = sem("x_turned"), sem("x_turn_free")
            projected, project_free = sem("x_projected"), sem("x_project_free")
            scored, max_ready, exp_done = sem("x_scored"), sem("x_max_ready"), sem("x_exp_done")
            rsum_ready, probs_ready = sem("x_rsum_ready"), sem("x_probs_ready")
            latent_filled, latent_free = sem("x_latent_filled"), sem("x_latent_free")

            TILES = XH * NT
            USES = NT + TILES
            PUSES = 2 * XP + NT
            LAG = 3
            block = ctx.enter_context(nc.Block())

            @block.tensor
            def _(pe):
                pe.sem_inc(latent_filled, 2)
                with pe.Fori(0, B) as b:
                    for t in range(NT):
                        pe.wait_ge(turn_free, b * USES + t + 1)
                        pe.wait_ge(y_ready, b * NT + t + 1)
                        for c in range(KD):
                            last = pe.transpose(turn_ps[t % 2][:, c * P:(c + 1) * P], expo[:, t, c * P:(c + 1) * P],
                                                ident[:, :])
                        last.then_inc(turned, 1)
                    for n in range(2 * XP):
                        pair = n % XP
                        cols = slice(pair * 2 * XR, (pair + 1) * 2 * XR)
                        pe.wait_ge(project_free, b * PUSES + n + 1)
                        if n < XP:
                            last = pe.matmul(project_ps[n % 2][:, :], kr_w[:, cols],
                                             kv_t[:, bass.ds(b, 1), :].rearrange("p a n -> p (a n)"),
                                             start=True, stop=True)
                        else:
                            if n == XP:
                                pe.wait_ge(turn_free, b * USES + NT + 2)
                            for c in range(KD):
                                last = pe.matmul(project_ps[n % 2][:, :], q_w[:, c, cols], y_t[:, c, :],
                                                 start=(c == 0), stop=(c == KD - 1))
                        last.then_inc(projected, 1)
                    pe.wait_ge(project_free, b * PUSES + 2 * XP + 2)
                    for i in range(TILES + 2 * NT + 1):
                        if i < TILES:
                            h, t = i // NT, i % NT
                            half = slice((h % 2) * XR, (h % 2 + 1) * XR)
                            pe.wait_ge(exp_done, b * TILES + i + 1)
                            pe.matmul(score_ps[i % 2][:, :], q_t[half, h // 2, t * P:(t + 1) * P],
                                      k_t[half, h // 2, :], start=True, stop=True).then_inc(scored, 1)
                        if 0 <= i - LAG < TILES:
                            n = i - LAG
                            pe.wait_ge(turn_free, b * USES + NT + n + 1)
                            pe.wait_ge(probs_ready, b * TILES + n + 1)
                            for c in range(NT):
                                last = pe.transpose(turn_ps[n % 2][:, c * P:(c + 1) * P],
                                                    expo[:, n % NE, c * P:(c + 1) * P], ident[:, :])
                            last.then_inc(turned, 1)
                        if i - 2 * NT >= 0 and i - 2 * NT < TILES:
                            h, k = (i - 2 * NT) // NT, i % NT
                            if k == 0:
                                pe.wait_ge(turn_free, b * USES + NT + h * NT + NT + 2)
                                pe.wait_ge(latent_free, b * XH + h + 1)
                                pe.wait_ge(kv_ready, b + 1)
                            last = pe.matmul(latent_ps[h % 2][:, :], kv_now[:, k, :], probs_t[:, h % 2, k, :],
                                             start=(k == 0), stop=(k == NT - 1))
                            if k == NT - 1:
                                last.then_inc(latent_filled, 1)
                    pe.wait_ge(latent_free, b * XH + XH + 2)
                    for t in range(NT):
                        pe.wait_ge(project_free, b * PUSES + 2 * XP + t + 1)
                        for h in range(XH):
                            last = pe.matmul(project_ps[t % 2][:, :], latent_t[:, h, t * P:(t + 1) * P], o_w[:, h, :],
                                             start=(h == 0), stop=(h == XH - 1))
                        last.then_inc(projected, 1)

            @block.scalar
            def _(act):
                act.sem_inc(exp_done, 2)
                act.sem_inc(turn_free, 2)
                act.sem_inc(latent_free, 2)
                layernorm_stats(None, act, x_res, stats, mean_var, std, rstd, ln_sems)[1]()
                with act.Fori(0, B) as b:
                    for t in range(NT):
                        act.wait_ge(turned, b * USES + t + 1)
                        act.activation(y_t[:, :, t * P:(t + 1) * P], turn_ps[t % 2][:, :].rearrange(
                            "p (c n) -> p c n", c=KD), ACT.Copy).then_inc(turn_free, 1)
                    for i in range(TILES + LAG + 2):
                        if i < TILES:
                            act.wait_ge(max_ready, b * TILES + i + 1)
                            act.activation(expo[:, i % NE, :], score_ps[i % 2][:, :], ACT.Exp,
                                           bias=neg_max[:, i % 8:i % 8 + 1], accum_out=sums[:, i % 8:i % 8 + 1]
                                           ).then_inc(exp_done, 1)
                        n = i - LAG
                        if 0 <= n < TILES:
                            h, t = n // NT, n % NT
                            act.wait_ge(turned, b * USES + NT + n + 1)
                            if t == 0:
                                act.wait_ge(latent_filled, b * XH + h + 1)
                            act.activation(probs_t[:, h % 2, :, t * P:(t + 1) * P],
                                           turn_ps[n % 2][:, :].rearrange("p (k n) -> p k n", k=NT), ACT.Copy
                                           ).then_inc(turn_free, 1)
                        if n >= 2 * NT and n % NT == 1 and n // NT - 2 < XH:
                            h = n // NT - 2
                            act.wait_ge(latent_filled, b * XH + h + 1 + 2)
                            act.activation(latent_t[:, h, :], latent_ps[h % 2][:, :], ACT.Copy).then_inc(latent_free, 1)
                    act.wait_ge(latent_filled, b * XH + XH + 2)
                    act.activation(latent_t[:, XH - 1, :], latent_ps[(XH - 1) % 2][:, :], ACT.Copy
                                   ).then_inc(latent_free, 1)

            @block.vector
            def _(dve):
                dve.sem_inc(project_free, 2)
                layernorm_stats(dve, None, x_res, stats, mean_var, std, rstd, ln_sems)[0]()
                with dve.Fori(0, B) as b:
                    for t in range(NT):
                        dve.tensor_scalar(expo[:, t, :], x_res[:, bass.ds(b * NT + t, 1), :].rearrange("p a c -> p (a c)"),
                                          mean_var[:, bass.ds(b * NT + t, 1), 0], rstd[:, bass.ds(b * NT + t, 1)],
                                          ALU.subtract, ALU.mult).then_inc(y_ready, 1)
                    dve.tensor_copy(kv_now[:, :, :], kv[:, bass.ds(b * NT, NT), :]).then_inc(kv_ready, 1)
                    for n in range(2 * XP):
                        dve.wait_ge(projected, b * PUSES + n + 1)
                        dve.tensor_copy([k_t, q_t][n // XP][:, n % XP, :], project_ps[n % 2][:, :]
                                        ).then_inc(project_free, 1)
                    for i in range(TILES + 1):
                        if i < TILES:
                            dve.wait_ge(scored, b * TILES + i + 1)
                            dve.tensor_reduce(neg_max[:, i % 8:i % 8 + 1], score_ps[i % 2][:, :], AX.X, ALU.max,
                                              negate=True).then_inc(max_ready, 1)
                        if i:
                            n = i - 1
                            dve.wait_ge(exp_done, b * TILES + n + 1 + 2)
                            dve.reciprocal(rsums[:, n % 8:n % 8 + 1], sums[:, n % 8:n % 8 + 1]).then_inc(rsum_ready, 1)
                            dve.wait_ge(rsum_ready, b * TILES + n + 1)
                            dve.tensor_scalar(expo[:, n % NE, :], expo[:, n % NE, :], rsums[:, n % 8:n % 8 + 1], None,
                                              ALU.mult).then_inc(probs_ready, 1)
                    for t in range(NT):
                        dve.wait_ge(projected, b * PUSES + 2 * XP + t + 1)
                        x_tile = x_res[:, bass.ds(b * NT + t, 1), :].rearrange("p a c -> p (a c)")
                        dve.tensor_tensor(x_tile, x_tile, project_ps[t % 2][:, :], ALU.add).then_inc(project_free, 1)


def gated_ffn_step(nc, sem, d, x_res, ident, out):
    with ExitStack() as outer:
        keep = lambda name, shape: outer.enter_context(nc.sbuf_tensor(name, shape, F32))
        up_w, gate_w = keep("f_up_w", [P, KD, DFF]), keep("f_gate_w", [P, KD, DFF])
        down_w = keep("f_down_w", [P, KF, D])
        hadamard = keep("f_hadamard", [P, P])
        su_up, su_down = keep("f_su_up", [P, KD]), keep("f_su_down", [P, KF])
        up_scale, gate_scale = keep("f_up_scale", [P, KF]), keep("f_gate_scale", [P, KF])
        down_scale = keep("f_down_scale", [P, D])
        ffn_loaded, small_loaded = sem("f_loaded"), sem("f_small_loaded")
        z_t = keep("f_z_t", [P, KF, N])
        scales_ready = sem("f_scales_ready")

        with ExitStack() as ctx:
            ps = lambda name, shape: ctx.enter_context(nc.psum_tensor(name, shape, F32))
            h_ps = [ps(f"f_h_ps{i}", [P, N]) for i in range(2)]
            down_loaded = sem("f_down_loaded")
            stage_done, filled, row_ready = sem("f_stage_done"), sem("f_h_filled"), sem("f_down_ready")
            block = ctx.enter_context(nc.Block())

            @block.sync
            def _(sp):
                sp.dma_start(down_w[:, :, :], d["down_t"]).then_inc(down_loaded, 16)
                sp.dma_start(up_w[:, :, :], d["up_t"]).then_inc(ffn_loaded, 16)
                sp.dma_start(gate_w[:, :, :], d["gate_t"]).then_inc(ffn_loaded, 16)

            @block.scalar
            def _(act):
                for dst, src in ((hadamard[:, :], d["hadamard"]), (su_up[:, :], d["su_up"]),
                                 (su_down[:, :], d["su_down"]), (up_scale[:, :], d["up_scale"]),
                                 (gate_scale[:, :], d["gate_scale"]),
                                 (down_scale[:, :], d["down_scale"].partition_broadcast(P))):
                    act.dma_start(dst, src).then_inc(small_loaded, 16)

            @block.vector
            def _(dve):
                dve.wait_ge(small_loaded, 16 * 6)
                dve.tensor_scalar(up_scale[:, :], up_scale[:, :], float(D) ** -0.5, None, ALU.mult)
                dve.tensor_scalar(gate_scale[:, :], gate_scale[:, :], float(D) ** -0.5, None, ALU.mult)
                dve.tensor_scalar(down_scale[:, :], down_scale[:, :], float(DFF) ** -0.5, None, ALU.mult
                                  ).then_inc(scales_ready, 1)
                dve.wait_ge(down_loaded, 16)
                source, target = down_w, z_t
                done = 0
                for step in (1, 2, 4, 8):
                    pairs = lambda m: m[:, :, :].rearrange("p (a two s) o -> p a two (s o)", two=2, s=step)
                    s, t = pairs(source), pairs(target)
                    dve.tensor_tensor(t[:, :, 0], s[:, :, 0], s[:, :, 1], ALU.add).then_inc(stage_done, 1)
                    dve.tensor_tensor(t[:, :, 1], s[:, :, 0], s[:, :, 1], ALU.subtract).then_inc(stage_done, 1)
                    done += 2
                    dve.wait_ge(stage_done, done)
                    source, target = target, source
                dve.wait_ge(scales_ready, 1)
                for k in range(KF):
                    dve.wait_ge(filled, k + 1)
                    dve.scalar_tensor_tensor(down_w[:, k, :], h_ps[k % 2][:, :], su_down[:, k:k + 1],
                                             down_scale[:, :], ALU.mult, ALU.mult).then_inc(row_ready, 1)

            @block.tensor
            def _(pe):
                pe.wait_ge(stage_done, 8)
                for k in range(KF):
                    if k >= 2:
                        pe.wait_ge(row_ready, k - 1)
                    pe.matmul(h_ps[k % 2][:, :], hadamard[:, :], down_w[:, k, :], start=True, stop=True
                              ).then_inc(filled, 1)

        with ExitStack() as ctx:
            sb = lambda name, shape: ctx.enter_context(nc.sbuf_tensor(name, shape, F32))
            ps = lambda name, shape: ctx.enter_context(nc.psum_tensor(name, shape, F32))
            stats, mean_var = sb("f_stats", [P, T, 6]), sb("f_mean_var", [P, T, 2])
            std, rstd = sb("f_std", [P, T]), sb("f_rstd", [P, T])
            y = sb("f_y", [P, NT, D])
            y_t, mixed_t = sb("f_y_t", [P, KD, N]), sb("f_mixed_t", [P, KD, N])
            silu = sb("f_silu", [P, 2, N])
            turn_ps = [ps(f"f_turn_ps{i}", [P, N]) for i in range(2)]
            up_ps = [ps(f"f_up_ps{i}", [P, N]) for i in range(2)]
            gate_ps = [ps(f"f_gate_ps{i}", [P, N]) for i in range(2)]
            down_ps = [ps(f"f_down_ps{i}", [P, N]) for i in range(2)]
            ln_sems = [sem("f_stats_done"), sem("f_var_done"), sem("f_std_done"), sem("f_rstd_done")]
            y_ready, turned, turn_free = sem("f_y_ready"), sem("f_turned"), sem("f_turn_free")
            mix_step, mixed_ready = sem("f_mix_step"), sem("f_mixed_ready")
            gate_filled, silu_ready, z_ready = sem("f_gate_filled"), sem("f_silu_ready"), sem("f_z_ready")
            down_filled, down_free, stored = sem("f_down_filled"), sem("f_down_free"), sem("f_stored")
            USES = 2 * KD
            block = ctx.enter_context(nc.Block())

            @block.sync
            def _(sp):
                out_v = out.rearrange("b (t p) c -> b p t c", p=P)
                with sp.Fori(0, B) as b:
                    sp.wait_ge(down_free, b * NT + NT + 2)
                    sp.dma_start(out_v[bass.ds(b, 1)].rearrange("a p t c -> (a p) t c"),
                                 x_res[:, bass.ds(b * NT, NT), :]).then_inc(stored, 16)
                sp.wait_ge(stored, 16 * B)

            @block.tensor
            def _(pe):
                pe.wait_ge(ffn_loaded, 32)
                with pe.Fori(0, B) as b:
                    pe.wait_ge(y_ready, b * NT + NT)
                    for c in range(KD):
                        pe.wait_ge(turn_free, b * USES + c + 1)
                        for t in range(NT):
                            last = pe.transpose(turn_ps[c % 2][:, t * P:(t + 1) * P], y[:, t, c * P:(c + 1) * P],
                                                ident[:, :])
                        last.then_inc(turned, 1)
                    pe.wait_ge(mix_step, b * 4 + 4)
                    for c in range(KD):
                        pe.wait_ge(turn_free, b * USES + KD + c + 1)
                        pe.matmul(turn_ps[c % 2][:, :], hadamard[:, :], y_t[:, c, :], start=True, stop=True
                                  ).then_inc(turned, 1)
                    pe.wait_ge(turn_free, b * USES + 2 * KD + 2)
                    for f in range(KF):
                        pe.wait_ge(z_ready, b * KF + f + 1)
                        for w, o in ((gate_w, gate_ps), (up_w, up_ps)):
                            for c in range(KD):
                                last = pe.matmul(o[f % 2][:, :], w[:, c, f * P:(f + 1) * P], mixed_t[:, c, :],
                                                 start=(c == 0), stop=(c == KD - 1))
                        last.then_inc(gate_filled, 1)
                    for t in range(NT):
                        pe.wait_ge(down_free, b * NT + t + 1)
                        for f in range(KF):
                            if t == 0:
                                pe.wait_ge(z_ready, b * KF + f + 1 + 2)
                            last = pe.matmul(down_ps[t % 2][:, :], z_t[:, f, t * P:(t + 1) * P], down_w[:, f, :],
                                             start=(f == 0), stop=(f == KF - 1))
                        last.then_inc(down_filled, 1)

            @block.scalar
            def _(act):
                act.sem_inc(turn_free, 2)
                layernorm_stats(None, act, x_res, stats, mean_var, std, rstd, ln_sems)[1]()
                with act.Fori(0, B) as b:
                    for c in range(KD):
                        act.wait_ge(turned, b * USES + c + 1)
                        act.activation(y_t[:, c, :], turn_ps[c % 2][:, :], ACT.Copy, scale=su_up[:, c:c + 1]
                                       ).then_inc(turn_free, 1)
                    for c in range(KD):
                        act.wait_ge(turned, b * USES + KD + c + 1)
                        act.activation(mixed_t[:, c, :], turn_ps[c % 2][:, :], ACT.Copy).then_inc(turn_free, 1)
                    for f in range(KF):
                        act.wait_ge(gate_filled, b * KF + f + 1)
                        act.wait_ge(z_ready, b * KF + f + 1)
                        act.activation(silu[:, f % 2, :], gate_ps[f % 2][:, :], ACT.Silu,
                                       scale=gate_scale[:, f:f + 1]).then_inc(silu_ready, 1)

            @block.vector
            def _(dve):
                dve.sem_inc(z_ready, 2)
                dve.sem_inc(down_free, 2)
                layernorm_stats(dve, None, x_res, stats, mean_var, std, rstd, ln_sems)[0]()
                with dve.Fori(0, B) as b:
                    for t in range(NT):
                        dve.tensor_scalar(y[:, t, :], x_res[:, bass.ds(b * NT + t, 1), :].rearrange("p a c -> p (a c)"),
                                          mean_var[:, bass.ds(b * NT + t, 1), 0], rstd[:, bass.ds(b * NT + t, 1)],
                                          ALU.subtract, ALU.mult).then_inc(y_ready, 1)
                    dve.wait_ge(turn_free, b * USES + KD + 2)
                    done = 0
                    for step, source, target in ((1, y_t, mixed_t), (2, mixed_t, y_t)):
                        pairs = lambda m: m[:, :, :].rearrange("p (a two s) n -> p a two (s n)", two=2, s=step)
                        s, t = pairs(source), pairs(target)
                        dve.tensor_tensor(t[:, :, 0], s[:, :, 0], s[:, :, 1], ALU.add).then_inc(mix_step, 1)
                        dve.tensor_tensor(t[:, :, 1], s[:, :, 0], s[:, :, 1], ALU.subtract).then_inc(mix_step, 1)
                        done += 2
                        dve.wait_ge(mix_step, b * 4 + done)
                    for f in range(KF):
                        dve.wait_ge(silu_ready, b * KF + f + 1)
                        dve.scalar_tensor_tensor(z_t[:, f, :], up_ps[f % 2][:, :], up_scale[:, f:f + 1],
                                                 silu[:, f % 2, :], ALU.mult, ALU.mult).then_inc(z_ready, 1)
                    for t in range(NT):
                        dve.wait_ge(down_filled, b * NT + t + 1)
                        x_tile = x_res[:, bass.ds(b * NT + t, 1), :].rearrange("p a c -> p (a c)")
                        dve.tensor_tensor(x_tile, x_tile, down_ps[t % 2][:, :], ALU.add).then_inc(down_free, 1)


def build(nc, a, out):
    with ExitStack() as ctx:
        sem = lambda name: ctx.enter_context(nc.semaphore(name))
        x_res = ctx.enter_context(nc.sbuf_tensor("x_res", [P, T, D], F32))
        ident = ctx.enter_context(nc.sbuf_tensor("ident", [P, P], F32))
        ident_ready = sem("ident_ready")
        with ExitStack() as ffn:
            ffn_w1 = ffn.enter_context(nc.sbuf_tensor("ffn_w1", [P, KD, DFF], F32))
            ffn_w2 = ffn.enter_context(nc.sbuf_tensor("ffn_w2", [P, KF, D], F32))
            ffn_loaded = sem("ffn_loaded")
            with nc.Block() as block:
                @block.sync
                def _(sp):
                    sp.dma_start(ident[:, :], a["ident"]).then_inc(ident_ready, 16)

            gat_step(nc, sem, dict(x=a["x"], ctx_t=a["ctx_t"], W0=a["gat_w0"], W1=a["gat_w1"],
                                   a_self0=a["L0_xattn_a_self0"], a_neigh0=a["L0_xattn_a_neigh0"],
                                   a_self1=a["L0_xattn_a_self1"], a_neigh1=a["L0_xattn_a_neigh1"],
                                   b0=a["gat_b0"], b1=a["gat_b1"], ffn_w1=a["ffn_w1"], ffn_w2=a["ffn_w2"]),
                     x_res, ident, ident_ready, ffn_w1, ffn_w2, ffn_loaded)
            routed_ffn_step(nc, sem, dict(Wr=a["L0_ffn_Wr"], br=a["L0_ffn_br"], b1=a["ffn_b1"], b2=a["L0_ffn_b2"],
                                          before=a["before"], not_before=a["not_before"], slots=a["slots"],
                                          ones=a["ones"]), x_res, ident, ffn_w1, ffn_w2, ffn_loaded)
        cross_attention_step(nc, sem, dict(wq=a["wq"], kcq=a["kcq"], wqr=a["wqr"],
                                           wo=a["wo"], kckv=a["kckv"], wkr=a["wkr"],
                                           ctx=a["ctx_512"], ctx_t=a["ctx_t"], cos=a["cos"], sin=a["sin"],
                                           cos_t=a["cos_t"], sin_t=a["sin_t"]), x_res, ident)
        gated_ffn_step(nc, sem, dict(up_t=a["up_t"], gate_t=a["gate_t"], down_t=a["down_t"],
                                     hadamard=a["hadamard"], su_up=a["su_up"], su_down=a["su_down"],
                                     up_scale=a["up_scale"], gate_scale=a["gate_scale"],
                                     down_scale=a["L1_ffn_Wscale_dp"]), x_res, ident, out)


def laid_out(i):
    def pairs(v):
        return i[v].reshape(GP, 2 * GO).T

    def columns(v):
        return v.reshape(-1, P).T

    def swap(v, *axes):
        return i[v].transpose(axes)

    def chunked(m):
        return m.reshape(-1, P, *m.shape[1:]).swapaxes(0, 1)

    names = ["x", "ctx_512", "L0_xattn_a_self0", "L0_xattn_a_neigh0", "L0_xattn_a_self1", "L0_xattn_a_neigh1",
             "L0_ffn_Wr", "L0_ffn_br", "L0_ffn_b2", "L1_ffn_Wscale_dp"]
    return {**{n: i[n] for n in names}, "ctx_t": swap("ctx_512", 0, 2, 1),
            "gat_w0": swap("L0_xattn_W0", 1, 0, 2).reshape(F_IN, -1),
            "gat_w1": chunked(swap("L0_xattn_W1", 1, 0, 2).reshape(D, -1)),
            "gat_b0": pairs("L0_xattn_b0"), "gat_b1": pairs("L0_xattn_b1"),
            "ffn_w1": chunked(i["L0_ffn_W1"]), "ffn_w2": chunked(i["L0_ffn_W2"]), "ffn_b1": columns(i["L0_ffn_b1"]),
            "kcq": chunked(swap("L1_xattn_w_kc_q", 2, 0, 1)), "wqr": chunked(swap("L1_xattn_W_qr", 1, 0, 2)),
            "wq": chunked(i["L1_xattn_Wq"]), "wo": chunked(swap("L1_xattn_Wo", 1, 0)),
            "kckv": swap("L1_xattn_w_kc_kv", 1, 0, 2), "wkr": swap("L1_xattn_W_kr", 1, 0, 2),
            "up_t": chunked(swap("L1_ffn_W_up", 1, 0)), "gate_t": chunked(swap("L1_ffn_W_gate", 1, 0)),
            "down_t": chunked(swap("L1_ffn_W_down", 1, 0)),
            "su_up": columns(i["L1_ffn_SU_ug"]), "su_down": columns(i["L1_ffn_SU_dp"]),
            "up_scale": columns(i["L1_ffn_Wscale_ug"][:DFF]), "gate_scale": columns(i["L1_ffn_Wscale_ug"][DFF:])}


def constants():
    import numpy as np
    f32 = np.float32
    row, column = np.arange(N).reshape(NT, P).T[:, :, None], np.arange(N)[None, None, :]
    slots = np.full((P, 2, P), -1.0, f32)
    for g in range(2):
        slots[:, g, g * TOPK:(g + 1) * TOPK] = np.arange(TOPK)
    inv_freq = f32(1.0) / f32(10000.0) ** (np.arange(0, F_IN, 2, dtype=f32) / f32(F_IN))
    freqs = np.arange(N, dtype=f32)[:, None] * inv_freq[None, :]
    cos = np.repeat(np.cos(freqs), 2, axis=-1)
    sin = np.repeat(np.sin(freqs), 2, axis=-1)
    sin[:, :F_IN // 2] *= f32(-1.0)
    rows = lambda m: m.reshape(NT, P, F_IN).transpose(1, 0, 2)
    hadamard = np.ones((1, 1), f32)
    while hadamard.shape[0] < P:
        hadamard = np.block([[hadamard, hadamard], [hadamard, -hadamard]])
    return {"cos": np.ascontiguousarray(rows(cos)), "sin": np.ascontiguousarray(rows(sin)),
            "cos_t": np.ascontiguousarray(cos.T), "sin_t": np.ascontiguousarray(sin.T), "hadamard": hadamard,
            "ident": np.eye(P, dtype=f32), "ones": np.ones((P, P), f32), "slots": slots,
            "before": (column < row).astype(f32), "not_before": (column >= row).astype(f32)}


def kernel(**inputs):
    import numpy as np
    import concourse.bacc as bacc
    from concourse.bass_utils import run_bass_kernel_spmd as run

    nc = bacc.Bacc("TRN2", target_bir_lowering=False, num_devices=1)
    arrays = {name: np.ascontiguousarray(v) for name, v in laid_out(inputs).items()}
    arrays.update(constants())
    a = {name: nc.dram_tensor(f"in_{name}", v.shape, F32, kind="ExternalInput").ap() for name, v in arrays.items()}
    out = nc.dram_tensor("out", (B, N, D), F32, kind="ExternalOutput").ap()
    build(nc, a, out)
    r = run(nc, [{f"in_{name}": v for name, v in arrays.items()}], core_ids=[0])
    return r.results[0]["out"]
```

```python
from contextlib import ExitStack

import concourse.bass as bass
from concourse import mybir

ALU = mybir.AluOpType
ACT = mybir.ActivationFunctionType
AX = mybir.AxisListType
F32 = mybir.dt.float32

P = 128
B, N, D = 4, 512, 512
NT = N // P
T = B * NT
KD = D // P
F_IN = 128
GH, GO = 8, 64
GP = GH // 2
TOPK = N // 8
DFF = 4 * D
KF = DFF // P
XH, XR = 16, 64
DCQ = 384
LN_EPS = 1e-5
MASK_VAL = -1.0e10
SLOPE = 0.2
BIG = 3.0e38


def layernorm_stats(dve, act, x_res, stats, mean_var, std, rstd, sems):
    stats_done, var_done, std_done, rstd_done = sems

    def on_vector(before=lambda t: None):
        for t in range(T):
            before(t)
            dve.bn_stats(stats[:, t, :], x_res[:, t, :]).then_inc(stats_done, 1)
        dve.wait_ge(stats_done, T)
        for t in range(T):
            dve.bn_aggr(mean_var[:, t, :], stats[:, t, :]).then_inc(stats_done, 1)
        dve.wait_ge(stats_done, 2 * T)
        dve.tensor_scalar(std[:, :], mean_var[:, :, 1], LN_EPS, None, ALU.add).then_inc(var_done, 1)
        dve.wait_ge(std_done, 1)
        dve.reciprocal(rstd[:, :], std[:, :]).then_inc(rstd_done, 1)
        dve.wait_ge(rstd_done, 1)

    def on_scalar():
        act.wait_ge(var_done, 1)
        act.activation(std[:, :], std[:, :], ACT.Sqrt).then_inc(std_done, 1)

    return on_vector, on_scalar


def gat_step(nc, sem, d, x_res, ident, ident_ready, ffn_w1, ffn_w2, ffn_loaded):
    with ExitStack() as ctx:
        sb = lambda name, shape: ctx.enter_context(nc.sbuf_tensor(name, shape, F32))
        ps = lambda name, shape: ctx.enter_context(nc.psum_tensor(name, shape, F32))

        mean_var = sb("g_mean_var", [P, T, 2])
        std, rstd = sb("g_std", [P, T]), sb("g_rstd", [P, T])
        weights = [sb("g_w0", [P, 1, GH * GO]), sb("g_w1", [P, KD, GH * GO])]
        vectors = [sb("g_v0", [P, 1, 2 * GH]), sb("g_v1", [P, KD, 2 * GH])]
        a_rows = sb("g_a_rows", [P, 4, GH * GO])
        bias = sb("g_bias", [P, 2, GP])
        ctx_in = sb("g_ctx_in", [P, B, N])
        ctx_t = sb("g_ctx_t", [P, 1, N])
        hidden_t = sb("g_hidden_t", [P, GP, N])
        last_t = sb("g_last_t", [P, GP, N])
        mask = sb("g_mask", [P, NT, N])
        row_min, mask_max = sb("g_row_min", [P, NT]), sb("g_mask_max", [P, NT])
        feat = sb("g_feat", [P, NT, GH * GO])
        self_neigh = sb("g_self_neigh", [P, NT, 2 * GH])
        self_part = sb("g_self_part", [P, NT, GH])
        neigh_row = sb("g_neigh_row", [P, 2, N])
        NA, NE = 4, 5
        base = sb("g_base", [P, NA, N])
        expo = sb("g_expo", [P, NE, N])
        neg_max, sums, rsums = sb("g_neg_max", [P, 8]), sb("g_sums", [P, 8]), sb("g_rsums", [P, 8])
        probs_t = sb("g_probs_t", [P, 2, NT, N])
        low, high = sb("g_low", [P, N]), sb("g_high", [P, N])
        product = low
        stats = high[:, 0:T * 6].rearrange("p (t s) -> p t s", t=T)

        neigh_ps = [ps(f"g_neigh_ps{i}", [P, N]) for i in range(2)]
        relu_ps = [ps(f"g_relu_ps{i}", [P, N]) for i in range(2)]
        turn_ps = [ps(f"g_turn_ps{i}", [P, N]) for i in range(2)]
        out_ps = [ps(f"g_out_ps{i}", [P, N]) for i in range(2)]

        x_loaded, w_loaded = sem("g_x_loaded"), sem("g_w_loaded")
        ctx_loaded, ctx_ready = sem("g_ctx_loaded"), sem("g_ctx_ready")
        ln_sems = [sem("g_stats_done"), sem("g_var_done"), sem("g_std_done"), sem("g_rstd_done")]
        product_done, vectors_ready = sem("g_product_done"), sem("g_vectors_ready")
        mask_step, parts_ready = sem("g_mask_step"), sem("g_parts_ready")
        neigh_filled, row_ready, base_ready = sem("g_neigh_filled"), sem("g_row_ready"), sem("g_base_ready")
        relu_ready, expo_ready, exp_done = sem("g_relu_ready"), sem("g_expo_ready"), sem("g_exp_done")
        rsum_ready, probs_ready = sem("g_rsum_ready"), sem("g_probs_ready")
        turned, turn_free = sem("g_turned"), sem("g_turn_free")
        attn_done, out_free = sem("g_attn_done"), sem("g_out_free")
        low_ready, low_exp, hidden_ready = sem("g_low_ready"), sem("g_low_exp"), sem("g_hidden_ready")
        high_ready = sem("g_high_ready")
        row_store = sem("g_row_store")

        TILES = GH * NT
        L_USES = 1 + NT + TILES
        USES = 2 * L_USES + NT
        assert USES % 2 == 0
        LAG = 4

        def use_of(layer, k):
            return layer * L_USES + k

        butterflies = DownButterflies(sem, d["down_t"], d["down_turned"], a_rows, sb)
        block = ctx.enter_context(nc.Block())

        @block.sync
        def _(sp):
            for b in range(B):
                sp.dma_start(x_res[:, b * NT:(b + 1) * NT, :],
                             d["x"][b].rearrange("(t p) c -> p t c", p=P)).then_inc(x_loaded, 16)
                sp.dma_start(ctx_in[:, b, :], d["ctx_t"][b]).then_inc(ctx_loaded, 16)
            sp.wait_ge(w_loaded, 16 * 8)
            sp.dma_start(ffn_w1[:, :, :], d["ffn_w1"]).then_inc(ffn_loaded, 16)
            sp.dma_start(ffn_w2[:, :, :], d["ffn_w2"]).then_inc(ffn_loaded, 16)
            sp.sem_inc(butterflies.stored, 16)
            sp.wait_ge(vectors_ready, 2 + 2 * KD)
            butterflies.load_and_store(sp)

        @block.gpsimd
        def _(pool):
            pool.sem_inc(base_ready, 8)
            with pool.Fori(0, B) as b:
                for layer in range(2):
                    for h in range(GH):
                        for t in range(NT):
                            j = (layer * GH + h) * NT + t
                            pool.wait_ge(row_ready, b * 2 * GH + layer * GH + h + 1)
                            pool.wait_ge(expo_ready, b * 2 * TILES + j + 1)
                            pool.tensor_tensor(base[:, j % NA, :], mask[:, t, :], neigh_row[:, h % 2, :],
                                               ALU.add).then_inc(base_ready, 1)
                        if h % 2:
                            butterflies.step(pool, b, layer * GH // 2 + h // 2)

        @block.tensor
        def _(pe):
            pe.sem_inc(attn_done, 2)
            pe.wait_ge(ident_ready, 16)
            pe.wait_ge(vectors_ready, 2 + 2 * KD)
            with pe.Fori(0, B) as b:
                def turn(u, pieces, source_ready=None):
                    pe.wait_ge(turn_free, b * USES + u + 1)
                    if source_ready:
                        pe.wait_ge(*source_ready)
                    for c, piece in enumerate(pieces):
                        last = pe.transpose(turn_ps[u % 2][:, c * P:(c + 1) * P], piece, ident[:, :])
                    last.then_inc(turned, 1)

                for layer in range(2):
                    source = [ctx_t, hidden_t][layer]
                    chunks = [1, KD][layer]
                    if layer == 0:
                        pe.wait_ge(ctx_ready, b + 1)
                    else:
                        pe.wait_ge(hidden_ready, b * 2 * GP + GP)
                    u = use_of(layer, 0)
                    pe.wait_ge(turn_free, b * USES + u + 1)
                    for t in range(NT):
                        for c in range(chunks):
                            last = pe.matmul(turn_ps[u % 2][:, t * 2 * GH:(t + 1) * 2 * GH],
                                             source[:, c, t * P:(t + 1) * P], vectors[layer][:, c, :],
                                             start=(c == 0), stop=(c == chunks - 1))
                    last.then_inc(turned, 1)

                    def feature(t):
                        u = use_of(layer, 1 + t)
                        pe.wait_ge(turn_free, b * USES + u + 1)
                        for c in range(chunks):
                            last = pe.matmul(turn_ps[u % 2][:, :], source[:, c, t * P:(t + 1) * P],
                                             weights[layer][:, c, :], start=(c == 0), stop=(c == chunks - 1))
                        last.then_inc(turned, 1)

                    def neighbour(h):
                        g = layer * GH + h
                        if h == 0:
                            pe.wait_ge(turn_free, b * USES + use_of(layer, 0) + 1 + 2)
                        pe.wait_ge(relu_ready, b * 2 * TILES + 4 * g + 4)
                        for t in range(NT):
                            last = pe.transpose(neigh_ps[g % 2][:, t * P:(t + 1) * P],
                                                self_neigh[:, t, GH + h:GH + h + 1].to_broadcast([P, P]),
                                                ident[:, :])
                        last.then_inc(neigh_filled, 1)

                    def attend(h, ks):
                        g = layer * GH + h
                        q = layer * GP + h // 2
                        if ks[0] == 0:
                            pe.wait_ge(turn_free, b * USES + use_of(layer, 1 + NT + h * NT + NT - 1) + 1 + 2)
                            if h % 2 == 0:
                                pe.wait_ge(out_free, b * 2 * GP + q + 1)
                        half = (h % 2) * GO
                        for k in ks:
                            last = pe.matmul(out_ps[q % 2][half:half + GO, :], feat[:, k, h * GO:(h + 1) * GO],
                                             probs_t[:, g % 2, k, :], start=(k == 0), stop=(k == NT - 1))
                        if ks[-1] == NT - 1:
                            last.then_inc(attn_done, 1)

                    neighbour(0)
                    feature(0)
                    neighbour(1)
                    for t in range(1, NT):
                        feature(t)
                    for h in range(GH):
                        for t in range(NT):
                            j = layer * TILES + h * NT + t
                            turn(use_of(layer, 1 + NT + h * NT + t),
                                 [expo[:, j % NE, c * P:(c + 1) * P] for c in range(NT)],
                                 (probs_ready, b * 2 * TILES + j + 1))
                            if h and t == 2:
                                attend(h - 1, [0, 1])
                            if t == 3 and h + 2 < GH:
                                neighbour(h + 2)
                            if h and t == 3:
                                attend(h - 1, [2, 3])
                    attend(GH - 1, [0, 1, 2, 3])
                pe.wait_ge(hidden_ready, b * 2 * GP + 2 * GP)
                for t in range(NT):
                    turn(use_of(2, t), [last_t[:, c, t * P:(t + 1) * P] for c in range(GP)])

        @block.scalar
        def _(act):
            act.sem_inc(relu_ready, 8)
            for i, name in enumerate(("a_self0", "a_neigh0", "a_self1", "a_neigh1")):
                act.dma_start(a_rows[:, i, :], d[name].rearrange("h o -> (h o)").partition_broadcast(P)
                              ).then_inc(w_loaded, 16)
            act.dma_start(weights[0][:, 0, :], d["W0"]).then_inc(w_loaded, 16)
            act.dma_start(weights[1][:, :, :], d["W1"]).then_inc(w_loaded, 16)
            for i, name in enumerate(("b0", "b1")):
                act.dma_start(bias[:, i, :], d[name]).then_inc(w_loaded, 16)
            layernorm_stats(None, act, x_res, stats, mean_var, std, rstd, ln_sems)[1]()
            with act.Fori(0, B) as b:
                for layer in range(2):
                    def elu_exp(q):
                        act.wait_ge(low_ready, b * 2 * GP + layer * GP + q + 1)
                        act.activation(low[:, :], low[:, :], ACT.Exp).then_inc(low_exp, 1)

                    def neighbour_row(h):
                        g = layer * GH + h
                        act.wait_ge(neigh_filled, b * 2 * GH + g + 1)
                        act.wait_ge(base_ready, b * 2 * TILES + 4 * g + 4)
                        act.activation(neigh_row[:, g % 2, :], neigh_ps[g % 2][:, :], ACT.Copy, scale=SLOPE
                                       ).then_inc(row_ready, 1)

                    neighbour_row(0)
                    for i in range(TILES + 1):
                        if i < TILES:
                            h, t = i // NT, i % NT
                            g = layer * GH + h
                            j = layer * TILES + i
                            if i == 0:
                                act.wait_ge(parts_ready, b * 2 + layer + 1)
                            act.wait_ge(expo_ready, b * 2 * TILES + j - 2 + 1 + NA)
                            act.activation(relu_ps[j % 2][:, :], neigh_ps[g % 2][:, :], ACT.Relu,
                                           bias=self_part[:, t, h:h + 1], scale=1.0 - SLOPE
                                           ).then_inc(relu_ready, 1)
                        if i:
                            j = layer * TILES + i - 1
                            act.wait_ge(expo_ready, b * 2 * TILES + j + 1 + NA)
                            act.activation(expo[:, j % NE, :], expo[:, j % NE, :], ACT.Exp,
                                           bias=neg_max[:, j % 8:j % 8 + 1], scale=-1.0,
                                           accum_out=sums[:, j % 8:j % 8 + 1]).then_inc(exp_done, 1)
                        if i % NT == 2 and i // NT + 1 < GH:
                            neighbour_row(i // NT + 1)
                        if i in (17, 25):
                            elu_exp((i - 17) // 8)
                    elu_exp(2)
                    elu_exp(3)

        @block.vector
        def _(dve):
            dve.sem_inc(expo_ready, NA)
            dve.sem_inc(turn_free, 2)
            dve.sem_inc(out_free, 2)
            dve.wait_ge(w_loaded, 16 * 8)
            dve.wait_ge(ctx_loaded, 16 * B)
            n_products = 0
            for layer in range(2):
                for c in range([1, KD][layer]):
                    for side in range(2):
                        if n_products:
                            dve.wait_ge(vectors_ready, n_products)
                        dve.tensor_tensor(product[:, :], weights[layer][:, c, :], a_rows[:, 2 * layer + side, :],
                                          ALU.mult).then_inc(product_done, 1)
                        n_products += 1
                        dve.wait_ge(product_done, n_products)
                        dve.tensor_reduce(vectors[layer][:, c, side * GH:(side + 1) * GH],
                                          product[:, :].rearrange("p (h o) -> p h o", h=GH), AX.X, ALU.add
                                          ).then_inc(vectors_ready, 1)
            layernorm_stats(dve, None, x_res, stats, mean_var, std, rstd, ln_sems)[0](
                lambda t: dve.wait_ge(x_loaded, 16 * (t // NT + 1)) if t % NT == 0 else None)
            with dve.Fori(0, B) as b:
                M_STEPS = 2 * NT + NT + 1 + NT
                for t in range(NT):
                    dve.tensor_scalar(mask[:, t, :], x_res[:, bass.ds(b * NT + t, 1), :].rearrange("p a c -> p (a c)"),
                                      mean_var[:, bass.ds(b * NT + t, 1), 0], rstd[:, bass.ds(b * NT + t, 1)],
                                      ALU.subtract, ALU.mult).then_inc(mask_step, 1)
                dve.wait_ge(mask_step, b * M_STEPS + NT)
                for t in range(NT):
                    dve.tensor_scalar(mask[:, t, :], mask[:, t, :], -1.0, 1.0, ALU.mult, ALU.add
                                      ).then_inc(mask_step, 1)
                dve.wait_ge(mask_step, b * M_STEPS + 2 * NT)
                for t in range(NT):
                    dve.tensor_reduce(row_min[:, t:t + 1], mask[:, t, :], AX.X, ALU.min).then_inc(mask_step, 1)
                dve.wait_ge(mask_step, b * M_STEPS + 3 * NT)
                dve.tensor_scalar(mask_max[:, :], row_min[:, :], MASK_VAL, None, ALU.mult).then_inc(mask_step, 1)
                dve.wait_ge(mask_step, b * M_STEPS + 3 * NT + 1)
                for t in range(NT):
                    dve.tensor_scalar(mask[:, t, :], mask[:, t, :], MASK_VAL, mask_max[:, t:t + 1],
                                      ALU.mult, ALU.subtract).then_inc(mask_step, 1)

                dve.tensor_copy(ctx_t[:, :, :], ctx_in[:, bass.ds(b, 1), :]).then_inc(ctx_ready, 1)

                for layer in range(2):
                    target = [hidden_t, last_t][layer]
                    u = use_of(layer, 0)
                    dve.wait_ge(turned, b * USES + u + 1)
                    columns = turn_ps[u % 2][:, 0:NT * 2 * GH].rearrange("p (t h) -> p t h", t=NT)
                    dve.tensor_scalar(self_part[:, :, :], columns[:, :, 0:GH], 1.0 - SLOPE, None, ALU.mult
                                      ).then_inc(parts_ready, 1)
                    dve.tensor_copy(self_neigh[:, :, :], columns).then_inc(turn_free, 1)

                    def copy(k):
                        u = use_of(layer, 1 + k)
                        dve.wait_ge(turned, b * USES + u + 1)
                        if k < NT:
                            dve.tensor_copy(feat[:, k, :], turn_ps[u % 2][:, :]).then_inc(turn_free, 1)
                            return
                        h, t = (k - NT) // NT, (k - NT) % NT
                        g = layer * GH + h
                        if t == 0:
                            dve.wait_ge(attn_done, b * 2 * GH + g + 1)
                        dve.tensor_copy(probs_t[:, g % 2, :, t * P:(t + 1) * P],
                                        turn_ps[u % 2][:, :].rearrange("p (k n) -> p k n", k=NT)
                                        ).then_inc(turn_free, 1)

                    def elu_parts(q):
                        gq = layer * GP + q
                        dve.wait_ge(attn_done, b * 2 * GH + 2 * gq + 2 + 2)
                        dve.tensor_scalar(low[:, :], out_ps[gq % 2][:, :], bias[:, layer, q:q + 1], 0.0,
                                          ALU.add, ALU.min).then_inc(low_ready, 1)
                        dve.tensor_scalar(high[:, :], out_ps[gq % 2][:, :], bias[:, layer, q:q + 1], 0.0,
                                          ALU.add, ALU.max).then_inc(out_free, 1)

                    def elu_sum(q):
                        gq = layer * GP + q
                        dve.wait_ge(low_exp, b * 2 * GP + gq + 1)
                        dve.wait_ge(out_free, b * 2 * GP + gq + 1 + 2)
                        dve.scalar_tensor_tensor(target[:, q, :], low[:, :], -1.0, high[:, :], ALU.add, ALU.add
                                                 ).then_inc(hidden_ready, 1)

                    for i in range(TILES + NT + LAG):
                        if i < TILES:
                            j = layer * TILES + i
                            dve.wait_ge(relu_ready, b * 2 * TILES + j + 1 + 8)
                            dve.wait_ge(base_ready, b * 2 * TILES + j + 1 + 8)
                        if i < TILES + LAG:
                            copy(i)
                        if i < TILES:
                            dve.tensor_tensor_reduce(expo[:, j % NE, :], relu_ps[j % 2][:, :], base[:, j % NA, :],
                                                     -1.0, BIG, ALU.add, ALU.min, neg_max[:, j % 8:j % 8 + 1]
                                                     ).then_inc(expo_ready, 1)
                        if 1 <= i <= TILES:
                            j = layer * TILES + i - 1
                            dve.wait_ge(exp_done, b * 2 * TILES + j + 1)
                            dve.reciprocal(rsums[:, j % 8:j % 8 + 1], sums[:, j % 8:j % 8 + 1]).then_inc(rsum_ready, 1)
                            dve.wait_ge(rsum_ready, b * 2 * TILES + j + 1)
                            dve.tensor_scalar(expo[:, j % NE, :], expo[:, j % NE, :], rsums[:, j % 8:j % 8 + 1], None,
                                              ALU.mult).then_inc(probs_ready, 1)
                        if i in (16, 24, 32):
                            elu_parts((i - 16) // 8)
                        if i in (18, 26, 34):
                            elu_sum((i - 18) // 8)
                    elu_parts(3)
                    elu_sum(3)

                for t in range(NT):
                    u = use_of(2, t)
                    dve.wait_ge(turned, b * USES + u + 1)
                    x_tile = x_res[:, bass.ds(b * NT + t, 1), :].rearrange("p a c -> p (a c)")
                    dve.tensor_tensor(x_tile, x_tile, turn_ps[u % 2][:, :], ALU.add).then_inc(turn_free, 1)


class DownButterflies:

    def __init__(self, sem, source, target, room, sb):
        self.source, self.target = source, target
        self.COLS = D // B
        self.a = room[:, :, :].rearrange("p a (k o) -> p (a k) o", o=self.COLS)
        self.b = sb("b_b", [P, KF, self.COLS])
        self.loaded, self.butterfly, self.stored = sem("b_loaded"), sem("b_butterfly"), sem("b_stored")
        self.STEPS = 8

    def load_and_store(self, sp):
        with sp.Fori(0, B) as s:
            sp.wait_ge(self.stored, 16 * s + 16)
            sp.dma_start(self.a[:, :, :], self.source[:, :, bass.ds(s * self.COLS, self.COLS)]
                         ).then_inc(self.loaded, 16)
            sp.wait_ge(self.butterfly, self.STEPS * (s + 1))
            sp.dma_start(self.target[:, :, bass.ds(s * self.COLS, self.COLS)], self.a[:, :, :]
                         ).then_inc(self.stored, 16)
        sp.wait_ge(self.stored, 16 * (B + 1))

    def step(self, pool, s, n):
        if n == 0:
            pool.wait_ge(self.loaded, 16 * (s + 1))
        else:
            pool.wait_ge(self.butterfly, self.STEPS * s + n // 2 * 2)
        source, target = (self.a, self.b) if n // 2 % 2 == 0 else (self.b, self.a)
        halves = lambda m: m[:, :, :].rearrange("p (g two s) o -> p g two (s o)", two=2, s=1 << (n // 2))
        x, y = halves(source), halves(target)
        pool.tensor_tensor(y[:, :, n % 2], x[:, :, 0], x[:, :, 1], [ALU.add, ALU.subtract][n % 2]
                           ).then_inc(self.butterfly, 1)


class DownWeights:

    def __init__(self, sem, d, target, sb, ps):
        self.d, self.target, self.ps = d, target, ps
        self.K = 4
        self.turned = sb("d_turned", [P, 2, self.K, D])
        self.mixed = sb("d_mixed", [P, self.K, D])
        self.hadamard, self.signs, self.scale = sb("d_hadamard", [P, P]), sb("d_signs", [P, KF]), sb("d_scale", [P, D])
        self.small_loaded, self.loaded = sem("d_small_loaded"), [sem("d_loaded0"), sem("d_loaded1")]
        self.filled, self.signed, self.scaled = sem("d_filled"), sem("d_signed"), sem("d_scaled")
        self.stored = sem("d_stored")

    def load_and_store(self, sp):
        K = self.K
        for dst, src in ((self.hadamard[:, :], self.d["hadamard"]), (self.signs[:, :], self.d["su_down"]),
                         (self.scale[:, :], self.d["down_scale"].partition_broadcast(P))):
            sp.dma_start(dst, src).then_inc(self.small_loaded, 16)
        for g in range(KF // K + 1):
            if g < KF // K:
                if g >= 2:
                    sp.wait_ge(self.filled, K * (g - 1))
                sp.dma_start(self.turned[:, g % 2, :, :], self.d["down_turned"][:, g * K:(g + 1) * K, :]
                             ).then_inc(self.loaded[g % 2], 16)
            if g:
                sp.wait_ge(self.scaled, K * g + 1)
                sp.dma_start(self.target[:, (g - 1) * K:g * K, :], self.mixed[:, :, :]).then_inc(self.stored, 16)
        sp.wait_ge(self.stored, 16 * KF // K)

    def group(self, g):
        return range(g * self.K, (g + 1) * self.K)

    def matmuls(self, pe, g):
        pe.wait_ge(self.small_loaded, 48)
        for k in self.group(g):
            if k % self.K == 0:
                pe.wait_ge(self.loaded[g % 2], 16 * (g // 2 + 1))
            if k >= 2:
                pe.wait_ge(self.signed, k - 1)
            pe.matmul(self.ps[k % 2][:, :], self.hadamard[:, :], self.turned[:, k // self.K % 2, k % self.K, :],
                      start=True, stop=True).then_inc(self.filled, 1)

    def sign(self, act, g):
        act.wait_ge(self.small_loaded, 48)
        for k in self.group(g):
            act.wait_ge(self.filled, k + 1)
            if k >= self.K and k % self.K == 0:
                act.wait_ge(self.stored, 16 * (k // self.K))
            act.activation(self.mixed[:, k % self.K, :], self.ps[k % 2][:, :], ACT.Copy,
                           scale=self.signs[:, k:k + 1]).then_inc(self.signed, 1)

    def scale_out(self, pool, g):
        if g == 0:
            pool.wait_ge(self.small_loaded, 48)
            pool.tensor_scalar(self.scale[:, :], self.scale[:, :], float(DFF) ** -0.5, None, ALU.mult
                               ).then_inc(self.scaled, 1)
            pool.wait_ge(self.scaled, 1)
        for k in self.group(g):
            pool.wait_ge(self.signed, k + 1)
            pool.tensor_tensor(self.mixed[:, k % self.K, :], self.mixed[:, k % self.K, :], self.scale[:, :],
                               ALU.mult).then_inc(self.scaled, 1)


def routed_ffn_step(nc, sem, d, x_res, ident, ffn_w1, ffn_w2, ffn_loaded, down_mixed):
    with ExitStack() as ctx:
        sb = lambda name, shape: ctx.enter_context(nc.sbuf_tensor(name, shape, F32))
        ps = lambda name, shape: ctx.enter_context(nc.psum_tensor(name, shape, F32))
        PT = 2 * NT
        KH = DFF // P
        stats, mean_var = sb("r_stats", [P, T, 6]), sb("r_mean_var", [P, T, 2])
        std, rstd = sb("r_std", [P, T]), sb("r_rstd", [P, T])
        wr_row, b2_row = sb("r_wr_row", [P, D]), sb("r_b2_row", [P, D])
        br, b1 = sb("r_br", [P, 1]), sb("r_b1", [P, KH])
        before, not_before = sb("r_before", [P, NT, N]), sb("r_not_before", [P, NT, N])
        slots = sb("r_slots", [P, 2, P])
        ones = sb("r_ones", [P, P])
        y = sb("r_y", [P, PT, D])
        scratch = sb("r_scratch", [P, 2, D])
        dots, logit = sb("r_dots", [P, PT]), sb("r_logit", [P, PT])
        logit_row = sb("r_logit_row", [P, 2, N])
        neg_max = sb("r_neg_max", [P, 2])
        above = sb("r_above", [P, 2, PT])
        rank, picked = sb("r_rank", [P, PT]), sb("r_picked", [P, PT])
        expo, weight = sb("r_expo", [P, PT]), sb("r_weight", [P, T])
        total, rtotal = sb("r_total", [P, 2]), sb("r_rtotal", [P, 2])
        onehot, onehot_t = sb("r_onehot", [P, PT, P]), sb("r_onehot_t", [P, T, P])
        fx_t = sb("r_fx_t", [P, KD, 4 * TOPK])
        hidden_t = sb("r_hidden_t", [P, KH, 4 * TOPK])
        picks_out = sb("r_picks_out", [P, 2, D])

        row_ps = [ps(f"r_row_ps{i}", [P, N]) for i in range(2)]
        total_ps = ps("r_total_ps", [P, N])
        fx_ps = ps("r_fx_ps", [P, N])
        turn_ps = [ps(f"r_turn_ps{i}", [P, N]) for i in range(2)]
        hidden_ps = [ps(f"r_hidden_ps{i}", [P, N]) for i in range(2)]

        loaded = sem("r_loaded")
        ln_sems = [sem("r_stats_done"), sem("r_var_done"), sem("r_std_done"), sem("r_rstd_done")]
        y_ready, dot_done, logit_ready = sem("r_y_ready"), sem("r_dot_done"), sem("r_logit_ready")
        row_filled, row_copied, max_ready = sem("r_row_filled"), sem("r_row_copied"), sem("r_max_ready")
        exp_done, count_done, rank_ready = sem("r_exp_done"), sem("r_count_done"), sem("r_rank_ready")
        chosen, total_filled, total_step = sem("r_chosen"), sem("r_total_filled"), sem("r_total_step")
        onehot_ready, gathered, fx_copied = sem("r_onehot_ready"), sem("r_gathered"), sem("r_fx_copied")
        turned, turn_copied, y_added = sem("r_turned"), sem("r_turn_copied"), sem("r_y_added")
        hidden_filled, hidden_ready = sem("r_hidden_filled"), sem("r_hidden_ready")
        out_filled, out_ready = sem("r_out_filled"), sem("r_out_ready")
        scattered, x_updated = sem("r_scattered"), sem("r_x_updated")
        LOADS = 8
        down_weights = DownWeights(sem, d, down_mixed, sb, hidden_ps)
        block = ctx.enter_context(nc.Block())

        @block.sync
        def _(sp):
            for dst, src in ((wr_row[:, :], d["Wr"].rearrange("d a -> (d a)").partition_broadcast(P)),
                             (b2_row[:, :], d["b2"].partition_broadcast(P)),
                             (br[:, :], d["br"].partition_broadcast(P)), (b1[:, :], d["b1"]),
                             (before[:, :, :], d["before"]), (not_before[:, :, :], d["not_before"]),
                             (slots[:, :, :], d["slots"]), (ones[:, :], d["ones"])):
                sp.dma_start(dst, src).then_inc(loaded, 16)
            down_weights.load_and_store(sp)

        @block.gpsimd
        def _(pool):
            for pair in range(2):
                for i in range(PT):
                    pool.wait_ge(y_ready, pair * PT + i + 1)
                    tile = pair * PT + i
                    pool.tensor_tensor(x_res[:, tile, :], x_res[:, tile, :], y[:, i, :], ALU.add
                                       ).then_inc(y_added, 1)
                for g in ((0, 1, 2), (3,))[pair]:
                    down_weights.scale_out(pool, g)

        @block.tensor
        def _(pe):
            down_weights.matmuls(pe, 0)
            pe.wait_ge(loaded, 16 * LOADS)
            for pair in range(2):
                pe.wait_ge(logit_ready, pair + 1)
                for g in range(2):
                    if pair:
                        pe.wait_ge(row_copied, 2 * (pair - 1) + g + 1)
                    for t in range(NT):
                        last = pe.transpose(row_ps[g][:, t * P:(t + 1) * P],
                                            logit[:, g * NT + t:g * NT + t + 1].to_broadcast([P, P]), ident[:, :])
                    last.then_inc(row_filled, 1)
                down_weights.matmuls(pe, 1 + 2 * pair)
                pe.wait_ge(chosen, pair + 1)
                pe.matmul(total_ps[:, 0:PT], ones[:, :], expo[:, :], start=True, stop=True).then_inc(total_filled, 1)
                pe.wait_ge(onehot_ready, PT * (pair + 1))
                if pair:
                    pe.wait_ge(fx_copied, pair)
                for c in range(KD):
                    for i in range(PT):
                        last = pe.matmul(fx_ps[:, c * P:(c + 1) * P], y[:, i, c * P:(c + 1) * P], onehot[:, i, :],
                                         start=(i == 0), stop=(i == PT - 1))
                last.then_inc(gathered, 1)
                for half in range(2):
                    if pair:
                        pe.wait_ge(turn_copied, 2 * (pair - 1) + half + 1)
                    for i in range(NT):
                        last = pe.transpose(turn_ps[half][:, i * P:(i + 1) * P], onehot[:, half * NT + i, :],
                                            ident[:, :])
                    last.then_inc(turned, 1)
                if pair == 0:
                    down_weights.matmuls(pe, 2)
            pe.wait_ge(fx_copied, 2)
            pe.wait_ge(ffn_loaded, 32)
            pe.wait_ge(down_weights.signed, KF)
            for f in range(KH):
                if f >= 2:
                    pe.wait_ge(hidden_ready, f - 1)
                for c in range(KD):
                    last = pe.matmul(hidden_ps[f % 2][:, 0:4 * TOPK], ffn_w1[:, c, f * P:(f + 1) * P], fx_t[:, c, :],
                                     start=(c == 0), stop=(c == KD - 1))
                last.then_inc(hidden_filled, 1)
            for r in range(2):
                for f in range(KH):
                    if r == 0:
                        pe.wait_ge(hidden_ready, f + 1)
                    last = pe.matmul(row_ps[r][:, :], hidden_t[:, f, r * P:(r + 1) * P], ffn_w2[:, f, :],
                                     start=(f == 0), stop=(f == KH - 1))
                last.then_inc(out_filled, 1)
            pe.wait_ge(turn_copied, 4)
            for tile in range(T):
                pe.wait_ge(out_ready, tile // PT + 1)
                if tile >= 2:
                    pe.wait_ge(x_updated, tile - 1)
                pe.matmul(turn_ps[tile % 2][:, :], onehot_t[:, tile, :], picks_out[:, tile // PT, :],
                          start=True, stop=True).then_inc(scattered, 1)

        @block.scalar
        def _(act):
            layernorm_stats(None, act, x_res, stats, mean_var, std, rstd, ln_sems)[1]()
            down_weights.sign(act, 0)
            for pair in range(2):
                act.wait_ge(max_ready, pair + 1)
                act.wait_ge(logit_ready, pair + 1)
                for g in range(2):
                    act.activation(expo[:, g * NT:(g + 1) * NT], logit[:, g * NT:(g + 1) * NT], ACT.Exp,
                                   bias=neg_max[:, g:g + 1]).then_inc(exp_done, 1)
                for g in ((1, 2), (3,))[pair]:
                    down_weights.sign(act, g)
            act.wait_ge(loaded, 16 * LOADS)
            for f in range(KH):
                act.wait_ge(hidden_filled, f + 1)
                act.activation(hidden_t[:, f, :], hidden_ps[f % 2][:, 0:4 * TOPK], ACT.Gelu, bias=b1[:, f:f + 1]
                               ).then_inc(hidden_ready, 1)

        @block.vector
        def _(dve):
            layernorm_stats(dve, None, x_res, stats, mean_var, std, rstd, ln_sems)[0]()
            dve.wait_ge(loaded, 16 * LOADS)
            for pair in range(2):
                if pair:
                    dve.wait_ge(gathered, pair)
                    dve.wait_ge(y_added, pair * PT)
                for i in range(PT):
                    tile = pair * PT + i
                    dve.tensor_scalar(y[:, i, :], x_res[:, tile, :], mean_var[:, tile, 0:1], rstd[:, tile:tile + 1],
                                      ALU.subtract, ALU.mult).then_inc(y_ready, 1)
                for i in range(PT):
                    n = pair * PT + i
                    dve.wait_ge(y_ready, n + 1)
                    if i == 0 and pair:
                        dve.wait_ge(count_done, 2 * PT * pair)
                    if i >= 2:
                        dve.wait_ge(dot_done, n - 1)
                    dve.tensor_tensor_reduce(scratch[:, i % 2, :], y[:, i, :], wr_row[:, :], 1.0, 0.0,
                                             ALU.mult, ALU.add, dots[:, i:i + 1]).then_inc(dot_done, 1)
                dve.wait_ge(dot_done, PT * (pair + 1))
                if pair:
                    dve.wait_ge(exp_done, 2 * pair)
                    dve.wait_ge(row_filled, 2 * pair)
                    dve.wait_ge(onehot_ready, PT * pair)
                dve.tensor_scalar(logit[:, :], dots[:, :], br[:, 0:1], None, ALU.add).then_inc(logit_ready, 1)
                for g in range(2):
                    dve.wait_ge(row_filled, 2 * pair + g + 1)
                    dve.tensor_copy(logit_row[:, g, :], row_ps[g][:, :]).then_inc(row_copied, 1)
                    dve.wait_ge(row_copied, 2 * pair + g + 1)
                dve.tensor_reduce(neg_max[:, :], logit_row[:, :, :], AX.X, ALU.max, negate=True
                                  ).then_inc(max_ready, 1)
                dve.wait_ge(logit_ready, pair + 1)
                for i in range(PT):
                    for side, (mask, op) in enumerate(((before, ALU.is_ge), (not_before, ALU.is_gt))):
                        n = (pair * PT + i) * 2 + side
                        if n % (2 * PT) >= 2:
                            dve.wait_ge(count_done, n - 1)
                        dve.scalar_tensor_tensor(scratch[:, side, :], logit_row[:, i // NT, :], logit[:, i:i + 1],
                                                 mask[:, i % NT, :], op, ALU.mult,
                                                 accum_out=above[:, side, i:i + 1]).then_inc(count_done, 1)
                dve.wait_ge(count_done, 2 * PT * (pair + 1))
                dve.tensor_tensor(rank[:, :], above[:, 0, :], above[:, 1, :], ALU.add).then_inc(rank_ready, 1)
                dve.wait_ge(rank_ready, pair + 1)
                if pair:
                    dve.wait_ge(turned, 2 * pair)
                for i in range(PT):
                    dve.tensor_scalar(onehot[:, i, :], slots[:, i // NT, :], rank[:, i:i + 1], None, ALU.is_equal
                                      ).then_inc(onehot_ready, 1)
                dve.tensor_scalar(picked[:, :], rank[:, :], float(TOPK), None, ALU.is_lt).then_inc(total_step, 1)
                dve.wait_ge(total_step, pair * 4 + 1)
                dve.wait_ge(exp_done, 2 * pair + 2)
                dve.tensor_tensor(expo[:, :], expo[:, :], picked[:, :], ALU.mult).then_inc(chosen, 1)
                dve.wait_ge(total_filled, pair + 1)
                dve.tensor_reduce(total[:, :], total_ps[:, 0:PT].rearrange("p (g t) -> p g t", g=2), AX.X, ALU.add
                                  ).then_inc(total_step, 1)
                dve.wait_ge(total_step, pair * 4 + 2)
                dve.reciprocal(rtotal[:, :], total[:, :]).then_inc(total_step, 1)
                dve.wait_ge(total_step, pair * 4 + 3)
                for g in range(2):
                    at = (2 * pair + g) * NT
                    w = dve.tensor_scalar(weight[:, at:at + NT], expo[:, g * NT:(g + 1) * NT], rtotal[:, g:g + 1],
                                          None, ALU.mult)
                w.then_inc(total_step, 1)
                dve.wait_ge(gathered, pair + 1)
                dve.tensor_copy(fx_t[:, :, pair * P:(pair + 1) * P],
                                fx_ps[:, :].rearrange("p (c r) -> p c r", c=KD)).then_inc(fx_copied, 1)
                for half in range(2):
                    dve.wait_ge(turned, 2 * pair + half + 1)
                    at = pair * PT + half * NT
                    dve.tensor_copy(onehot_t[:, at:at + NT, :], turn_ps[half][:, :].rearrange(
                        "p (t n) -> p t n", t=NT)).then_inc(turn_copied, 1)
            for r in range(2):
                dve.wait_ge(out_filled, r + 1)
                dve.tensor_tensor(picks_out[:, r, :], row_ps[r][:, :], b2_row[:, :], ALU.add).then_inc(out_ready, 1)
            dve.wait_ge(total_step, 8)
            dve.wait_ge(y_added, T)
            for tile in range(T):
                dve.wait_ge(scattered, tile + 1)
                dve.scalar_tensor_tensor(x_res[:, tile, :], turn_ps[tile % 2][:, :], weight[:, tile:tile + 1],
                                         x_res[:, tile, :], ALU.mult, ALU.add).then_inc(x_updated, 1)


def cross_attention_step(nc, sem, d, x_res, ident):
    with ExitStack() as outer:
        keep = lambda name, shape: outer.enter_context(nc.sbuf_tensor(name, shape, F32))
        XP = XH // 2
        q_w = keep("x_q_w", [P, KD, XH * XR])
        o_w = keep("x_o_w", [P, XH, D])
        kr_w = keep("x_kr_w", [P, XH * XR])
        kv = keep("x_kv", [P, T, F_IN])
        kv_t = keep("x_kv_t", [P, B, N])

        with ExitStack() as ctx:
            sb = lambda name, shape: ctx.enter_context(nc.sbuf_tensor(name, shape, F32))
            ps = lambda name, shape: ctx.enter_context(nc.psum_tensor(name, shape, F32))
            KC = DCQ // P
            wq, kcq_t = sb("x_wq", [P, XH, D]), sb("x_kcq_t", [P, KC, XH, P])
            wqr, latent = sb("x_wqr", [P, KC, XH, XR]), sb("x_latent", [P, XH, XR])
            wo_t, kckv = sb("x_wo_t", [P, 4, D]), sb("x_kckv", [P, XH, P])
            swapped, cos, sin = sb("x_swapped", [P, T, F_IN]), sb("x_cos", [P, NT, F_IN]), sb("x_sin", [P, NT, F_IN])
            cos_t, sin_t = sb("x_cos_t", [P, N]), sb("x_sin_t", [P, N])
            swapped_t = swapped[:, :, :].rearrange("p (b t) f -> p b (t f)", b=B)
            mm_ps = [ps(f"x_mm_ps{i}", [P, N]) for i in range(4)]
            ctx_loaded, rope_step = sem("x_ctx_loaded"), sem("x_rope_step")
            a_loaded, q_loaded, tables_loaded = sem("x_a_loaded"), sem("x_q_loaded"), sem("x_tables_loaded")
            o_loaded = [sem(f"x_o_loaded{i}") for i in range(2)]
            filled, copied = sem("x_filled"), sem("x_copied")
            block = ctx.enter_context(nc.Block())
            AP_, QP, OP = 2, KD * 2, XH
            wo_v = d["wo"]

            @block.sync
            def _(sp):
                sp.dma_start(kcq_t[:, :, :, :], d["kcq"]).then_inc(a_loaded, 16)
                sp.dma_start(wqr[:, :, :, :], d["wqr"]).then_inc(a_loaded, 16)
                sp.dma_start(wq[:, :, :], d["wq"]).then_inc(q_loaded, 16)
                for n in range(XH // 2):
                    if n >= 2:
                        sp.wait_ge(filled, AP_ + QP + 2 * n - 2)
                    at = 2 * (n % 2)
                    sp.dma_start(wo_t[:, at:at + 2, :], wo_v[:, 2 * n:2 * n + 2, :]).then_inc(o_loaded[n % 2], 16)

            @block.gpsimd
            def _(pool):
                steps = 0

                def step(ins):
                    nonlocal steps
                    steps += 1
                    ins.then_inc(rope_step, 1)
                    pool.wait_ge(rope_step, steps)

                pool.wait_ge(ctx_loaded, 16 * 8)
                for b in range(B):
                    at = slice(b * NT, (b + 1) * NT)
                    step(pool.tensor_tensor(kv[:, at, :], kv[:, at, :], cos[:, :, :], ALU.mult))
                    step(pool.tensor_tensor(swapped[:, at, :], swapped[:, at, :], sin[:, :, :], ALU.mult))
                    step(pool.tensor_tensor(kv[:, at, :], kv[:, at, :], swapped[:, at, :], ALU.add))
                pool.wait_ge(ctx_loaded, 16 * 10)
                pool.wait_ge(tables_loaded, 32)
                for b in range(B):
                    step(pool.tensor_tensor(kv_t[:, b, :], kv_t[:, b, :], cos_t[:, :], ALU.mult))
                    step(pool.tensor_tensor(swapped_t[:, b, :], swapped_t[:, b, :], sin_t[:, :], ALU.mult))
                    step(pool.tensor_tensor(kv_t[:, b, :], kv_t[:, b, :], swapped_t[:, b, :], ALU.add))

            @block.tensor
            def _(pe):
                use = 0

                def begin():
                    if use >= 4:
                        pe.wait_ge(copied, use - 3)
                    return mm_ps[use % 4]

                pe.wait_ge(a_loaded, 32)
                for half in range(AP_):
                    out = begin()
                    for i in range(8):
                        h = half * 8 + i
                        for c in range(KC):
                            last = pe.matmul(out[:, i * XR:(i + 1) * XR], kcq_t[:, c, h, :], wqr[:, c, h, :],
                                             start=(c == 0), stop=(c == KC - 1))
                    last.then_inc(filled, 1)
                    use += 1
                pe.wait_ge(q_loaded, 16)
                pe.wait_ge(copied, AP_)
                for c in range(KD):
                    for half in range(2):
                        out = begin()
                        for i in range(8):
                            h = half * 8 + i
                            last = pe.matmul(out[:, i * XR:(i + 1) * XR], wq[:, h, c * P:(c + 1) * P],
                                             latent[:, h, :], start=True, stop=True)
                        last.then_inc(filled, 1)
                        use += 1
                pe.wait_ge(ctx_loaded, 16 * 8)
                for h in range(XH):
                    out = begin()
                    pe.wait_ge(o_loaded[h // 2 % 2], 16 * (h // 4 + 1))
                    pe.matmul(out[:, :], kckv[:, h, :], wo_t[:, h % 4, :], start=True, stop=True).then_inc(filled, 1)
                    use += 1

            @block.scalar
            def _(act):
                ctx_v = d["ctx"].rearrange("b (t p) f -> p (b t) f", p=P)
                H = F_IN // 2
                ctx_t_v = d["ctx_t"].rearrange("b f n -> f b n")
                for dst, src in ((kv[:, :, :], ctx_v), (swapped[:, :, 0:H], ctx_v[:, :, H:F_IN]),
                                 (swapped[:, :, H:F_IN], ctx_v[:, :, 0:H]), (cos[:, :, :], d["cos"]),
                                 (sin[:, :, :], d["sin"]), (kr_w[:, :].rearrange("p (h r) -> p h r", h=XH),
                                                            d["wkr"]),
                                 (kv_t[:, :, :], ctx_t_v),
                                 (kckv[:, :, :], d["kckv"])):
                    act.dma_start(dst, src).then_inc(ctx_loaded, 16)
                act.dma_start(cos_t[:, :], d["cos_t"]).then_inc(tables_loaded, 16)
                act.dma_start(sin_t[:, :], d["sin_t"]).then_inc(tables_loaded, 16)
                act.wait_ge(rope_step, 3 * B)
                act.dma_start(swapped_t[0:H, :, :], ctx_t_v[H:F_IN]).then_inc(ctx_loaded, 16)
                act.dma_start(swapped_t[H:F_IN, :, :], ctx_t_v[0:H]).then_inc(ctx_loaded, 16)

            @block.vector
            def _(dve):
                use = 0
                for half in range(AP_):
                    dve.wait_ge(filled, use + 1)
                    dve.tensor_copy(latent[:, half * 8:(half + 1) * 8, :], mm_ps[use % 4][:, :].rearrange(
                        "p (h r) -> p h r", h=8)).then_inc(copied, 1)
                    use += 1
                for c in range(KD):
                    for half in range(2):
                        dve.wait_ge(filled, use + 1)
                        dve.tensor_copy(q_w[:, c, half * N:(half + 1) * N], mm_ps[use % 4][:, :]).then_inc(copied, 1)
                        use += 1
                for h in range(XH):
                    dve.wait_ge(filled, use + 1)
                    dve.tensor_copy(o_w[:, h, :], mm_ps[use % 4][:, :]).then_inc(copied, 1)
                    use += 1

        with ExitStack() as ctx:
            F32R = mybir.dt.float32r
            sb = lambda name, shape, dt=F32: ctx.enter_context(nc.sbuf_tensor(name, shape, dt))
            ps = lambda name, shape: ctx.enter_context(nc.psum_tensor(name, shape, F32))
            stats, mean_var = sb("x_stats", [P, T, 6]), sb("x_mean_var", [P, T, 2])
            std, rstd = sb("x_std", [P, T]), sb("x_rstd", [P, T])
            NE = 4
            expo = sb("x_expo", [P, NE, N])
            y_t = sb("x_y_t", [P, KD, N])
            kv_now = sb("x_kv_now", [P, NT, F_IN])
            kv_split = [sb("x_kv_high", [P, NT, F_IN], F32R), sb("x_kv_low", [P, NT, F_IN], F32R)]
            kq_split = [sb("x_kq_high", [P, 2, 2, N], F32R), sb("x_kq_low", [P, 2, 2, N], F32R)]
            neg_max, sums, rsums = sb("x_neg_max", [P, 8]), sb("x_sums", [P, 8]), sb("x_rsums", [P, 8])
            probs_split = [sb("x_probs_high", [P, 2, NT, N], F32R), sb("x_probs_low", [P, 2, NT, N], F32R)]
            latent_t = sb("x_latent_t", [P, XH, N])
            score_ps = [ps(f"x_score_ps{i}", [P, N]) for i in range(2)]
            turn_ps = [ps(f"x_turn_ps{i}", [P, N]) for i in range(2)]
            latent_ps = [ps(f"x_latent_ps{i}", [P, N]) for i in range(2)]
            project_ps = [ps(f"x_project_ps{i}", [P, N]) for i in range(2)]
            HIGH, LOW = 0, 1
            PRODUCTS = ((HIGH, LOW), (LOW, HIGH), (HIGH, HIGH))

            ln_sems = [sem("x_stats_done"), sem("x_var_done"), sem("x_std_done"), sem("x_rstd_done")]
            y_ready, kv_ready, kv_high, kv_low = sem("x_y_ready"), sem("x_kv_ready"), sem("x_kv_high"), sem("x_kv_low")
            turned, turn_high, turn_free = sem("x_turned"), sem("x_turn_high"), sem("x_turn_free")
            projected, project_free = sem("x_projected"), sem("x_project_free")
            kq_high = sem("x_kq_high")
            scored, max_ready, exp_done = sem("x_scored"), sem("x_max_ready"), sem("x_exp_done")
            rsum_ready, probs_ready = sem("x_rsum_ready"), sem("x_probs_ready")
            latent_filled, latent_free = sem("x_latent_filled"), sem("x_latent_free")

            TILES = XH * NT
            PT = 2 * NT
            USES = NT + TILES
            PUSES = 2 * XP + NT
            LAG = 3
            OUT_AT = TILES + 2 * NT

            block = ctx.enter_context(nc.Block())

            @block.tensor
            def _(pe):
                def turn_y(b, t):
                    pe.wait_ge(turn_free, b * USES + t + 1)
                    pe.wait_ge(y_ready, b * NT + t + 1)
                    for c in range(KD):
                        last = pe.transpose(turn_ps[t % 2][:, c * P:(c + 1) * P], expo[:, t, c * P:(c + 1) * P],
                                            ident[:, :])
                    last.then_inc(turned, 1)

                def keys(b, pair, count):
                    pe.wait_ge(project_free, count + 1)
                    pe.matmul(project_ps[0][:, :], kr_w[:, pair * P:(pair + 1) * P],
                              kv_t[:, bass.ds(b, 1), :].rearrange("p a n -> p (a n)"), start=True, stop=True
                              ).then_inc(projected, 1)

                def queries(pair, c, count):
                    if c == 0:
                        pe.wait_ge(project_free, count + 1)
                    q = pe.matmul(project_ps[1][:, :], q_w[:, c, pair * P:(pair + 1) * P], y_t[:, c, :],
                                  start=(c == 0), stop=(c == KD - 1))
                    if c == KD - 1:
                        q.then_inc(projected, 1)

                def first_pair(b, count):
                    keys(b, 0, count)
                    pe.wait_ge(turn_free, b * USES + NT + 2)
                    for c in range(KD):
                        queries(0, c, count + 1)

                def graph(b, final):
                    for i in range(OUT_AT):
                        if i < TILES:
                            h, t = i // NT, i % NT
                            half = slice((h % 2) * XR, (h % 2 + 1) * XR)
                            if i % PT == 0 and i:
                                pe.wait_ge(project_free, b * PUSES + 2 * (i // PT) + 2 + 2)
                            pe.wait_ge(exp_done, b * TILES + i + 1)
                            for n, (q, k) in enumerate(PRODUCTS):
                                last = pe.matmul(score_ps[i % 2][:, :],
                                                 kq_split[q][half, h // 2 % 2, 1, t * P:(t + 1) * P],
                                                 kq_split[k][half, h // 2 % 2, 0, :], start=(n == 0), stop=(n == 2))
                            last.then_inc(scored, 1)
                            pair, step = i // PT + 1, i % PT
                            if pair < XP:
                                if step == 1:
                                    keys(b, pair, b * PUSES + 2 * pair)
                                if 2 <= step < 2 + KD:
                                    queries(pair, step - 2, b * PUSES + 2 * pair + 1)
                        if 0 <= i - LAG < TILES:
                            n = i - LAG
                            pe.wait_ge(turn_free, b * USES + NT + n + 1)
                            pe.wait_ge(probs_ready, b * TILES + n + 1)
                            for c in range(NT):
                                last = pe.transpose(turn_ps[n % 2][:, c * P:(c + 1) * P],
                                                    expo[:, n % NE, c * P:(c + 1) * P], ident[:, :])
                            last.then_inc(turned, 1)
                        if i >= 2 * NT:
                            h, k = (i - 2 * NT) // NT, i % NT
                            if k == 0:
                                pe.wait_ge(turn_free, b * USES + NT + h * NT + NT + 2)
                                pe.wait_ge(latent_free, b * XH + h + 1)
                                pe.wait_ge(kv_low, b + 1)
                            for n, (w, p) in enumerate(PRODUCTS):
                                last = pe.matmul(latent_ps[h % 2][:, :], kv_split[w][:, k, :],
                                                 probs_split[p][:, h % 2, k, :], start=(k == 0 and n == 0),
                                                 stop=(k == NT - 1 and n == 2))
                            if k == NT - 1:
                                last.then_inc(latent_filled, 1)
                        if not final and 0 <= i - TILES - LAG < NT:
                            turn_y(b + 1, i - TILES - LAG)
                    count = b * PUSES + 2 * XP
                    if not final:
                        first_pair(b + 1, count)
                        count = count + 2
                    pe.wait_ge(latent_free, b * XH + XH + 2)
                    for t in range(NT):
                        pe.wait_ge(project_free, count + t + 1)
                        for h in range(XH):
                            last = pe.matmul(project_ps[t % 2][:, :], latent_t[:, h, t * P:(t + 1) * P], o_w[:, h, :],
                                             start=(h == 0), stop=(h == XH - 1))
                        last.then_inc(projected, 1)

                pe.sem_inc(latent_filled, 2)
                for t in range(NT):
                    turn_y(0, t)
                first_pair(0, 0)
                pe.wait_ge(project_free, 2 + 2)
                with pe.Fori(0, B - 1) as b:
                    graph(b, final=False)
                graph(B - 1, final=True)

            @block.scalar
            def _(act):
                def kq_highs(count, parity, which):
                    act.wait_ge(projected, count + 1)
                    act.activation(kq_split[HIGH][:, parity, which, :], project_ps[which][:, :], ACT.Copy
                                   ).then_inc(kq_high, 1)

                def graph(b, final):
                    act.wait_ge(turned, b * USES + NT)
                    act.wait_ge(kv_ready, b + 1)
                    act.wait_ge(latent_filled, b * XH + 2)
                    act.activation(kv_split[HIGH][:, :, :], kv_now[:, :, :], ACT.Copy).then_inc(kv_high, 1)
                    for i in range(OUT_AT + 1):
                        if i < TILES:
                            act.wait_ge(max_ready, b * TILES + i + 1)
                            act.activation(expo[:, i % NE, :], score_ps[i % 2][:, :], ACT.Exp,
                                           bias=neg_max[:, i % 8:i % 8 + 1], accum_out=sums[:, i % 8:i % 8 + 1]
                                           ).then_inc(exp_done, 1)
                        pair, step = i // PT + 1, i % PT
                        if pair < XP and step in (2, 6):
                            kq_highs(b * PUSES + 2 * pair + (step == 6), pair % 2, int(step == 6))
                        n = i - LAG
                        if 0 <= n < TILES:
                            h, t = n // NT, n % NT
                            act.wait_ge(turned, b * USES + NT + n + 1)
                            if t == 0:
                                act.wait_ge(latent_filled, b * XH + h + 1)
                            act.activation(probs_split[HIGH][:, h % 2, :, t * P:(t + 1) * P],
                                           turn_ps[n % 2][:, :].rearrange("p (k n) -> p k n", k=NT), ACT.Copy
                                           ).then_inc(turn_high, 1)
                        if i >= 3 * NT and i % NT == 0:
                            h = i // NT - 3
                            act.wait_ge(latent_filled, b * XH + h + 1 + 2)
                            act.activation(latent_t[:, h, :], latent_ps[h % 2][:, :], ACT.Copy).then_inc(latent_free, 1)
                    if not final:
                        for which in range(2):
                            kq_highs(b * PUSES + 2 * XP + which, 0, which)

                act.sem_inc(exp_done, 2)
                act.sem_inc(latent_free, 2)
                layernorm_stats(None, act, x_res, stats, mean_var, std, rstd, ln_sems)[1]()
                for which in range(2):
                    kq_highs(which, 0, which)
                with act.Fori(0, B - 1) as b:
                    graph(b, final=False)
                graph(B - 1, final=True)

            @block.vector
            def _(dve):
                def normed(b, t):
                    dve.tensor_scalar(expo[:, t, :], x_res[:, bass.ds(b * NT + t, 1), :].rearrange("p a c -> p (a c)"),
                                      mean_var[:, bass.ds(b * NT + t, 1), 0], rstd[:, bass.ds(b * NT + t, 1)],
                                      ALU.subtract, ALU.mult).then_inc(y_ready, 1)

                def y_copy(b, t):
                    dve.wait_ge(turned, b * USES + t + 1)
                    dve.tensor_copy(y_t[:, :, t * P:(t + 1) * P], turn_ps[t % 2][:, :].rearrange(
                        "p (c n) -> p c n", c=KD)).then_inc(turn_free, 1)

                def kq_lows(count, parity, which):
                    dve.wait_ge(kq_high, count + 1)
                    dve.tensor_tensor(kq_split[LOW][:, parity, which, :], project_ps[which][:, :],
                                      kq_split[HIGH][:, parity, which, :].bitcast(F32), ALU.subtract
                                      ).then_inc(project_free, 1)

                def graph(b, final):
                    dve.tensor_copy(kv_now[:, :, :], kv[:, bass.ds(b * NT, NT), :]).then_inc(kv_ready, 1)
                    for i in range(OUT_AT + 1):
                        if i < TILES:
                            dve.wait_ge(scored, b * TILES + i + 1)
                            dve.tensor_reduce(neg_max[:, i % 8:i % 8 + 1], score_ps[i % 2][:, :], AX.X, ALU.max,
                                              negate=True).then_inc(max_ready, 1)
                        if 1 <= i <= TILES:
                            n = i - 1
                            dve.wait_ge(exp_done, b * TILES + n + 1 + 2)
                            dve.reciprocal(rsums[:, n % 8:n % 8 + 1], sums[:, n % 8:n % 8 + 1]).then_inc(rsum_ready, 1)
                            dve.wait_ge(rsum_ready, b * TILES + n + 1)
                            dve.tensor_scalar(expo[:, n % NE, :], expo[:, n % NE, :], rsums[:, n % 8:n % 8 + 1], None,
                                              ALU.mult).then_inc(probs_ready, 1)
                        if i == 1:
                            dve.wait_ge(kv_high, b + 1)
                            dve.tensor_tensor(kv_split[LOW][:, :, :], kv_now[:, :, :],
                                              kv_split[HIGH][:, :, :].bitcast(F32), ALU.subtract).then_inc(kv_low, 1)
                        pair, step = i // PT + 1, i % PT
                        if pair < XP and step in (3, 6):
                            which = int(step == 6)
                            kq_lows(b * 2 * XP + 2 * pair + which, pair % 2, which)
                        n = i - LAG - 1
                        if 0 <= n < TILES:
                            h, t = n // NT, n % NT
                            at = slice(t * P, (t + 1) * P)
                            dve.wait_ge(turn_high, b * TILES + n + 1)
                            dve.tensor_tensor(probs_split[LOW][:, h % 2, :, at],
                                              turn_ps[n % 2][:, :].rearrange("p (k n) -> p k n", k=NT),
                                              probs_split[HIGH][:, h % 2, :, at].bitcast(F32), ALU.subtract
                                              ).then_inc(turn_free, 1)
                        if not final and 0 <= i - TILES < NT:
                            t = i - TILES
                            dve.wait_ge(turned, b * USES + USES - NT + t + 1)
                            normed(b + 1, t)
                        if not final and 0 <= i - TILES - LAG - 1 < NT:
                            y_copy(b + 1, i - TILES - LAG - 1)
                    count = b * PUSES + 2 * XP
                    if not final:
                        for which in range(2):
                            kq_lows(b * 2 * XP + 2 * XP + which, 0, which)
                        count = count + 2
                    for t in range(NT):
                        dve.wait_ge(projected, count + t + 1)
                        x_tile = x_res[:, bass.ds(b * NT + t, 1), :].rearrange("p a c -> p (a c)")
                        dve.tensor_tensor(x_tile, x_tile, project_ps[t % 2][:, :], ALU.add).then_inc(project_free, 1)

                dve.sem_inc(turn_free, 2)
                dve.sem_inc(project_free, 2)
                layernorm_stats(dve, None, x_res, stats, mean_var, std, rstd, ln_sems)[0]()
                for t in range(NT):
                    normed(0, t)
                for t in range(NT):
                    y_copy(0, t)
                for which in range(2):
                    kq_lows(which, 0, which)
                with dve.Fori(0, B - 1) as b:
                    graph(b, final=False)
                graph(B - 1, final=True)


def gated_ffn_step(nc, sem, d, x_res, ident, out):
    F32R = mybir.dt.float32r
    with ExitStack() as ctx:
        sb = lambda name, shape, dt=F32: ctx.enter_context(nc.sbuf_tensor(name, shape, dt))
        ps = lambda name, shape: ctx.enter_context(nc.psum_tensor(name, shape, F32))
        stats, mean_var = sb("f_stats", [P, T, 6]), sb("f_mean_var", [P, T, 2])
        std, rstd = sb("f_std", [P, T]), sb("f_rstd", [P, T])
        hadamard, su_up = sb("f_hadamard", [P, P]), sb("f_su_up", [P, KD])
        scales = sb("f_scales", [P, 2, KF])
        scale_now = sb("f_scale_now", [P, 2, 2])
        y, y_t, half_t = sb("f_y", [P, NT, D]), sb("f_y_t", [P, KD, N]), sb("f_half_t", [P, KD, N])
        mixed = [sb("f_mixed_high", [P, B, KD, N], F32R), sb("f_mixed_low", [P, B, KD, N], F32R)]
        WCOLS = 2 * KD * P + D
        raw = sb("f_raw", [P, 2, WCOLS])
        split = [sb("f_w_high", [P, 2, WCOLS], F32R), sb("f_w_low", [P, 2, WCOLS], F32R)]
        silu, z = sb("f_silu", [P, 2, N]), sb("f_z", [P, 2, N])
        z_split = [sb("f_z_high", [P, 2, N], F32R), sb("f_z_low", [P, 2, N], F32R)]
        turn_ps = [ps(f"f_turn_ps{i}", [P, N]) for i in range(2)]
        gate_ps = [ps(f"f_gate_ps{i}", [P, N]) for i in range(2)]
        up_ps = [ps(f"f_up_ps{i}", [P, N]) for i in range(2)]
        down_ps = [ps(f"f_down_ps{i}", [P, N]) for i in range(2)]
        HIGH, LOW = 0, 1
        PRODUCTS = ((HIGH, LOW), (LOW, HIGH), (HIGH, HIGH))

        small_loaded, scales_ready = sem("f_small_loaded"), sem("f_scales_ready")
        raw_loaded = [sem("f_raw_loaded0"), sem("f_raw_loaded1")]
        w_high, w_ready = sem("f_w_high"), sem("f_w_ready")
        ln_sems = [sem("f_stats_done"), sem("f_var_done"), sem("f_std_done"), sem("f_rstd_done")]
        y_ready, turned, y_copied = sem("f_y_ready"), sem("f_turned"), sem("f_y_copied")
        mix_step, mixed_filled = sem("f_mix_step"), sem("f_mixed_filled")
        mixed_high, mixed_ready = sem("f_mixed_high"), sem("f_mixed_ready")
        gate_filled, up_filled, silu_ready = sem("f_gate_filled"), sem("f_up_filled"), sem("f_silu_ready")
        z_ready, z_high, z_low = sem("f_z_ready"), sem("f_z_high"), sem("f_z_low")
        down_filled, down_free, stored = sem("f_down_filled"), sem("f_down_free"), sem("f_stored")
        block = ctx.enter_context(nc.Block())

        LOOPS = (KF - 2) // 2

        @block.sync
        def _(sp):
            for dst, src in ((hadamard[:, :], d["hadamard"]), (su_up[:, :], d["su_up"]),
                             (scales[:, 0, :], d["gate_scale"]), (scales[:, 1, :], d["up_scale"])):
                sp.dma_start(dst, src).then_inc(small_loaded, 16)

            def load(g, i):
                static = isinstance(g, int)
                if not static or g >= 2:
                    sp.wait_ge(w_ready, g - 1)
                ug = d["up_gate"][:, g, :] if static else d["up_gate"][:, bass.ds(g, 1), :].rearrange(
                    "p a n -> p (a n)")
                dn = d["down"][:, g, :] if static else d["down"][:, bass.ds(g, 1), :].rearrange("p a n -> p (a n)")
                sp.dma_start(raw[:, i, 0:2 * KD * P], ug).then_inc(raw_loaded[i], 16)
                sp.dma_start(raw[:, i, 2 * KD * P:WCOLS], dn).then_inc(raw_loaded[i], 16)

            load(0, 0)
            load(1, 1)
            with sp.Fori(0, LOOPS) as i:
                load(2 * i + 2, 0)
                load(2 * i + 3, 1)
            out_v = out.rearrange("b (t p) c -> b p t c", p=P)
            for b in range(B):
                sp.wait_ge(down_free, ((KF - 1) * B + b + 1) * NT + 2)
                sp.dma_start(out_v[b], x_res[:, b * NT:(b + 1) * NT, :]).then_inc(stored, 16)
            sp.wait_ge(stored, 16 * B)

        @block.gpsimd
        def _(pool):
            def weights_low(g, i):
                pool.wait_ge(w_high, 3 * g + 3)
                third = WCOLS // 3
                for n in range(3):
                    cols = slice(n * third, (n + 1) * third)
                    last = pool.tensor_tensor(split[LOW][:, i, cols], raw[:, i, cols],
                                              split[HIGH][:, i, cols].bitcast(F32), ALU.subtract)
                last.then_inc(w_ready, 1)

            def chunk(g, i, more=True):
                for b in range(B):
                    s = g * B + b
                    pool.wait_ge(z_high, s + 1)
                    pool.tensor_tensor(z_split[LOW][:, b % 2, :], z[:, b % 2, :],
                                       z_split[HIGH][:, b % 2, :].bitcast(F32), ALU.subtract).then_inc(z_low, 1)
                    if b == 2 and more:
                        weights_low(g + 1, 1 - i)

            pool.sem_inc(z_low, 2)
            weights_low(0, 0)
            chunk(0, 0)
            with pool.Fori(0, LOOPS) as i:
                chunk(2 * i + 1, 1)
                chunk(2 * i + 2, 0)
            chunk(KF - 1, 1, more=False)

        @block.tensor
        def _(pe):
            def turns(b):
                pe.wait_ge(y_ready, b * NT + NT)
                for c in range(KD):
                    if c >= 2:
                        pe.wait_ge(y_copied, b * KD + c - 1)
                    elif b:
                        pe.wait_ge(mixed_ready, (b - 1) * KD + c + 3)
                    for t in range(NT):
                        last = pe.transpose(turn_ps[c % 2][:, t * P:(t + 1) * P], y[:, t, c * P:(c + 1) * P],
                                            ident[:, :])
                    last.then_inc(turned, 1)

            def mix(b):
                pe.wait_ge(mix_step, b * 4 + 4)
                for c in range(KD):
                    if c < 2:
                        pe.wait_ge(y_copied, b * KD + c + 3)
                    else:
                        pe.wait_ge(mixed_ready, b * KD + c - 1)
                    pe.matmul(turn_ps[c % 2][:, :], hadamard[:, :], y_t[:, c, :], start=True, stop=True
                              ).then_inc(mixed_filled, 1)

            def up_gate(g, i, b, first=False):
                s = g * B + b
                if first:
                    pe.wait_ge(mixed_ready, (b + 1) * KD)
                if b == 0:
                    pe.wait_ge(w_ready, g + 1)
                for which, (target, filled, free) in enumerate(((gate_ps, gate_filled, silu_ready),
                                                                (up_ps, up_filled, z_ready))):
                    pe.wait_ge(free, s + 1)
                    n = 0
                    for c in range(KD):
                        at = (which * KD + c) * P
                        for w, m in PRODUCTS:
                            last = pe.matmul(target[b % 2][:, :], split[w][:, i, at:at + P], mixed[m][:, b, c, :],
                                             start=(n == 0), stop=(n == 3 * KD - 1))
                            n += 1
                    last.then_inc(filled, 1)

            def down(g, i, b):
                s = g * B + b
                pe.wait_ge(z_low, s + 1 + 2)
                for t in range(NT):
                    pe.wait_ge(down_free, s * NT + t + 1)
                    for n, (w, m) in enumerate(PRODUCTS):
                        last = pe.matmul(down_ps[t % 2][:, :], z_split[w][:, b % 2, t * P:(t + 1) * P],
                                         split[m][:, i, 2 * KD * P:WCOLS], start=(n == 0), stop=(n == 2))
                    last.then_inc(down_filled, 1)

            pe.sem_inc(down_filled, 2 * NT)
            pe.wait_ge(small_loaded, 64)
            turns(0)
            mix(0)
            turns(1)
            for b in range(B):
                up_gate(0, 0, b, first=True)
                if b + 1 < B:
                    mix(b + 1)
                if b + 2 < B:
                    turns(b + 2)
                if b:
                    down(0, 0, b - 1)

            def chunk(g, i):
                up_gate(g, i, 0)
                down(g - 1, 1 - i, B - 1)
                for b in range(1, B):
                    up_gate(g, i, b)
                    down(g, i, b - 1)

            with pe.Fori(0, LOOPS) as i:
                chunk(2 * i + 1, 1)
                chunk(2 * i + 2, 0)
            chunk(KF - 1, 1)
            down(KF - 1, 1, B - 1)

        @block.scalar
        def _(act):
            def weights_high(g, i, loads):
                act.wait_ge(raw_loaded[i], 32 * loads)
                if not isinstance(g, int) or g >= 2:
                    act.wait_ge(down_filled, (g - 1) * B * NT + 2 * NT)
                third = WCOLS // 3
                for n in range(3):
                    cols = slice(n * third, (n + 1) * third)
                    act.activation(split[HIGH][:, i, cols], raw[:, i, cols], ACT.Copy).then_inc(w_high, 1)

            def turned_copies(b):
                for c in range(KD):
                    act.wait_ge(turned, b * KD + c + 1)
                    act.activation(y_t[:, c, :], turn_ps[c % 2][:, :], ACT.Copy, scale=su_up[:, c:c + 1]
                                   ).then_inc(y_copied, 1)

            def mixed_highs(b):
                for c in range(KD):
                    act.wait_ge(mixed_filled, b * KD + c + 1)
                    act.activation(mixed[HIGH][:, b, c, :], turn_ps[c % 2][:, :], ACT.Copy).then_inc(mixed_high, 1)

            def hidden(g, i, b):
                s = g * B + b
                if b == 0:
                    act.wait_ge(scales_ready, g + 2)
                act.wait_ge(gate_filled, s + 1)
                act.wait_ge(z_ready, s + 1)
                act.activation(silu[:, b % 2, :], gate_ps[b % 2][:, :], ACT.Silu, scale=scale_now[:, i, 0:1]
                               ).then_inc(silu_ready, 1)
                act.wait_ge(z_ready, s + 1 + 2)
                act.wait_ge(down_filled, s * NT + NT)
                act.activation(z_split[HIGH][:, b % 2, :], z[:, b % 2, :], ACT.Copy).then_inc(z_high, 1)

            act.sem_inc(silu_ready, 2)
            weights_high(0, 0, 1)
            layernorm_stats(None, act, x_res, stats, mean_var, std, rstd, ln_sems)[1]()
            act.wait_ge(small_loaded, 64)
            turned_copies(0)
            mixed_highs(0)
            turned_copies(1)
            for b in range(B):
                if b + 1 < B:
                    mixed_highs(b + 1)
                if b + 2 < B:
                    turned_copies(b + 2)
                hidden(0, 0, b)
                if b == 1:
                    weights_high(1, 1, 1)

            def chunk(g, i, loads, more=True):
                for b in range(B):
                    hidden(g, i, b)
                    if b == 1 and more:
                        weights_high(g + 1, 1 - i, loads)

            with act.Fori(0, LOOPS) as i:
                chunk(2 * i + 1, 1, i + 2)
                chunk(2 * i + 2, 0, i + 2)
            chunk(KF - 1, 1, 0, more=False)

        @block.vector
        def _(dve):
            dve.sem_inc(z_ready, 2)
            dve.sem_inc(down_free, 2)
            layernorm_stats(dve, None, x_res, stats, mean_var, std, rstd, ln_sems)[0]()
            dve.wait_ge(small_loaded, 64)
            dve.tensor_scalar(scales[:, :, :], scales[:, :, :], float(D) ** -0.5, None, ALU.mult
                              ).then_inc(scales_ready, 1)

            def normed(b):
                if b:
                    dve.wait_ge(turned, b * KD)
                for t in range(NT):
                    tile = b * NT + t
                    dve.tensor_scalar(y[:, t, :], x_res[:, tile, :], mean_var[:, tile, 0:1], rstd[:, tile:tile + 1],
                                      ALU.subtract, ALU.mult).then_inc(y_ready, 1)

            def butterflies(b):
                dve.wait_ge(y_copied, b * KD + KD)
                done = b * 4
                for step, source, target in ((1, y_t, half_t), (2, half_t, y_t)):
                    halves = lambda m: m[:, :, :].rearrange("p (a two s) n -> p a two (s n)", two=2, s=step)
                    s, t = halves(source), halves(target)
                    dve.tensor_tensor(t[:, :, 0], s[:, :, 0], s[:, :, 1], ALU.add).then_inc(mix_step, 1)
                    dve.tensor_tensor(t[:, :, 1], s[:, :, 0], s[:, :, 1], ALU.subtract).then_inc(mix_step, 1)
                    done += 2
                    dve.wait_ge(mix_step, done)

            def mixed_lows(b):
                for c in range(KD):
                    dve.wait_ge(mixed_high, b * KD + c + 1)
                    dve.tensor_tensor(mixed[LOW][:, b, c, :], turn_ps[c % 2][:, :],
                                      mixed[HIGH][:, b, c, :].bitcast(F32), ALU.subtract).then_inc(mixed_ready, 1)

            def hidden(g, i, b):
                s = g * B + b
                if b == 0:
                    now = scales[:, :, g:g + 1] if isinstance(g, int) else scales[:, :, bass.ds(g, 1)]
                    dve.wait_ge(scales_ready, g + 1)
                    dve.tensor_copy(scale_now[:, i, :], now.rearrange("p k a -> p (k a)")).then_inc(scales_ready, 1)
                    dve.wait_ge(scales_ready, g + 2)
                dve.wait_ge(silu_ready, s + 1 + 2)
                dve.wait_ge(up_filled, s + 1)
                dve.wait_ge(z_low, s + 1)
                dve.scalar_tensor_tensor(z[:, b % 2, :], up_ps[b % 2][:, :], scale_now[:, i, 1:2], silu[:, b % 2, :],
                                         ALU.mult, ALU.mult).then_inc(z_ready, 1)

            def update(g, b):
                s = g * B + b
                for t in range(NT):
                    dve.wait_ge(down_filled, s * NT + t + 1 + 2 * NT)
                    dve.tensor_tensor(x_res[:, b * NT + t, :], x_res[:, b * NT + t, :], down_ps[t % 2][:, :],
                                      ALU.add).then_inc(down_free, 1)

            normed(0)
            butterflies(0)
            normed(1)
            mixed_lows(0)
            butterflies(1)
            for b in range(B):
                if b + 2 < B:
                    normed(b + 2)
                if b + 1 < B:
                    mixed_lows(b + 1)
                hidden(0, 0, b)
                if b + 2 < B:
                    butterflies(b + 2)
                if b:
                    update(0, b - 1)

            def chunk(g, i):
                hidden(g, i, 0)
                update(g - 1, B - 1)
                for b in range(1, B):
                    hidden(g, i, b)
                    update(g, b - 1)

            with dve.Fori(0, LOOPS) as i:
                chunk(2 * i + 1, 1)
                chunk(2 * i + 2, 0)
            chunk(KF - 1, 1)
            update(KF - 1, B - 1)


def build(nc, a, out):
    with ExitStack() as ctx:
        sem = lambda name: ctx.enter_context(nc.semaphore(name))
        x_res = ctx.enter_context(nc.sbuf_tensor("x_res", [P, T, D], F32))
        ident = ctx.enter_context(nc.sbuf_tensor("ident", [P, P], F32))
        ident_ready = sem("ident_ready")
        down_turned = nc.dram_tensor("down_turned", (P, KF, D), F32, kind="Internal").ap()
        down_mixed = nc.dram_tensor("down_mixed", (P, KF, D), F32, kind="Internal").ap()
        with ExitStack() as ffn:
            ffn_w1 = ffn.enter_context(nc.sbuf_tensor("ffn_w1", [P, KD, DFF], F32))
            ffn_w2 = ffn.enter_context(nc.sbuf_tensor("ffn_w2", [P, KF, D], F32))
            ffn_loaded = sem("ffn_loaded")
            with nc.Block() as block:
                @block.sync
                def _(sp):
                    sp.dma_start(ident[:, :], a["ident"]).then_inc(ident_ready, 16)

            gat_step(nc, sem, dict(x=a["x"], ctx_t=a["ctx_t"], W0=a["gat_w0"], W1=a["gat_w1"],
                                   a_self0=a["L0_xattn_a_self0"], a_neigh0=a["L0_xattn_a_neigh0"],
                                   a_self1=a["L0_xattn_a_self1"], a_neigh1=a["L0_xattn_a_neigh1"],
                                   b0=a["gat_b0"], b1=a["gat_b1"], ffn_w1=a["ffn_w1"], ffn_w2=a["ffn_w2"],
                                   down_t=a["down_t"], down_turned=down_turned),
                     x_res, ident, ident_ready, ffn_w1, ffn_w2, ffn_loaded)
            routed_ffn_step(nc, sem, dict(Wr=a["L0_ffn_Wr"], br=a["L0_ffn_br"], b1=a["ffn_b1"], b2=a["L0_ffn_b2"],
                                          before=a["before"], not_before=a["not_before"], slots=a["slots"],
                                          ones=a["ones"], hadamard=a["hadamard"], su_down=a["su_down"],
                                          down_scale=a["L1_ffn_Wscale_dp"], down_turned=down_turned),
                            x_res, ident, ffn_w1, ffn_w2, ffn_loaded, down_mixed)
        cross_attention_step(nc, sem, dict(wq=a["wq"], kcq=a["kcq"], wqr=a["wqr"],
                                           wo=a["wo"], kckv=a["kckv"], wkr=a["wkr"],
                                           ctx=a["ctx_512"], ctx_t=a["ctx_t"], cos=a["cos"], sin=a["sin"],
                                           cos_t=a["cos_t"], sin_t=a["sin_t"]), x_res, ident)
        gated_ffn_step(nc, sem, dict(up_gate=a["up_gate"], down=down_mixed, hadamard=a["hadamard"],
                                     su_up=a["su_up"], up_scale=a["up_scale"], gate_scale=a["gate_scale"]),
                       x_res, ident, out)


def laid_out(i):
    import numpy as np

    def pairs(v):
        return i[v].reshape(GP, 2 * GO).T

    def columns(v):
        return v.reshape(-1, P).T

    def swap(v, *axes):
        return i[v].transpose(axes)

    def chunked(m):
        return m.reshape(-1, P, *m.shape[1:]).swapaxes(0, 1)

    up_gate = np.stack([chunked(swap(n, 1, 0)).reshape(P, KD, KF, P) for n in ("L1_ffn_W_gate", "L1_ffn_W_up")])
    up_gate = up_gate.transpose(1, 3, 0, 2, 4).reshape(P, KF, 2 * KD * P)
    names = ["x", "ctx_512", "L0_xattn_a_self0", "L0_xattn_a_neigh0", "L0_xattn_a_self1", "L0_xattn_a_neigh1",
             "L0_ffn_Wr", "L0_ffn_br", "L0_ffn_b2", "L1_ffn_Wscale_dp"]
    return {**{n: i[n] for n in names}, "ctx_t": swap("ctx_512", 0, 2, 1),
            "gat_w0": swap("L0_xattn_W0", 1, 0, 2).reshape(F_IN, -1),
            "gat_w1": chunked(swap("L0_xattn_W1", 1, 0, 2).reshape(D, -1)),
            "gat_b0": pairs("L0_xattn_b0"), "gat_b1": pairs("L0_xattn_b1"),
            "ffn_w1": chunked(i["L0_ffn_W1"]), "ffn_w2": chunked(i["L0_ffn_W2"]), "ffn_b1": columns(i["L0_ffn_b1"]),
            "kcq": chunked(swap("L1_xattn_w_kc_q", 2, 0, 1)), "wqr": chunked(swap("L1_xattn_W_qr", 1, 0, 2)),
            "wq": chunked(i["L1_xattn_Wq"]), "wo": chunked(swap("L1_xattn_Wo", 1, 0)),
            "kckv": swap("L1_xattn_w_kc_kv", 1, 0, 2), "wkr": swap("L1_xattn_W_kr", 1, 0, 2),
            "up_gate": up_gate,
            "down_t": chunked(swap("L1_ffn_W_down", 1, 0)),
            "su_up": columns(i["L1_ffn_SU_ug"]), "su_down": columns(i["L1_ffn_SU_dp"]),
            "up_scale": columns(i["L1_ffn_Wscale_ug"][:DFF]), "gate_scale": columns(i["L1_ffn_Wscale_ug"][DFF:])}


def constants():
    import numpy as np
    f32 = np.float32
    row, column = np.arange(N).reshape(NT, P).T[:, :, None], np.arange(N)[None, None, :]
    slots = np.full((P, 2, P), -1.0, f32)
    for g in range(2):
        slots[:, g, g * TOPK:(g + 1) * TOPK] = np.arange(TOPK)
    inv_freq = f32(1.0) / f32(10000.0) ** (np.arange(0, F_IN, 2, dtype=f32) / f32(F_IN))
    freqs = np.arange(N, dtype=f32)[:, None] * inv_freq[None, :]
    cos = np.repeat(np.cos(freqs), 2, axis=-1)
    sin = np.repeat(np.sin(freqs), 2, axis=-1)
    sin[:, :F_IN // 2] *= f32(-1.0)
    rows = lambda m: m.reshape(NT, P, F_IN).transpose(1, 0, 2)
    hadamard = np.ones((1, 1), f32)
    while hadamard.shape[0] < P:
        hadamard = np.block([[hadamard, hadamard], [hadamard, -hadamard]])
    return {"cos": np.ascontiguousarray(rows(cos)), "sin": np.ascontiguousarray(rows(sin)),
            "cos_t": np.ascontiguousarray(cos.T), "sin_t": np.ascontiguousarray(sin.T), "hadamard": hadamard,
            "ident": np.eye(P, dtype=f32), "ones": np.ones((P, P), f32), "slots": slots,
            "before": (column < row).astype(f32), "not_before": (column >= row).astype(f32)}


def kernel(**inputs):
    import numpy as np
    import concourse.bacc as bacc
    from concourse.bass_utils import run_bass_kernel_spmd as run

    nc = bacc.Bacc("TRN2", target_bir_lowering=False, num_devices=1)
    arrays = {name: np.ascontiguousarray(v) for name, v in laid_out(inputs).items()}
    arrays.update(constants())
    a = {name: nc.dram_tensor(f"in_{name}", v.shape, F32, kind="ExternalInput").ap() for name, v in arrays.items()}
    out = nc.dram_tensor("out", (B, N, D), F32, kind="ExternalOutput").ap()
    build(nc, a, out)
    r = run(nc, [{f"in_{name}": v for name, v in arrays.items()}], core_ids=[0])
    return r.results[0]["out"]
```

```python
from contextlib import ExitStack

import concourse.bass as bass
from concourse import mybir

ALU = mybir.AluOpType
ACT = mybir.ActivationFunctionType
AX = mybir.AxisListType
F32 = mybir.dt.float32

P = 128
B, N, D = 4, 512, 512
NT = N // P
T = B * NT
KD = D // P
F_IN = 128
GH, GO = 8, 64
GP = GH // 2
TOPK = N // 8
DFF = 4 * D
KF = DFF // P
XH, XR = 16, 64
DCQ = 384
LN_EPS = 1e-5
MASK_VAL = -1.0e10
SLOPE = 0.2
BIG = 3.0e38


def layernorm_stats(dve, act, x_res, stats, mean_var, std, rstd, sems, have_stats=False):
    stats_done, var_done, std_done, rstd_done = sems

    def on_vector(before=lambda t: None):
        done = 0
        if not have_stats:
            for t in range(T):
                before(t)
                dve.bn_stats(stats[:, t, :], x_res[:, t, :]).then_inc(stats_done, 1)
            done = T
            dve.wait_ge(stats_done, done)
        for t in range(T):
            dve.bn_aggr(mean_var[:, t, :], stats[:, t, :]).then_inc(stats_done, 1)
        dve.wait_ge(stats_done, done + T)
        dve.tensor_scalar(std[:, :], mean_var[:, :, 1], LN_EPS, None, ALU.add).then_inc(var_done, 1)
        dve.wait_ge(std_done, 1)
        dve.reciprocal(rstd[:, :], std[:, :]).then_inc(rstd_done, 1)
        dve.wait_ge(rstd_done, 1)

    def on_scalar():
        act.wait_ge(var_done, 1)
        act.activation(std[:, :], std[:, :], ACT.Sqrt).then_inc(std_done, 1)

    return on_vector, on_scalar


def gat_step(nc, sem, d, x_res, ident, ident_ready, ffn_w1, ffn_loaded):
    with ExitStack() as ctx:
        sb = lambda name, shape: ctx.enter_context(nc.sbuf_tensor(name, shape, F32))
        ps = lambda name, shape: ctx.enter_context(nc.psum_tensor(name, shape, F32))

        mean_var = sb("g_mean_var", [P, T, 2])
        std, rstd = sb("g_std", [P, T]), sb("g_rstd", [P, T])
        weights = [sb("g_w0", [P, 1, GH * GO]), sb("g_w1", [P, KD, GH * GO])]
        vectors = [sb("g_v0", [P, 1, 2 * GH]), sb("g_v1", [P, KD, 2 * GH])]
        a_rows = sb("g_a_rows", [P, 4, GH * GO])
        bias = sb("g_bias", [P, 2, GH * GO])
        ctx_t = sb("g_ctx_t", [P, 2, N])
        hidden_t = sb("g_hidden_t", [P, 2, GP, N])
        head_out, low = sb("g_head_out", [P, 2, NT, P]), sb("g_low", [P, N])
        mask = sb("g_mask", [P, 2, NT, N])
        row_min, mask_max = sb("g_row_min", [P, NT]), sb("g_mask_max", [P, NT])
        feat = sb("g_feat", [P, 2, NT, GH * GO])
        self_neigh = sb("g_self_neigh", [P, 2, NT, 2 * GH])
        self_part = sb("g_self_part", [P, 2, NT, GH])
        neigh_row = sb("g_neigh_row", [P, 2, N])
        NA, NE = 4, 5
        base = sb("g_base", [P, NA, N])
        expo = sb("g_expo", [P, NE, N])
        neg_max, sums, rsums = sb("g_neg_max", [P, 8]), sb("g_sums", [P, 2, NT, 2]), sb("g_rsums", [P, NT, 2])
        KC, QH = DCQ // P, XH // 2
        kcq_t, wqr = sb("g_kcq_t", [P, KC, QH, P]), sb("g_wqr", [P, KC, QH, XR])
        q_latent = wqr[:, 0, :, :]
        q_loaded, q_stored = [sem("g_kcq_loaded"), sem("g_wqr_loaded")], sem("g_q_stored")
        NS = 4
        probs_t = sb("g_probs_t", [P, NS, NT, P])
        product = low
        stats = head_out[:, 0, 0, 0:T * 6].rearrange("p (t s) -> p t s", t=T)

        neigh_ps = [ps(f"g_neigh_ps{i}", [P, N]) for i in range(2)]
        relu_ps = [ps(f"g_relu_ps{i}", [P, N]) for i in range(2)]
        turn_ps = [ps(f"g_turn_ps{i}", [P, N]) for i in range(2)]
        out_ps = [ps(f"g_out_ps{i}", [P, N]) for i in range(2)]

        x_loaded, w_loaded = [sem(f"g_x_loaded{b}") for b in range(B)], sem("g_w_loaded")
        ctx_loaded = sem("g_ctx_loaded")
        ln_sems = [sem("g_stats_done"), sem("g_var_done"), sem("g_std_done"), sem("g_rstd_done")]
        product_done, vectors_ready = sem("g_product_done"), sem("g_vectors_ready")
        mask_step, parts_ready = sem("g_mask_step"), sem("g_parts_ready")
        neigh_filled, row_ready, base_ready = sem("g_neigh_filled"), sem("g_row_ready"), sem("g_base_ready")
        relu_ready, expo_ready, exp_done = sem("g_relu_ready"), sem("g_expo_ready"), sem("g_exp_done")
        rsum_ready = sem("g_rsum_ready")
        turned, turn_free = sem("g_turned"), sem("g_turn_free")
        attn_done, out_free = sem("g_attn_done"), sem("g_out_free")
        low_ready, low_exp, elu_ready = sem("g_low_ready"), sem("g_low_exp"), sem("g_elu_ready")
        x_added = sem("g_x_added")

        SEGMENTS = [(0, 0), (0, 1), (1, 0), (1, 1)]
        SEG = GH * NT
        TILES = len(SEGMENTS) * SEG
        HEADS, PAIRS = TILES // NT, TILES // (2 * NT)
        MASK_STEPS = 4 * NT + 1
        LAG = NT
        DIVIDE, LOW_EXP, ELU = 13, 14, 15

        def extras(i):
            segment, step = i // SEG, i % SEG
            found = []
            if step in (16, 24) and SEGMENTS[segment][0] == 0:
                found.append(("pair", segment, (step - 16) // 8))
            if step in (0, 8) and segment and SEGMENTS[segment - 1][0] == 0:
                found.append(("pair", segment - 1, 2 + step // 8))
            if segment == len(SEGMENTS) - 1 and step in (6, 12, 18, 24):
                found.append(("latent", segment, step // 6 - 1))
            if segment + 1 < len(SEGMENTS):
                if step == 13:
                    found.append(("self", segment + 1, 0))
                if step in (16, 20, 24, 28):
                    found.append(("feature", segment + 1, (step - 16) // 4))
            return found

        order = [("self", 0, 0)] + [("feature", 0, t) for t in range(NT)]
        for i in range(TILES):
            order += [("tile", i // SEG, i % SEG)] + extras(i)
        USES = len(order)
        assert USES % 2 == 0

        def use_of(*use):
            return order.index(use)

        butterflies = DownButterflies(sem, d["down_t"], d["down_turned"], a_rows, sb)
        block = ctx.enter_context(nc.Block())

        @block.sync
        def _(sp):
            for b in range(B):
                if b == 1:
                    sp.wait_ge(w_loaded, 16 * 8)
                sp.dma_start(x_res[:, b * NT:(b + 1) * NT, :],
                             d["x"][b].rearrange("(t p) c -> p t c", p=P)).then_inc(x_loaded[b], 16)
            sp.dma_start(ffn_w1[:, :, :], d["ffn_w1"]).then_inc(ffn_loaded, 16)
            sp.sem_inc(butterflies.stored, 16)
            sp.wait_ge(vectors_ready, 2 + 2 * KD)
            butterflies.load_and_store(sp)

        @block.gpsimd
        def _(pool):
            pool.sem_inc(base_ready, 8)
            with pool.Fori(0, B // 2) as p:
                for i in range(TILES):
                    head, (layer, graph) = i // NT, SEGMENTS[i // SEG]
                    pool.wait_ge(row_ready, p * HEADS + head + 1)
                    pool.wait_ge(expo_ready, p * TILES + i + 1)
                    pool.tensor_tensor(base[:, i % NA, :], mask[:, graph, i % NT, :], neigh_row[:, head % 2, :],
                                       ALU.add).then_inc(base_ready, 1)
                    if i % (2 * NT) == 2 * NT - 1:
                        step = i // (2 * NT)
                        butterflies.step(pool, 2 * p + step // butterflies.STEPS, step % butterflies.STEPS)

        @block.tensor
        def _(pe):
            pe.sem_inc(attn_done, NS)
            pe.wait_ge(ident_ready, 16)
            pe.wait_ge(vectors_ready, 2 + 2 * KD)
            with pe.Fori(0, B // 2) as p:
                def turn(u, pieces, source_ready):
                    pe.wait_ge(turn_free, p * USES + u + 1)
                    pe.wait_ge(*source_ready)
                    for c, piece in enumerate(pieces):
                        last = pe.transpose(turn_ps[u % 2][:, c * P:(c + 1) * P], piece, ident[:, :])
                    last.then_inc(turned, 1)

                def source(segment, c, t):
                    layer, graph = SEGMENTS[segment]
                    at = slice(t * P, (t + 1) * P)
                    return ctx_t[:, graph, at] if layer == 0 else hidden_t[:, graph, c, at]

                def self_terms(segment):
                    layer, graph = SEGMENTS[segment]
                    if layer == 0:
                        pe.wait_ge(ctx_loaded, 16 * p + 16)
                    else:
                        pe.wait_ge(turn_free, p * USES + use_of("pair", graph, GP - 1) + 1 + 2)
                    u = use_of("self", segment, 0)
                    pe.wait_ge(turn_free, p * USES + u + 1)
                    chunks = [1, KD][layer]
                    for t in range(NT):
                        for c in range(chunks):
                            last = pe.matmul(turn_ps[u % 2][:, t * 2 * GH:(t + 1) * 2 * GH], source(segment, c, t),
                                             vectors[layer][:, c, :], start=(c == 0), stop=(c == chunks - 1))
                    last.then_inc(turned, 1)

                def feature(segment, t):
                    layer, graph = SEGMENTS[segment]
                    u = use_of("feature", segment, t)
                    pe.wait_ge(turn_free, p * USES + u + 1)
                    chunks = [1, KD][layer]
                    for c in range(chunks):
                        last = pe.matmul(turn_ps[u % 2][:, :], source(segment, c, t), weights[layer][:, c, :],
                                         start=(c == 0), stop=(c == chunks - 1))
                    last.then_inc(turned, 1)

                def neighbour(head):
                    segment, h = head // GH, head % GH
                    if h == 0:
                        pe.wait_ge(turn_free, p * USES + use_of("self", segment, 0) + 1 + 2)
                    pe.wait_ge(relu_ready, p * TILES + NT * head + NT)
                    for t in range(NT):
                        last = pe.transpose(neigh_ps[head % 2][:, t * P:(t + 1) * P],
                                            self_neigh[:, segment % 2, t, GH + h:GH + h + 1].to_broadcast([P, P]),
                                            ident[:, :])
                    last.then_inc(neigh_filled, 1)

                def query_latents(segment, n):
                    u = use_of("latent", segment, n)
                    pe.wait_ge(turn_free, p * USES + u + 1)
                    for loaded in q_loaded:
                        pe.wait_ge(loaded, 16 * p + 16)
                    for i in range(QH // 4):
                        for c in range(KC):
                            last = pe.matmul(turn_ps[u % 2][:, i * XR:(i + 1) * XR], kcq_t[:, c, n * QH // 4 + i, :],
                                             wqr[:, c, n * QH // 4 + i, :], start=(c == 0), stop=(c == KC - 1))
                    last.then_inc(turned, 1)

                def turn_pair(segment, q):
                    pair = segment * GP + q
                    turn(use_of("pair", segment, q), [head_out[:, pair % 2, t, :] for t in range(NT)],
                         (elu_ready, p * PAIRS + pair + 1))

                def attend(i):
                    segment, pair, h, t = i // SEG, i // (2 * NT), i // NT % GH, i % NT
                    pe.wait_ge(turn_free, p * USES + use_of("tile", segment, i % SEG) + 1 + 2)
                    if i % (2 * NT) == 0:
                        pe.wait_ge(out_free, p * PAIRS + pair + 1)
                    at = (t * 2 + h % 2) * GO
                    for k in range(NT):
                        last = pe.matmul(out_ps[pair % 2][:, at:at + GO], probs_t[:, i % NS, k, :],
                                         feat[:, segment % 2, k, h * GO:(h + 1) * GO],
                                         start=(k == 0), stop=(k == NT - 1))
                    last.then_inc(attn_done, 1)

                self_terms(0)
                neighbour(0)
                neighbour(1)
                for t in range(NT):
                    feature(0, t)
                for i in range(TILES):
                    if i % NT == NT - 1 and i // NT + 2 < HEADS:
                        neighbour(i // NT + 2)
                    turn(use_of("tile", i // SEG, i % SEG), [expo[:, i % NE, c * P:(c + 1) * P] for c in range(NT)],
                         (exp_done, p * TILES + i + 1))
                    if i >= 2:
                        attend(i - 2)
                    for kind, segment, n in extras(i):
                        if kind == "pair":
                            turn_pair(segment, n)
                        elif kind == "self":
                            self_terms(segment)
                        elif kind == "latent":
                            query_latents(segment, n)
                        else:
                            feature(segment, n)
                attend(TILES - 2)
                attend(TILES - 1)

        @block.scalar
        def _(act):
            act.sem_inc(relu_ready, 8)
            act.sem_inc(q_stored, 16)
            for i, name in enumerate(("a_self0", "a_neigh0", "a_self1", "a_neigh1")):
                act.dma_start(a_rows[:, i, :], d[name].rearrange("h o -> (h o)").partition_broadcast(P)
                              ).then_inc(w_loaded, 16)
            act.dma_start(weights[0][:, 0, :], d["W0"]).then_inc(w_loaded, 16)
            act.dma_start(weights[1][:, :, :], d["W1"]).then_inc(w_loaded, 16)
            for i, name in enumerate(("b0", "b1")):
                act.dma_start(bias[:, i, :], d[name].rearrange("h o -> (h o)").partition_broadcast(P)
                              ).then_inc(w_loaded, 16)
            layernorm_stats(None, act, x_res, stats, mean_var, std, rstd, ln_sems)[1]()
            with act.Fori(0, B // 2) as p:
                def neighbour_row(head):
                    act.wait_ge(neigh_filled, p * HEADS + head + 1)
                    act.wait_ge(base_ready, p * TILES + NT * head + NT)
                    act.activation(neigh_row[:, head % 2, :], neigh_ps[head % 2][:, :], ACT.Copy, scale=SLOPE
                                   ).then_inc(row_ready, 1)

                act.wait_ge(q_stored, 16 * p + 16)
                act.dma_start(ctx_t[:, :, :], d["ctx_t"][bass.ds(2 * p, 2)].rearrange("b f n -> f b n")
                              ).then_inc(ctx_loaded, 16)
                for dst, src, done in ((kcq_t, d["kcq"], q_loaded[0]), (wqr, d["wqr"], q_loaded[1])):
                    act.dma_start(dst[:, :, :, :], src[:, :, bass.ds(p * QH, QH), :]).then_inc(done, 16)
                neighbour_row(0)
                for i in range(TILES - SEG + LOW_EXP + 3 * 8 + 1):
                    if i < TILES:
                        segment, head, t = i // SEG, i // NT, i % NT
                        if i % SEG == 0:
                            act.wait_ge(parts_ready, p * len(SEGMENTS) + segment + 1)
                        act.wait_ge(expo_ready, p * TILES + i - 2 + 1 + NA)
                        act.activation(relu_ps[i % 2][:, :], neigh_ps[head % 2][:, :], ACT.Relu,
                                       bias=self_part[:, segment % 2, t, head % GH:head % GH + 1], scale=1.0 - SLOPE
                                       ).then_inc(relu_ready, 1)
                    if 1 <= i <= TILES:
                        n = i - 1
                        act.wait_ge(expo_ready, p * TILES + n + 1 + NA)
                        act.activation(expo[:, n % NE, :], expo[:, n % NE, :], ACT.Exp,
                                       bias=neg_max[:, n % 8:n % 8 + 1], scale=-1.0,
                                       accum_out=sums[:, n // 8 % 2, n % NT, n // NT % 2:n // NT % 2 + 1]
                                       ).then_inc(exp_done, 1)
                    if i % NT == 2 and i // NT + 1 < HEADS:
                        neighbour_row(i // NT + 1)
                    if i >= LOW_EXP and (i - LOW_EXP) % 8 == 0:
                        act.wait_ge(low_ready, p * PAIRS + (i - LOW_EXP) // 8 + 1)
                        act.activation(low[:, :], low[:, :], ACT.Exp).then_inc(low_exp, 1)
                act.wait_ge(turn_free, p * USES + use_of("latent", len(SEGMENTS) - 1, 3) + 1 + 2)
                act.dma_start(d["q_latent"][:, bass.ds(p * QH, QH), :], q_latent[:, :, :]).then_inc(q_stored, 16)
            act.wait_ge(q_stored, 16 * (B // 2 + 1))

        @block.vector
        def _(dve):
            dve.sem_inc(expo_ready, NA)
            dve.sem_inc(turn_free, 2)
            dve.sem_inc(out_free, 2)
            dve.wait_ge(w_loaded, 16 * 8)
            n_products = 0
            for layer in range(2):
                for c in range([1, KD][layer]):
                    for side in range(2):
                        if n_products:
                            dve.wait_ge(vectors_ready, n_products)
                        dve.tensor_tensor(product[:, :], weights[layer][:, c, :], a_rows[:, 2 * layer + side, :],
                                          ALU.mult).then_inc(product_done, 1)
                        n_products += 1
                        dve.wait_ge(product_done, n_products)
                        dve.tensor_reduce(vectors[layer][:, c, side * GH:(side + 1) * GH],
                                          product[:, :].rearrange("p (h o) -> p h o", h=GH), AX.X, ALU.add
                                          ).then_inc(vectors_ready, 1)
            layernorm_stats(dve, None, x_res, stats, mean_var, std, rstd, ln_sems)[0](
                lambda t: dve.wait_ge(x_loaded[t // NT], 16) if t % NT == 0 else None)
            with dve.Fori(0, B // 2) as p:
                def mask_of(graph):
                    first = p * 2 * MASK_STEPS + graph * MASK_STEPS
                    tile = lambda t: bass.ds(p * 2 * NT + graph * NT + t, 1)
                    own = mask[:, graph, :, :]

                    def normed(t):
                        dve.tensor_scalar(own[:, t, :], x_res[:, tile(t), :].rearrange("p a c -> p (a c)"),
                                          mean_var[:, tile(t), 0], rstd[:, tile(t)], ALU.subtract, ALU.mult
                                          ).then_inc(mask_step, 1)

                    def complement(t):
                        dve.wait_ge(mask_step, first + NT)
                        dve.tensor_scalar(own[:, t, :], own[:, t, :], -1.0, 1.0, ALU.mult, ALU.add
                                          ).then_inc(mask_step, 1)

                    def smallest(t):
                        dve.wait_ge(mask_step, first + 2 * NT)
                        dve.tensor_reduce(row_min[:, t:t + 1], own[:, t, :], AX.X, ALU.min).then_inc(mask_step, 1)

                    def scaled(t):
                        if t == 0:
                            dve.wait_ge(mask_step, first + 3 * NT)
                            dve.tensor_scalar(mask_max[:, :], row_min[:, :], MASK_VAL, None, ALU.mult
                                              ).then_inc(mask_step, 1)
                            dve.wait_ge(mask_step, first + 3 * NT + 1)
                        dve.tensor_scalar(own[:, t, :], own[:, t, :], MASK_VAL, mask_max[:, t:t + 1],
                                          ALU.mult, ALU.subtract).then_inc(mask_step, 1)

                    return [(step, t) for step in (normed, complement, smallest, scaled) for t in range(NT)]

                def self_copy(segment):
                    u = use_of("self", segment, 0)
                    dve.wait_ge(turned, p * USES + u + 1)
                    columns = turn_ps[u % 2][:, 0:NT * 2 * GH].rearrange("p (t h) -> p t h", t=NT)
                    dve.tensor_scalar(self_part[:, segment % 2, :, :], columns[:, :, 0:GH], 1.0 - SLOPE, None,
                                      ALU.mult).then_inc(parts_ready, 1)
                    dve.tensor_copy(self_neigh[:, segment % 2, :, :], columns).then_inc(turn_free, 1)

                def latent_copy(segment, n):
                    u = use_of("latent", segment, n)
                    dve.wait_ge(turned, p * USES + u + 1)
                    dve.tensor_copy(q_latent[:, n * QH // 4:(n + 1) * QH // 4, :].rearrange("p h r -> p (h r)"),
                                    turn_ps[u % 2][:, 0:QH // 4 * XR]).then_inc(turn_free, 1)

                def feature_copy(segment, t):
                    u = use_of("feature", segment, t)
                    dve.wait_ge(turned, p * USES + u + 1)
                    dve.tensor_tensor(feat[:, segment % 2, t, :], turn_ps[u % 2][:, :],
                                      bias[:, SEGMENTS[segment][0], :], ALU.add).then_inc(turn_free, 1)

                def tile_copy(i):
                    u = use_of("tile", i // SEG, i % SEG)
                    dve.wait_ge(turned, p * USES + u + 1)
                    dve.wait_ge(attn_done, p * TILES + i + 1)
                    dve.tensor_copy(probs_t[:, i % NS, :, :], turn_ps[u % 2][:, :].rearrange(
                        "p (k n) -> p k n", k=NT)).then_inc(turn_free, 1)

                def pair_copy(segment, q):
                    u = use_of("pair", segment, q)
                    dve.wait_ge(turned, p * USES + u + 1)
                    dve.tensor_scalar(hidden_t[:, segment, q, :], turn_ps[u % 2][:, :], -1.0, None, ALU.add
                                      ).then_inc(turn_free, 1)

                def divide(pair):
                    dve.wait_ge(attn_done, p * TILES + (pair + 1) * 2 * NT + NS)
                    dve.reciprocal(rsums[:, :, :], sums[:, pair % 2, :, :]).then_inc(rsum_ready, 1)
                    dve.wait_ge(rsum_ready, p * PAIRS + pair + 1)
                    dve.tensor_tensor(head_out[:, pair % 2, :, :].rearrange("p t (h o) -> p (t h) o", h=2),
                                      out_ps[pair % 2][:, :].rearrange("p (g o) -> p g o", o=GO),
                                      rsums[:, :, :].rearrange("p t h -> p (t h)").unsqueeze(2).to_broadcast(
                                          [P, 2 * NT, GO]), ALU.mult).then_inc(out_free, 1)
                    dve.wait_ge(out_free, p * PAIRS + pair + 1 + 2)
                    dve.tensor_scalar(low[:, :], head_out[:, pair % 2, :, :].rearrange("p t c -> p (t c)"), 0.0,
                                      None, ALU.min).then_inc(low_ready, 1)

                def elu(pair):
                    layer, graph = SEGMENTS[pair // GP]
                    rows = head_out[:, pair % 2, :, :].rearrange("p t c -> p (t c)")
                    dve.wait_ge(low_exp, p * PAIRS + pair + 1)
                    dve.scalar_tensor_tensor(rows, rows, 0.0, low[:, :], ALU.max, ALU.add).then_inc(elu_ready, 1)
                    if layer == 1:
                        q = pair % GP
                        x_part = x_res[:, bass.ds(p * 2 * NT + graph * NT, NT), q * P:(q + 1) * P]
                        dve.wait_ge(elu_ready, p * PAIRS + pair + 1)
                        dve.scalar_tensor_tensor(x_part, head_out[:, pair % 2, :, :], -1.0, x_part, ALU.add, ALU.add
                                                 ).then_inc(x_added, 1)

                for step, t in mask_of(0):
                    step(t)
                self_copy(0)
                second_mask = mask_of(1)
                for i in range(TILES - SEG + ELU + 3 * 8 + 1):
                    if i < TILES:
                        dve.wait_ge(relu_ready, p * TILES + i + 1 + 8)
                        dve.wait_ge(base_ready, p * TILES + i + 1 + 8)
                    if i < NT:
                        feature_copy(0, i)
                    elif i - LAG < TILES:
                        tile_copy(i - LAG)
                        for kind, segment, n in extras(i - LAG):
                            if kind == "pair":
                                pair_copy(segment, n)
                            elif kind == "self":
                                self_copy(segment)
                            elif kind == "latent":
                                latent_copy(segment, n)
                            else:
                                feature_copy(segment, n)
                    if i < TILES:
                        dve.tensor_tensor_reduce(expo[:, i % NE, :], relu_ps[i % 2][:, :], base[:, i % NA, :],
                                                 -1.0, BIG, ALU.add, ALU.min, neg_max[:, i % 8:i % 8 + 1]
                                                 ).then_inc(expo_ready, 1)
                    if 4 <= i < 4 + len(second_mask):
                        step, t = second_mask[i - 4]
                        step(t)
                    if i >= DIVIDE and (i - DIVIDE) % 8 == 0:
                        divide((i - DIVIDE) // 8)
                    if i >= ELU and (i - ELU) % 8 == 0:
                        elu((i - ELU) // 8)


class DownButterflies:

    def __init__(self, sem, source, target, room, sb):
        self.source, self.target = source, target
        self.COLS = D // B
        self.a = room[:, :, :].rearrange("p a (k o) -> p (a k) o", o=self.COLS)
        self.b = sb("b_b", [P, KF, self.COLS])
        self.loaded, self.butterfly, self.stored = sem("b_loaded"), sem("b_butterfly"), sem("b_stored")
        self.STEPS = 8

    def load_and_store(self, sp):
        with sp.Fori(0, B) as s:
            sp.wait_ge(self.stored, 16 * s + 16)
            sp.dma_start(self.a[:, :, :], self.source[:, :, bass.ds(s * self.COLS, self.COLS)]
                         ).then_inc(self.loaded, 16)
            sp.wait_ge(self.butterfly, self.STEPS * (s + 1))
            sp.dma_start(self.target[:, :, bass.ds(s * self.COLS, self.COLS)], self.a[:, :, :]
                         ).then_inc(self.stored, 16)
        sp.wait_ge(self.stored, 16 * (B + 1))

    def step(self, pool, s, n):
        if n == 0:
            pool.wait_ge(self.loaded, 16 * (s + 1))
        else:
            pool.wait_ge(self.butterfly, self.STEPS * s + n // 2 * 2)
        source, target = (self.a, self.b) if n // 2 % 2 == 0 else (self.b, self.a)
        halves = lambda m: m[:, :, :].rearrange("p (g two s) o -> p g two (s o)", two=2, s=1 << (n // 2))
        x, y = halves(source), halves(target)
        pool.tensor_tensor(y[:, :, n % 2], x[:, :, 0], x[:, :, 1], [ALU.add, ALU.subtract][n % 2]
                           ).then_inc(self.butterfly, 1)


class DownWeights:

    def __init__(self, sem, d, target, sb, ps):
        self.d, self.target, self.ps = d, target, ps
        self.K = 4
        self.turned = sb("d_turned", [P, 2, self.K, D])
        self.mixed = sb("d_mixed", [P, self.K, D])
        self.hadamard, self.signs, self.scale = sb("d_hadamard", [P, P]), sb("d_signs", [P, KF]), sb("d_scale", [P, D])
        self.small_loaded, self.loaded = sem("d_small_loaded"), [sem("d_loaded0"), sem("d_loaded1")]
        self.filled, self.signed, self.scaled = sem("d_filled"), sem("d_signed"), sem("d_scaled")
        self.stored = sem("d_stored")

    def load_and_store(self, sp):
        K = self.K
        for dst, src in ((self.hadamard[:, :], self.d["hadamard"]), (self.signs[:, :], self.d["su_down"]),
                         (self.scale[:, :], self.d["down_scale"].partition_broadcast(P))):
            sp.dma_start(dst, src).then_inc(self.small_loaded, 16)
        for g in range(KF // K + 1):
            if g < KF // K:
                if g >= 2:
                    sp.wait_ge(self.filled, K * (g - 1))
                sp.dma_start(self.turned[:, g % 2, :, :], self.d["down_turned"][:, g * K:(g + 1) * K, :]
                             ).then_inc(self.loaded[g % 2], 16)
            if g:
                sp.wait_ge(self.scaled, K * g + 1)
                sp.dma_start(self.target[:, (g - 1) * K:g * K, :], self.mixed[:, :, :]).then_inc(self.stored, 16)
        sp.wait_ge(self.stored, 16 * KF // K)

    def group(self, g):
        return range(g * self.K, (g + 1) * self.K)

    def matmuls(self, pe, g):
        pe.wait_ge(self.small_loaded, 48)
        for k in self.group(g):
            if k % self.K == 0:
                pe.wait_ge(self.loaded[g % 2], 16 * (g // 2 + 1))
            if k >= 2:
                pe.wait_ge(self.signed, k - 1)
            pe.matmul(self.ps[k % 2][:, :], self.hadamard[:, :], self.turned[:, k // self.K % 2, k % self.K, :],
                      start=True, stop=True).then_inc(self.filled, 1)

    def sign(self, act, g):
        act.wait_ge(self.small_loaded, 48)
        for k in self.group(g):
            act.wait_ge(self.filled, k + 1)
            if k >= self.K and k % self.K == 0:
                act.wait_ge(self.stored, 16 * (k // self.K))
            act.activation(self.mixed[:, k % self.K, :], self.ps[k % 2][:, :], ACT.Copy,
                           scale=self.signs[:, k:k + 1]).then_inc(self.signed, 1)

    def scale_out(self, pool, g):
        if g == 0:
            pool.wait_ge(self.small_loaded, 48)
            pool.tensor_scalar(self.scale[:, :], self.scale[:, :], float(DFF) ** -0.5, None, ALU.mult
                               ).then_inc(self.scaled, 1)
            pool.wait_ge(self.scaled, 1)
        for k in self.group(g):
            pool.wait_ge(self.signed, k + 1)
            pool.tensor_tensor(self.mixed[:, k % self.K, :], self.mixed[:, k % self.K, :], self.scale[:, :],
                               ALU.mult).then_inc(self.scaled, 1)


def routed_ffn_step(nc, sem, d, x_res, ident, ffn_w1, ffn_loaded, down_mixed):
    with ExitStack() as ctx:
        sb = lambda name, shape: ctx.enter_context(nc.sbuf_tensor(name, shape, F32))
        ps = lambda name, shape: ctx.enter_context(nc.psum_tensor(name, shape, F32))
        PT = 2 * NT
        KH = DFF // P
        stats, mean_var = sb("r_stats", [P, T, 6]), sb("r_mean_var", [P, T, 2])
        std, rstd = sb("r_std", [P, T]), sb("r_rstd", [P, T])
        wr_row, b2_row = sb("r_wr_row", [P, D]), sb("r_b2_row", [P, D])
        br, b1 = sb("r_br", [P, 1]), sb("r_b1", [P, KH])
        before, not_before = sb("r_before", [P, NT, N]), sb("r_not_before", [P, NT, N])
        slots = sb("r_slots", [P, 2, P])
        ones = sb("r_ones", [P, P])
        y = sb("r_y", [P, PT, D])
        scratch = sb("r_scratch", [P, 2, D])
        dots, logit = sb("r_dots", [P, PT]), sb("r_logit", [P, PT])
        logit_row = sb("r_logit_row", [P, 2, N])
        neg_max = sb("r_neg_max", [P, 2])
        above = sb("r_above", [P, 2, PT])
        rank, picked = sb("r_rank", [P, PT]), sb("r_picked", [P, PT])
        expo, weight = sb("r_expo", [P, PT]), sb("r_weight", [P, T])
        total, rtotal = sb("r_total", [P, 2]), sb("r_rtotal", [P, 2])
        onehot, onehot_t = sb("r_onehot", [P, PT, P]), sb("r_onehot_t", [P, T, P])
        fx_t = sb("r_fx_t", [P, KD, 4 * TOPK])
        hidden_t = sb("r_hidden_t", [P, KH, 4 * TOPK])
        picks_out = sb("r_picks_out", [P, 2, D])

        row_ps = [ps(f"r_row_ps{i}", [P, N]) for i in range(2)]
        total_ps = ps("r_total_ps", [P, N])
        fx_ps = ps("r_fx_ps", [P, N])
        turn_ps = [ps(f"r_turn_ps{i}", [P, N]) for i in range(2)]
        hidden_ps = [ps(f"r_hidden_ps{i}", [P, N]) for i in range(2)]

        ffn_w2 = sb("r_ffn_w2", [P, KF, D])
        loaded, w2_loaded = sem("r_loaded"), sem("r_w2_loaded")
        ln_sems = [sem("r_stats_done"), sem("r_var_done"), sem("r_std_done"), sem("r_rstd_done")]
        y_ready, dot_done, logit_ready = sem("r_y_ready"), sem("r_dot_done"), sem("r_logit_ready")
        row_filled, row_copied, max_ready = sem("r_row_filled"), sem("r_row_copied"), sem("r_max_ready")
        exp_done, count_done, rank_ready = sem("r_exp_done"), sem("r_count_done"), sem("r_rank_ready")
        chosen, total_filled, total_step = sem("r_chosen"), sem("r_total_filled"), sem("r_total_step")
        onehot_ready, gathered, fx_copied = sem("r_onehot_ready"), sem("r_gathered"), sem("r_fx_copied")
        turned, turn_copied, y_added = sem("r_turned"), sem("r_turn_copied"), sem("r_y_added")
        hidden_filled, hidden_ready = sem("r_hidden_filled"), sem("r_hidden_ready")
        out_filled, out_ready = sem("r_out_filled"), sem("r_out_ready")
        scattered, x_updated = sem("r_scattered"), sem("r_x_updated")
        LOADS = 8
        down_weights = DownWeights(sem, d, down_mixed, sb, hidden_ps)
        block = ctx.enter_context(nc.Block())

        @block.sync
        def _(sp):
            for dst, src in ((wr_row[:, :], d["Wr"].rearrange("d a -> (d a)").partition_broadcast(P)),
                             (b2_row[:, :], d["b2"].partition_broadcast(P)),
                             (br[:, :], d["br"].partition_broadcast(P)), (b1[:, :], d["b1"]),
                             (before[:, :, :], d["before"]), (not_before[:, :, :], d["not_before"]),
                             (slots[:, :, :], d["slots"]), (ones[:, :], d["ones"])):
                sp.dma_start(dst, src).then_inc(loaded, 16)
            down_weights.load_and_store(sp)

        @block.gpsimd
        def _(pool):
            for pair in range(2):
                for i in range(PT):
                    pool.wait_ge(y_ready, pair * PT + i + 1)
                    tile = pair * PT + i
                    pool.tensor_tensor(x_res[:, tile, :], x_res[:, tile, :], y[:, i, :], ALU.add
                                       ).then_inc(y_added, 1)
                for g in ((0, 1, 2), (3,))[pair]:
                    down_weights.scale_out(pool, g)

        @block.tensor
        def _(pe):
            down_weights.matmuls(pe, 0)
            pe.wait_ge(loaded, 16 * LOADS)
            for pair in range(2):
                pe.wait_ge(logit_ready, pair + 1)
                for g in range(2):
                    if pair:
                        pe.wait_ge(row_copied, 2 * (pair - 1) + g + 1)
                    for t in range(NT):
                        last = pe.transpose(row_ps[g][:, t * P:(t + 1) * P],
                                            logit[:, g * NT + t:g * NT + t + 1].to_broadcast([P, P]), ident[:, :])
                    last.then_inc(row_filled, 1)
                down_weights.matmuls(pe, 1 + 2 * pair)
                pe.wait_ge(chosen, pair + 1)
                pe.matmul(total_ps[:, 0:PT], ones[:, :], expo[:, :], start=True, stop=True).then_inc(total_filled, 1)
                pe.wait_ge(onehot_ready, PT * (pair + 1))
                if pair:
                    pe.wait_ge(fx_copied, pair)
                for c in range(KD):
                    for i in range(PT):
                        last = pe.matmul(fx_ps[:, c * P:(c + 1) * P], y[:, i, c * P:(c + 1) * P], onehot[:, i, :],
                                         start=(i == 0), stop=(i == PT - 1))
                last.then_inc(gathered, 1)
                for half in range(2):
                    if pair:
                        pe.wait_ge(turn_copied, 2 * (pair - 1) + half + 1)
                    for i in range(NT):
                        last = pe.transpose(turn_ps[half][:, i * P:(i + 1) * P], onehot[:, half * NT + i, :],
                                            ident[:, :])
                    last.then_inc(turned, 1)
                if pair == 0:
                    down_weights.matmuls(pe, 2)
            pe.wait_ge(fx_copied, 2)
            pe.wait_ge(ffn_loaded, 16)
            pe.wait_ge(w2_loaded, 16)
            pe.wait_ge(down_weights.signed, KF)
            for f in range(KH):
                if f >= 2:
                    pe.wait_ge(hidden_ready, f - 1)
                for c in range(KD):
                    last = pe.matmul(hidden_ps[f % 2][:, 0:4 * TOPK], ffn_w1[:, c, f * P:(f + 1) * P], fx_t[:, c, :],
                                     start=(c == 0), stop=(c == KD - 1))
                last.then_inc(hidden_filled, 1)
            for r in range(2):
                for f in range(KH):
                    if r == 0:
                        pe.wait_ge(hidden_ready, f + 1)
                    last = pe.matmul(row_ps[r][:, :], hidden_t[:, f, r * P:(r + 1) * P], ffn_w2[:, f, :],
                                     start=(f == 0), stop=(f == KH - 1))
                last.then_inc(out_filled, 1)
            pe.wait_ge(turn_copied, 4)
            for tile in range(T):
                pe.wait_ge(out_ready, tile // PT + 1)
                if tile >= 2:
                    pe.wait_ge(x_updated, tile - 1)
                pe.matmul(turn_ps[tile % 2][:, :], onehot_t[:, tile, :], picks_out[:, tile // PT, :],
                          start=True, stop=True).then_inc(scattered, 1)

        @block.scalar
        def _(act):
            layernorm_stats(None, act, x_res, stats, mean_var, std, rstd, ln_sems)[1]()
            act.dma_start(ffn_w2[:, :, :], d["ffn_w2"]).then_inc(w2_loaded, 16)
            down_weights.sign(act, 0)
            for pair in range(2):
                act.wait_ge(max_ready, pair + 1)
                act.wait_ge(logit_ready, pair + 1)
                for g in range(2):
                    act.activation(expo[:, g * NT:(g + 1) * NT], logit[:, g * NT:(g + 1) * NT], ACT.Exp,
                                   bias=neg_max[:, g:g + 1]).then_inc(exp_done, 1)
                down_weights.sign(act, 1 + 2 * pair)
                if pair == 0:
                    down_weights.sign(act, 2)
            act.wait_ge(loaded, 16 * LOADS)
            for f in range(KH):
                act.wait_ge(hidden_filled, f + 1)
                act.activation(hidden_t[:, f, :], hidden_ps[f % 2][:, 0:4 * TOPK], ACT.Gelu, bias=b1[:, f:f + 1]
                               ).then_inc(hidden_ready, 1)

        @block.vector
        def _(dve):
            layernorm_stats(dve, None, x_res, stats, mean_var, std, rstd, ln_sems)[0]()
            dve.wait_ge(loaded, 16 * LOADS)
            for pair in range(2):
                if pair:
                    dve.wait_ge(gathered, pair)
                    dve.wait_ge(y_added, pair * PT)
                for i in range(PT):
                    tile = pair * PT + i
                    dve.tensor_scalar(y[:, i, :], x_res[:, tile, :], mean_var[:, tile, 0:1], rstd[:, tile:tile + 1],
                                      ALU.subtract, ALU.mult).then_inc(y_ready, 1)
                for i in range(PT):
                    n = pair * PT + i
                    dve.wait_ge(y_ready, n + 1)
                    if i == 0 and pair:
                        dve.wait_ge(count_done, 2 * PT * pair)
                    if i >= 2:
                        dve.wait_ge(dot_done, n - 1)
                    dve.tensor_tensor_reduce(scratch[:, i % 2, :], y[:, i, :], wr_row[:, :], 1.0, 0.0,
                                             ALU.mult, ALU.add, dots[:, i:i + 1]).then_inc(dot_done, 1)
                dve.wait_ge(dot_done, PT * (pair + 1))
                if pair:
                    dve.wait_ge(exp_done, 2 * pair)
                    dve.wait_ge(row_filled, 2 * pair)
                    dve.wait_ge(onehot_ready, PT * pair)
                dve.tensor_scalar(logit[:, :], dots[:, :], br[:, 0:1], None, ALU.add).then_inc(logit_ready, 1)
                for g in range(2):
                    dve.wait_ge(row_filled, 2 * pair + g + 1)
                    dve.tensor_copy(logit_row[:, g, :], row_ps[g][:, :]).then_inc(row_copied, 1)
                    dve.wait_ge(row_copied, 2 * pair + g + 1)
                dve.tensor_reduce(neg_max[:, :], logit_row[:, :, :], AX.X, ALU.max, negate=True
                                  ).then_inc(max_ready, 1)
                dve.wait_ge(logit_ready, pair + 1)
                for i in range(PT):
                    for side, (mask, op) in enumerate(((before, ALU.is_ge), (not_before, ALU.is_gt))):
                        n = (pair * PT + i) * 2 + side
                        if n % (2 * PT) >= 2:
                            dve.wait_ge(count_done, n - 1)
                        dve.scalar_tensor_tensor(scratch[:, side, :], logit_row[:, i // NT, :], logit[:, i:i + 1],
                                                 mask[:, i % NT, :], op, ALU.mult,
                                                 accum_out=above[:, side, i:i + 1]).then_inc(count_done, 1)
                dve.wait_ge(count_done, 2 * PT * (pair + 1))
                dve.tensor_tensor(rank[:, :], above[:, 0, :], above[:, 1, :], ALU.add).then_inc(rank_ready, 1)
                dve.wait_ge(rank_ready, pair + 1)
                if pair:
                    dve.wait_ge(turned, 2 * pair)
                for i in range(PT):
                    dve.tensor_scalar(onehot[:, i, :], slots[:, i // NT, :], rank[:, i:i + 1], None, ALU.is_equal
                                      ).then_inc(onehot_ready, 1)
                dve.tensor_scalar(picked[:, :], rank[:, :], float(TOPK), None, ALU.is_lt).then_inc(total_step, 1)
                dve.wait_ge(total_step, pair * 4 + 1)
                dve.wait_ge(exp_done, 2 * pair + 2)
                dve.tensor_tensor(expo[:, :], expo[:, :], picked[:, :], ALU.mult).then_inc(chosen, 1)
                dve.wait_ge(total_filled, pair + 1)
                dve.tensor_reduce(total[:, :], total_ps[:, 0:PT].rearrange("p (g t) -> p g t", g=2), AX.X, ALU.add
                                  ).then_inc(total_step, 1)
                dve.wait_ge(total_step, pair * 4 + 2)
                dve.reciprocal(rtotal[:, :], total[:, :]).then_inc(total_step, 1)
                dve.wait_ge(total_step, pair * 4 + 3)
                for g in range(2):
                    at = (2 * pair + g) * NT
                    w = dve.tensor_scalar(weight[:, at:at + NT], expo[:, g * NT:(g + 1) * NT], rtotal[:, g:g + 1],
                                          None, ALU.mult)
                w.then_inc(total_step, 1)
                dve.wait_ge(gathered, pair + 1)
                dve.tensor_copy(fx_t[:, :, pair * P:(pair + 1) * P],
                                fx_ps[:, :].rearrange("p (c r) -> p c r", c=KD)).then_inc(fx_copied, 1)
                for half in range(2):
                    dve.wait_ge(turned, 2 * pair + half + 1)
                    at = pair * PT + half * NT
                    dve.tensor_copy(onehot_t[:, at:at + NT, :], turn_ps[half][:, :].rearrange(
                        "p (t n) -> p t n", t=NT)).then_inc(turn_copied, 1)
            for r in range(2):
                dve.wait_ge(out_filled, r + 1)
                dve.tensor_tensor(picks_out[:, r, :], row_ps[r][:, :], b2_row[:, :], ALU.add).then_inc(out_ready, 1)
            dve.wait_ge(total_step, 8)
            dve.wait_ge(y_added, T)
            for tile in range(T):
                dve.wait_ge(scattered, tile + 1)
                dve.scalar_tensor_tensor(x_res[:, tile, :], turn_ps[tile % 2][:, :], weight[:, tile:tile + 1],
                                         x_res[:, tile, :], ALU.mult, ALU.add).then_inc(x_updated, 1)


def cross_attention_step(nc, sem, d, x_res, ident, next_stats):
    with ExitStack() as outer:
        F32R = mybir.dt.float32r
        HIGH, LOW = 0, 1
        keep = lambda name, shape, dt=F32: outer.enter_context(nc.sbuf_tensor(name, shape, dt))
        XP = XH // 2
        q_w = keep("x_q_w", [P, KD, XH * XR])
        o_split = [keep("x_o_high", [P, XH, D], F32R), keep("x_o_low", [P, XH, D], F32R)]
        kr_w = keep("x_kr_w", [P, XH * XR])
        kv_t = keep("x_kv_t", [P, B, N])
        mean_var, rstd = keep("x_mean_var", [P, T, 2]), keep("x_rstd", [P, T])

        with ExitStack() as ctx:
            sb = lambda name, shape: ctx.enter_context(nc.sbuf_tensor(name, shape, F32))
            ps = lambda name, shape: ctx.enter_context(nc.psum_tensor(name, shape, F32))
            wq = sb("x_wq", [P, 2, XH, P])
            latent = sb("x_latent", [P, XH, XR])
            kckv = sb("x_kckv", [P, XH, P])
            stats, std = sb("x_stats", [P, T, 6]), sb("x_std", [P, T])
            wo_t = sb("x_wo_t", [P, 8, D])
            swapped_t = sb("x_swapped_t", [P, B, N])
            cos_t, sin_t = sb("x_cos_t", [P, N]), sb("x_sin_t", [P, N])
            mm_ps = [ps(f"x_mm_ps{i}", [P, N]) for i in range(4)]
            ctx_loaded, rope_step = sem("x_ctx_loaded"), sem("x_rope_step")
            ln_sems = [sem("x_stats_done"), sem("x_var_done"), sem("x_std_done"), sem("x_rstd_done")]
            a_loaded, q_loaded = sem("x_a_loaded"), [sem(f"x_q_loaded{i}") for i in range(2)]
            o_loaded = [sem(f"x_o_loaded{i}") for i in range(2)]
            filled, copied = sem("x_filled"), sem("x_copied")
            o_high, o_low = sem("x_o_high_done"), sem("x_o_low_done")
            block = ctx.enter_context(nc.Block())
            QP = KD * 2
            wo_v = d["wo"]
            LOADS = 7

            @block.sync
            def _(sp):
                sp.dma_start(latent[:, :, :], d["latent"]).then_inc(a_loaded, 16)

                def load_q(c):
                    sp.dma_start(wq[:, c % 2, :, :], d["wq"][:, :, c * P:(c + 1) * P]).then_inc(q_loaded[c % 2], 16)

                def load_o(n):
                    at = 4 * (n % 2)
                    sp.dma_start(wo_t[:, at:at + 4, :], wo_v[:, 4 * n:4 * n + 4, :]).then_inc(o_loaded[n % 2], 16)

                load_q(0)
                load_q(1)
                load_o(0)
                for c in range(2, KD):
                    sp.wait_ge(filled, 2 * (c - 1))
                    load_q(c)
                load_o(1)
                for n in range(2, XH // 4):
                    sp.wait_ge(filled, QP + 4 * (n - 1))
                    load_o(n)

            @block.gpsimd
            def _(pool):
                steps = 0

                def step(ins):
                    nonlocal steps
                    steps += 1
                    ins.then_inc(rope_step, 1)
                    pool.wait_ge(rope_step, steps)

                pool.wait_ge(ctx_loaded, 16 * LOADS)
                for b in range(B):
                    step(pool.tensor_tensor(kv_t[:, b, :], kv_t[:, b, :], cos_t[:, :], ALU.mult))
                    step(pool.tensor_tensor(swapped_t[:, b, :], swapped_t[:, b, :], sin_t[:, :], ALU.mult))
                    step(pool.tensor_tensor(kv_t[:, b, :], kv_t[:, b, :], swapped_t[:, b, :], ALU.add))

            @block.tensor
            def _(pe):
                use = 0

                def begin():
                    if 4 <= use < QP + 4:
                        pe.wait_ge(copied, use - 3)
                    return mm_ps[use % 4]

                pe.wait_ge(a_loaded, 16)
                for c in range(KD):
                    pe.wait_ge(q_loaded[c % 2], 16 * (c // 2 + 1))
                    for half in range(2):
                        out = begin()
                        for i in range(8):
                            h = half * 8 + i
                            last = pe.matmul(out[:, i * XR:(i + 1) * XR], wq[:, c % 2, h, :],
                                             latent[:, h, :], start=True, stop=True)
                        last.then_inc(filled, 1)
                        use += 1
                pe.wait_ge(ctx_loaded, 16 * LOADS)
                for h in range(XH):
                    out = begin()
                    pe.wait_ge(o_loaded[h // 4 % 2], 16 * (h // 8 + 1))
                    if h >= 4:
                        pe.wait_ge(o_low, h - 3)
                    pe.matmul(out[:, :], kckv[:, h, :], wo_t[:, h % 8, :], start=True, stop=True).then_inc(filled, 1)
                    use += 1

            @block.scalar
            def _(act):
                H = F_IN // 2
                ctx_t_v = d["ctx_t"].rearrange("b f n -> f b n")
                for dst, src in ((kv_t[:, :, :], ctx_t_v), (swapped_t[0:H, :, :], ctx_t_v[H:F_IN]),
                                 (swapped_t[H:F_IN, :, :], ctx_t_v[0:H]), (cos_t[:, :], d["cos_t"]),
                                 (sin_t[:, :], d["sin_t"]),
                                 (kr_w[:, :].rearrange("p (h r) -> p h r", h=XH), d["wkr"]),
                                 (kckv[:, :, :], d["kckv"])):
                    act.dma_start(dst, src).then_inc(ctx_loaded, 16)
                layernorm_stats(None, act, x_res, stats, mean_var, std, rstd, ln_sems)[1]()
                for h in range(XH):
                    use = QP + h
                    act.wait_ge(filled, use + 1)
                    act.activation(o_split[HIGH][:, h, :], mm_ps[use % 4][:, :], ACT.Copy).then_inc(o_high, 1)

            @block.vector
            def _(dve):
                layernorm_stats(dve, None, x_res, stats, mean_var, std, rstd, ln_sems)[0]()
                use = 0
                for c in range(KD):
                    for half in range(2):
                        dve.wait_ge(filled, use + 1)
                        dve.tensor_copy(q_w[:, c, half * N:(half + 1) * N], mm_ps[use % 4][:, :]).then_inc(copied, 1)
                        use += 1
                for h in range(XH):
                    dve.wait_ge(o_high, h + 1)
                    dve.tensor_tensor(o_split[LOW][:, h, :], mm_ps[use % 4][:, :],
                                      o_split[HIGH][:, h, :].bitcast(F32), ALU.subtract).then_inc(o_low, 1)
                    use += 1

        with ExitStack() as ctx:
            sb = lambda name, shape, dt=F32: ctx.enter_context(nc.sbuf_tensor(name, shape, dt))
            ps = lambda name, shape: ctx.enter_context(nc.psum_tensor(name, shape, F32))
            NE = 4
            expo = sb("x_expo", [P, NE, N])
            y_t = sb("x_y_t", [P, KD, N])
            kv_now = sb("x_kv_now", [P, N])
            kv_split = [sb("x_kv_high", [P, NT, F_IN], F32R), sb("x_kv_low", [P, NT, F_IN], F32R)]
            kq_split = [sb("x_kq_high", [P, 2, 2, N], F32R), sb("x_kq_low", [P, 2, 2, N], F32R)]
            neg_max, sums, rsums = sb("x_neg_max", [P, 8]), sb("x_sums", [P, 8]), sb("x_rsums", [P, 8])
            probs_split = [sb("x_probs_high", [P, 2, NT, N], F32R), sb("x_probs_low", [P, 2, NT, N], F32R)]
            LS = 3
            latent_split = [sb("x_latent_high", [P, LS, N], F32R), sb("x_latent_low", [P, LS, N], F32R)]
            score_ps = [ps(f"x_score_ps{i}", [P, N]) for i in range(2)]
            turn_ps = [ps(f"x_turn_ps{i}", [P, N]) for i in range(2)]
            latent_ps, out_ps = ps("x_latent_ps", [P, N]), ps("x_out_ps", [P, D])
            project_ps = [ps(f"x_project_ps{i}", [P, N]) for i in range(2)]
            PRODUCTS = ((HIGH, LOW), (LOW, HIGH), (HIGH, HIGH))

            y_ready, kv_ready = sem("x_y_ready"), sem("x_kv_ready")
            turned, turn_high, turn_free = sem("x_turned"), sem("x_turn_high"), sem("x_turn_free")
            projected, project_free = sem("x_projected"), sem("x_project_free")
            kq_high = sem("x_kq_high")
            scored, max_ready, exp_done = sem("x_scored"), sem("x_max_ready"), sem("x_exp_done")
            rsum_ready, probs_ready = sem("x_rsum_ready"), sem("x_probs_ready")
            latent_filled, latent_high, latent_free = sem("x_latent_filled"), sem("x_latent_high"), sem("x_latent_free")
            out_filled, out_free = sem("x_out_filled"), sem("x_out_free")
            stats_done = sem("x_next_stats_done")

            TILES = XH * NT
            PT = 2 * NT
            USES = NT + TILES
            KQ = 2 * XP
            OUTS = XP * NT
            LU = 1 + XH
            OUT_STEPS = (2, 3, 5, 6)
            LAG = 3
            STEPS = TILES + 2 * NT

            def output_at(i):
                pair, step = i // PT - 2, i % PT
                return (pair, OUT_STEPS.index(step)) if pair >= 0 and step in OUT_STEPS else None

            def keys_at(i):
                if i == 0:
                    return 1
                return (i // PT + 2) if i % PT == PT - 1 and i // PT + 2 < XP else None

            block = ctx.enter_context(nc.Block())

            @block.tensor
            def _(pe):
                def turn_y(b, t):
                    pe.wait_ge(turn_free, b * USES + t + 1)
                    pe.wait_ge(y_ready, b * NT + t + 1)
                    for c in range(KD):
                        last = pe.transpose(turn_ps[t % 2][:, c * P:(c + 1) * P], expo[:, t, c * P:(c + 1) * P],
                                            ident[:, :])
                    last.then_inc(turned, 1)

                def keys(b, pair, count):
                    pe.wait_ge(kv_ready, b + 1)
                    pe.wait_ge(project_free, count + 1)
                    pe.matmul(project_ps[0][:, :], kr_w[:, pair * P:(pair + 1) * P],
                              kv_now[:, :], start=True, stop=True).then_inc(projected, 1)

                def queries(pair, c, count):
                    if c == 0:
                        pe.wait_ge(project_free, count + 1)
                    q = pe.matmul(project_ps[1][:, :], q_w[:, c, pair * P:(pair + 1) * P], y_t[:, c, :],
                                  start=(c == 0), stop=(c == KD - 1))
                    if c == KD - 1:
                        q.then_inc(projected, 1)

                def first_pair(b, count):
                    keys(b, 0, count)
                    pe.wait_ge(turn_free, b * USES + NT + 2)
                    for c in range(KD):
                        queries(0, c, count + 1)

                def graph(b, final):
                    pe.wait_ge(latent_free, b * LU + 1)
                    for k in range(NT):
                        last = pe.transpose(latent_ps[:, k * P:(k + 1) * P], kv_now[:, k * P:(k + 1) * P], ident[:, :])
                    last.then_inc(latent_filled, 1)
                    for i in range(STEPS):
                        if i < TILES:
                            h, t = i // NT, i % NT
                            half = slice((h % 2) * XR, (h % 2 + 1) * XR)
                            if i % PT == 0:
                                pe.wait_ge(project_free, b * KQ + 2 * (i // PT) + 2 + 2)
                            pe.wait_ge(exp_done, b * TILES + i + 1)
                            for n, (q, k) in enumerate(PRODUCTS):
                                last = pe.matmul(score_ps[i % 2][:, :],
                                                 kq_split[q][half, h // 2 % 2, 1, t * P:(t + 1) * P],
                                                 kq_split[k][half, h // 2 % 2, 0, :], start=(n == 0), stop=(n == 2))
                            last.then_inc(scored, 1)
                            pair, step = i // PT + 1, i % PT
                            if pair < XP and 1 <= step < 1 + KD:
                                queries(pair, step - 1, b * KQ + 2 * pair + 1)
                            if keys_at(i):
                                keys(b, keys_at(i), b * KQ + 2 * keys_at(i))
                        if 0 <= i - LAG < TILES:
                            n = i - LAG
                            pe.wait_ge(turn_free, b * USES + NT + n + 1)
                            pe.wait_ge(probs_ready, b * TILES + n + 1)
                            for c in range(NT):
                                last = pe.transpose(turn_ps[n % 2][:, c * P:(c + 1) * P],
                                                    expo[:, n % NE, c * P:(c + 1) * P], ident[:, :])
                            last.then_inc(turned, 1)
                        if i >= 2 * NT and i % NT < 2:
                            h, ks = (i - 2 * NT) // NT, ((0, 1), (2, 3))[i % NT]
                            if 0 in ks:
                                pe.wait_ge(turn_free, b * USES + NT + h * NT + NT + 2)
                                pe.wait_ge(latent_free, b * LU + 1 + h + 1)
                            for k in ks:
                                for n, (w, p) in enumerate(PRODUCTS):
                                    last = pe.matmul(latent_ps[:, :], kv_split[w][:, k, :],
                                                     probs_split[p][:, h % 2, k, :], start=(k == 0 and n == 0),
                                                     stop=(k == NT - 1 and n == 2))
                            if NT - 1 in ks:
                                last.then_inc(latent_filled, 1)
                        if not final and 0 <= i - TILES - LAG < NT:
                            turn_y(b + 1, i - TILES - LAG)
                        if output_at(i):
                            output(b, *output_at(i))
                    if not final:
                        first_pair(b + 1, (b + 1) * KQ)
                    for t in range(NT):
                        output(b, XP - 1, t)

                def output(b, pair, t):
                    pe.wait_ge(latent_free, b * LU + 1 + 2 * pair + 2 + 1)
                    pe.wait_ge(out_free, b * OUTS + pair * NT + t + 1)
                    for i, h in enumerate((2 * pair, 2 * pair + 1)):
                        for n, (v, w) in enumerate(PRODUCTS):
                            last = pe.matmul(out_ps[:, :], latent_split[v][:, h % LS, t * P:(t + 1) * P],
                                             o_split[w][:, h, :], start=(i == 0 and n == 0), stop=(i == 1 and n == 2))
                    last.then_inc(out_filled, 1)

                pe.sem_inc(latent_filled, 2)
                pe.sem_inc(out_filled, 2 * NT)
                for t in range(NT):
                    turn_y(0, t)
                first_pair(0, 0)
                with pe.Fori(0, B - 1) as b:
                    graph(b, final=False)
                graph(B - 1, final=True)

            @block.scalar
            def _(act):
                def kq_highs(count, parity, which):
                    act.wait_ge(projected, count + 1)
                    act.activation(kq_split[HIGH][:, parity, which, :], project_ps[which][:, :], ACT.Copy
                                   ).then_inc(kq_high, 1)

                def graph(b, final):
                    act.wait_ge(turned, b * USES + NT)
                    act.wait_ge(latent_filled, b * LU + 1 + 2)
                    act.activation(kv_split[HIGH][:, :, :], latent_ps[:, :].rearrange("p (k f) -> p k f", k=NT),
                                   ACT.Copy).then_inc(latent_high, 1)
                    for i in range(STEPS):
                        if i < TILES:
                            act.wait_ge(max_ready, b * TILES + i + 1)
                            act.activation(expo[:, i % NE, :], score_ps[i % 2][:, :], ACT.Exp,
                                           bias=neg_max[:, i % 8:i % 8 + 1], accum_out=sums[:, i % 8:i % 8 + 1]
                                           ).then_inc(exp_done, 1)
                        pair, step = i // PT + 1, i % PT
                        if pair < XP and step in (1, 5):
                            kq_highs(b * KQ + 2 * pair + (step == 5), pair % 2, int(step == 5))
                        n = i - LAG
                        if 0 <= n < TILES:
                            h, t = n // NT, n % NT
                            act.wait_ge(turned, b * USES + NT + n + 1)
                            if t == 0:
                                act.wait_ge(latent_filled, b * LU + h + 2)
                            act.activation(probs_split[HIGH][:, h % 2, :, t * P:(t + 1) * P],
                                           turn_ps[n % 2][:, :].rearrange("p (k n) -> p k n", k=NT), ACT.Copy
                                           ).then_inc(turn_high, 1)
                        if i >= 2 * NT and i % NT == 2:
                            h = i // NT - 2
                            act.wait_ge(out_filled, b * OUTS + (h - LS) // 2 * NT + NT + 2 * NT)
                            act.wait_ge(latent_filled, b * LU + 1 + h + 1 + 2)
                            act.activation(latent_split[HIGH][:, h % LS, :], latent_ps[:, :], ACT.Copy
                                           ).then_inc(latent_high, 1)
                    if not final:
                        for which in range(2):
                            kq_highs((b + 1) * KQ + which, 0, which)

                act.sem_inc(exp_done, 2)
                for which in range(2):
                    kq_highs(which, 0, which)
                with act.Fori(0, B - 1) as b:
                    graph(b, final=False)
                graph(B - 1, final=True)

            @block.vector
            def _(dve):
                def normed(b, t):
                    dve.tensor_scalar(expo[:, t, :], x_res[:, bass.ds(b * NT + t, 1), :].rearrange("p a c -> p (a c)"),
                                      mean_var[:, bass.ds(b * NT + t, 1), 0], rstd[:, bass.ds(b * NT + t, 1)],
                                      ALU.subtract, ALU.mult).then_inc(y_ready, 1)

                def y_copy(b, t):
                    dve.wait_ge(turned, b * USES + t + 1)
                    dve.tensor_copy(y_t[:, :, t * P:(t + 1) * P], turn_ps[t % 2][:, :].rearrange(
                        "p (c n) -> p c n", c=KD)).then_inc(turn_free, 1)

                def kv_copy(b):
                    dve.tensor_copy(kv_now[:, :], kv_t[:, bass.ds(b, 1), :].rearrange("p a n -> p (a n)")
                                    ).then_inc(kv_ready, 1)

                def kq_lows(count, parity, which):
                    dve.wait_ge(kq_high, count + 1)
                    dve.tensor_tensor(kq_split[LOW][:, parity, which, :], project_ps[which][:, :],
                                      kq_split[HIGH][:, parity, which, :].bitcast(F32), ALU.subtract
                                      ).then_inc(project_free, 1)

                def graph(b, final):
                    for i in range(STEPS):
                        if i and output_at(i - 1):
                            update(b, *output_at(i - 1))
                        if final and PT <= i < PT + T - NT:
                            statistics(i - PT)
                        if i < TILES:
                            dve.wait_ge(scored, b * TILES + i + 1)
                            dve.tensor_reduce(neg_max[:, i % 8:i % 8 + 1], score_ps[i % 2][:, :], AX.X, ALU.max,
                                              negate=True).then_inc(max_ready, 1)
                        if 1 <= i <= TILES:
                            n = i - 1
                            dve.wait_ge(exp_done, b * TILES + n + 1 + 2)
                            dve.reciprocal(rsums[:, n % 8:n % 8 + 1], sums[:, n % 8:n % 8 + 1]).then_inc(rsum_ready, 1)
                            dve.wait_ge(rsum_ready, b * TILES + n + 1)
                            dve.tensor_scalar(expo[:, n % NE, :], expo[:, n % NE, :], rsums[:, n % 8:n % 8 + 1], None,
                                              ALU.mult).then_inc(probs_ready, 1)
                        if i >= 2 * NT and i % NT == 3:
                            h = i // NT - 2
                            dve.wait_ge(latent_high, b * LU + 1 + h + 1)
                            dve.tensor_tensor(latent_split[LOW][:, h % LS, :], latent_ps[:, :],
                                              latent_split[HIGH][:, h % LS, :].bitcast(F32), ALU.subtract
                                              ).then_inc(latent_free, 1)
                        if i == 1:
                            dve.wait_ge(latent_high, b * LU + 1)
                            dve.tensor_tensor(kv_split[LOW][:, :, :], latent_ps[:, :].rearrange(
                                "p (k f) -> p k f", k=NT), kv_split[HIGH][:, :, :].bitcast(F32), ALU.subtract
                                ).then_inc(latent_free, 1)
                        pair, step = i // PT + 1, i % PT
                        if pair < XP and step in (1, 5):
                            which = int(step == 5)
                            kq_lows(b * KQ + 2 * pair + which, pair % 2, which)
                        n = i - LAG - 1
                        if 0 <= n < TILES:
                            h, t = n // NT, n % NT
                            at = slice(t * P, (t + 1) * P)
                            dve.wait_ge(turn_high, b * TILES + n + 1)
                            dve.tensor_tensor(probs_split[LOW][:, h % 2, :, at],
                                              turn_ps[n % 2][:, :].rearrange("p (k n) -> p k n", k=NT),
                                              probs_split[HIGH][:, h % 2, :, at].bitcast(F32), ALU.subtract
                                              ).then_inc(turn_free, 1)
                        if not final and i == TILES - 1:
                            kv_copy(b + 1)
                        if not final and 0 <= i - TILES < NT:
                            t = i - TILES
                            dve.wait_ge(turned, b * USES + USES - NT + t + 1)
                            normed(b + 1, t)
                        if not final and 0 <= i - TILES - LAG - 1 < NT:
                            y_copy(b + 1, i - TILES - LAG - 1)
                    if not final:
                        for which in range(2):
                            kq_lows((b + 1) * KQ + which, 0, which)
                    for t in range(NT):
                        update(b, XP - 1, t)
                        if final:
                            dve.wait_ge(out_free, b * OUTS + (XP - 1) * NT + t + 1 + 1)
                            statistics(b * NT + t)

                def statistics(tile):
                    dve.bn_stats(next_stats[:, tile, :], x_res[:, tile, :]).then_inc(stats_done, 1)

                def update(b, pair, t):
                    dve.wait_ge(out_filled, b * OUTS + pair * NT + t + 1 + 2 * NT)
                    x_tile = x_res[:, bass.ds(b * NT + t, 1), :].rearrange("p a c -> p (a c)")
                    dve.tensor_tensor(x_tile, x_tile, out_ps[:, :], ALU.add).then_inc(out_free, 1)

                dve.sem_inc(turn_free, 2)
                dve.sem_inc(project_free, 2)
                dve.sem_inc(latent_free, 1)
                dve.sem_inc(out_free, 1)
                kv_copy(0)
                for t in range(NT):
                    normed(0, t)
                for t in range(NT):
                    y_copy(0, t)
                for which in range(2):
                    kq_lows(which, 0, which)
                with dve.Fori(0, B - 1) as b:
                    graph(b, final=False)
                graph(B - 1, final=True)


def gated_ffn_step(nc, sem, d, x_res, ident, stats, out):
    F32R = mybir.dt.float32r
    with ExitStack() as ctx:
        sb = lambda name, shape, dt=F32: ctx.enter_context(nc.sbuf_tensor(name, shape, dt))
        ps = lambda name, shape: ctx.enter_context(nc.psum_tensor(name, shape, F32))
        mean_var = sb("f_mean_var", [P, T, 2])
        std, rstd = sb("f_std", [P, T]), sb("f_rstd", [P, T])
        hadamard, su_up = sb("f_hadamard", [P, P]), sb("f_su_up", [P, KD])
        scales = sb("f_scales", [P, 2, KF])
        scale_now = sb("f_scale_now", [P, 2, 2])
        y, y_t, half_t = sb("f_y", [P, NT, D]), sb("f_y_t", [P, KD, N]), sb("f_half_t", [P, KD, N])
        mixed = [sb("f_mixed_high", [P, B, KD, N], F32R), sb("f_mixed_low", [P, B, KD, N], F32R)]
        WCOLS = 2 * KD * P + D
        raw = sb("f_raw", [P, 2, WCOLS])
        split = [sb("f_w_high", [P, 2, WCOLS], F32R), sb("f_w_low", [P, 2, WCOLS], F32R)]
        silu, z = sb("f_silu", [P, 2, N]), sb("f_z", [P, 2, N])
        z_split = [sb("f_z_high", [P, 2, N], F32R), sb("f_z_low", [P, 2, N], F32R)]
        turn_ps = [ps(f"f_turn_ps{i}", [P, N]) for i in range(2)]
        gate_ps = [ps(f"f_gate_ps{i}", [P, N]) for i in range(2)]
        up_ps = [ps(f"f_up_ps{i}", [P, N]) for i in range(2)]
        down_ps = [ps(f"f_down_ps{i}", [P, N]) for i in range(2)]
        HIGH, LOW = 0, 1
        PRODUCTS = ((HIGH, LOW), (LOW, HIGH), (HIGH, HIGH))

        small_loaded, scales_ready = sem("f_small_loaded"), sem("f_scales_ready")
        raw_loaded = [sem("f_raw_loaded0"), sem("f_raw_loaded1")]
        w_high, w_ready = sem("f_w_high"), sem("f_w_ready")
        ln_sems = [sem("f_stats_done"), sem("f_var_done"), sem("f_std_done"), sem("f_rstd_done")]
        y_ready, turned, y_copied = sem("f_y_ready"), sem("f_turned"), sem("f_y_copied")
        mix_step, mixed_filled = sem("f_mix_step"), sem("f_mixed_filled")
        mixed_high, mixed_ready = sem("f_mixed_high"), sem("f_mixed_ready")
        gate_filled, up_filled, silu_ready = sem("f_gate_filled"), sem("f_up_filled"), sem("f_silu_ready")
        z_ready, z_high, z_low = sem("f_z_ready"), sem("f_z_high"), sem("f_z_low")
        down_filled, down_free, stored = sem("f_down_filled"), sem("f_down_free"), sem("f_stored")
        block = ctx.enter_context(nc.Block())

        LOOPS = (KF - 2) // 2

        @block.sync
        def _(sp):
            for dst, src in ((hadamard[:, :], d["hadamard"]), (su_up[:, :], d["su_up"]),
                             (scales[:, 0, :], d["gate_scale"]), (scales[:, 1, :], d["up_scale"])):
                sp.dma_start(dst, src).then_inc(small_loaded, 16)

            def load(g, i):
                static = isinstance(g, int)
                if not static or g >= 2:
                    sp.wait_ge(w_ready, g - 1)
                ug = d["up_gate"][:, g, :] if static else d["up_gate"][:, bass.ds(g, 1), :].rearrange(
                    "p a n -> p (a n)")
                dn = d["down"][:, g, :] if static else d["down"][:, bass.ds(g, 1), :].rearrange("p a n -> p (a n)")
                sp.dma_start(raw[:, i, 0:2 * KD * P], ug).then_inc(raw_loaded[i], 16)
                sp.dma_start(raw[:, i, 2 * KD * P:WCOLS], dn).then_inc(raw_loaded[i], 16)

            load(0, 0)
            load(1, 1)
            with sp.Fori(0, LOOPS) as i:
                load(2 * i + 2, 0)
                load(2 * i + 3, 1)
            out_v = out.rearrange("b (t p) c -> b p t c", p=P)
            for b in range(B):
                sp.wait_ge(down_free, ((KF - 1) * B + b + 1) * NT + 2)
                sp.dma_start(out_v[b], x_res[:, b * NT:(b + 1) * NT, :]).then_inc(stored, 16)
            sp.wait_ge(stored, 16 * B)

        @block.gpsimd
        def _(pool):
            def weights_low(g, i):
                pool.wait_ge(w_high, 3 * g + 3)
                third = WCOLS // 3
                for n in range(3):
                    cols = slice(n * third, (n + 1) * third)
                    last = pool.tensor_tensor(split[LOW][:, i, cols], raw[:, i, cols],
                                              split[HIGH][:, i, cols].bitcast(F32), ALU.subtract)
                last.then_inc(w_ready, 1)

            def chunk(g, i, more=True):
                for b in range(B):
                    s = g * B + b
                    pool.wait_ge(z_high, s + 1)
                    pool.tensor_tensor(z_split[LOW][:, b % 2, :], z[:, b % 2, :],
                                       z_split[HIGH][:, b % 2, :].bitcast(F32), ALU.subtract).then_inc(z_low, 1)
                    if b == 2 and more:
                        weights_low(g + 1, 1 - i)

            pool.sem_inc(z_low, 2)
            weights_low(0, 0)
            chunk(0, 0)
            with pool.Fori(0, LOOPS) as i:
                chunk(2 * i + 1, 1)
                chunk(2 * i + 2, 0)
            chunk(KF - 1, 1, more=False)

        @block.tensor
        def _(pe):
            def turns(b):
                pe.wait_ge(y_ready, b * NT + NT)
                for c in range(KD):
                    if c >= 2:
                        pe.wait_ge(y_copied, b * KD + c - 1)
                    elif b:
                        pe.wait_ge(mixed_ready, (b - 1) * KD + c + 3)
                    for t in range(NT):
                        last = pe.transpose(turn_ps[c % 2][:, t * P:(t + 1) * P], y[:, t, c * P:(c + 1) * P],
                                            ident[:, :])
                    last.then_inc(turned, 1)

            def mix(b):
                pe.wait_ge(mix_step, b * 4 + 4)
                for c in range(KD):
                    if c < 2:
                        pe.wait_ge(y_copied, b * KD + c + 3)
                    else:
                        pe.wait_ge(mixed_ready, b * KD + c - 1)
                    pe.matmul(turn_ps[c % 2][:, :], hadamard[:, :], y_t[:, c, :], start=True, stop=True
                              ).then_inc(mixed_filled, 1)

            def up_gate(g, i, b, first=False):
                s = g * B + b
                if first:
                    pe.wait_ge(mixed_ready, (b + 1) * KD)
                if b == 0:
                    pe.wait_ge(w_ready, g + 1)
                for which, (target, filled, free) in enumerate(((gate_ps, gate_filled, silu_ready),
                                                                (up_ps, up_filled, z_ready))):
                    pe.wait_ge(free, s + 1)
                    n = 0
                    for c in range(KD):
                        at = (which * KD + c) * P
                        for w, m in PRODUCTS:
                            last = pe.matmul(target[b % 2][:, :], split[w][:, i, at:at + P], mixed[m][:, b, c, :],
                                             start=(n == 0), stop=(n == 3 * KD - 1))
                            n += 1
                    last.then_inc(filled, 1)

            def down(g, i, b):
                s = g * B + b
                pe.wait_ge(z_low, s + 1 + 2)
                for t in range(NT):
                    pe.wait_ge(down_free, s * NT + t + 1)
                    for n, (w, m) in enumerate(PRODUCTS):
                        last = pe.matmul(down_ps[t % 2][:, :], z_split[w][:, b % 2, t * P:(t + 1) * P],
                                         split[m][:, i, 2 * KD * P:WCOLS], start=(n == 0), stop=(n == 2))
                    last.then_inc(down_filled, 1)

            pe.sem_inc(down_filled, 2 * NT)
            pe.wait_ge(small_loaded, 64)
            turns(0)
            mix(0)
            turns(1)
            for b in range(B):
                up_gate(0, 0, b, first=True)
                if b + 1 < B:
                    mix(b + 1)
                if b + 2 < B:
                    turns(b + 2)
                if b:
                    down(0, 0, b - 1)

            def chunk(g, i):
                up_gate(g, i, 0)
                down(g - 1, 1 - i, B - 1)
                for b in range(1, B):
                    up_gate(g, i, b)
                    down(g, i, b - 1)

            with pe.Fori(0, LOOPS) as i:
                chunk(2 * i + 1, 1)
                chunk(2 * i + 2, 0)
            chunk(KF - 1, 1)
            down(KF - 1, 1, B - 1)

        @block.scalar
        def _(act):
            def weights_high(g, i, loads):
                act.wait_ge(raw_loaded[i], 32 * loads)
                if not isinstance(g, int) or g >= 2:
                    act.wait_ge(down_filled, (g - 1) * B * NT + 2 * NT)
                third = WCOLS // 3
                for n in range(3):
                    cols = slice(n * third, (n + 1) * third)
                    act.activation(split[HIGH][:, i, cols], raw[:, i, cols], ACT.Copy).then_inc(w_high, 1)

            def turned_copies(b):
                for c in range(KD):
                    act.wait_ge(turned, b * KD + c + 1)
                    act.activation(y_t[:, c, :], turn_ps[c % 2][:, :], ACT.Copy, scale=su_up[:, c:c + 1]
                                   ).then_inc(y_copied, 1)

            def mixed_highs(b):
                for c in range(KD):
                    act.wait_ge(mixed_filled, b * KD + c + 1)
                    act.activation(mixed[HIGH][:, b, c, :], turn_ps[c % 2][:, :], ACT.Copy).then_inc(mixed_high, 1)

            def hidden(g, i, b):
                s = g * B + b
                if b == 0:
                    act.wait_ge(scales_ready, g + 2)
                act.wait_ge(gate_filled, s + 1)
                act.wait_ge(z_ready, s + 1)
                act.activation(silu[:, b % 2, :], gate_ps[b % 2][:, :], ACT.Silu, scale=scale_now[:, i, 0:1]
                               ).then_inc(silu_ready, 1)
                act.wait_ge(z_ready, s + 1 + 2)
                act.wait_ge(down_filled, s * NT + NT)
                act.activation(z_split[HIGH][:, b % 2, :], z[:, b % 2, :], ACT.Copy).then_inc(z_high, 1)

            act.sem_inc(silu_ready, 2)
            layernorm_stats(None, act, x_res, stats, mean_var, std, rstd, ln_sems, have_stats=True)[1]()
            act.wait_ge(small_loaded, 64)
            turned_copies(0)
            weights_high(0, 0, 1)
            mixed_highs(0)
            turned_copies(1)
            for b in range(B):
                if b + 1 < B:
                    mixed_highs(b + 1)
                if b + 2 < B:
                    turned_copies(b + 2)
                hidden(0, 0, b)
                if b == 1:
                    weights_high(1, 1, 1)

            def chunk(g, i, loads, more=True):
                for b in range(B):
                    hidden(g, i, b)
                    if b == 1 and more:
                        weights_high(g + 1, 1 - i, loads)

            with act.Fori(0, LOOPS) as i:
                chunk(2 * i + 1, 1, i + 2)
                chunk(2 * i + 2, 0, i + 2)
            chunk(KF - 1, 1, 0, more=False)

        @block.vector
        def _(dve):
            dve.sem_inc(z_ready, 2)
            dve.sem_inc(down_free, 2)
            layernorm_stats(dve, None, x_res, stats, mean_var, std, rstd, ln_sems, have_stats=True)[0]()
            dve.wait_ge(small_loaded, 64)
            dve.tensor_scalar(scales[:, :, :], scales[:, :, :], float(D) ** -0.5, None, ALU.mult
                              ).then_inc(scales_ready, 1)

            def normed(b):
                if b:
                    dve.wait_ge(turned, b * KD)
                for t in range(NT):
                    tile = b * NT + t
                    dve.tensor_scalar(y[:, t, :], x_res[:, tile, :], mean_var[:, tile, 0:1], rstd[:, tile:tile + 1],
                                      ALU.subtract, ALU.mult).then_inc(y_ready, 1)

            def butterflies(b):
                dve.wait_ge(y_copied, b * KD + KD)
                done = b * 4
                for step, source, target in ((1, y_t, half_t), (2, half_t, y_t)):
                    halves = lambda m: m[:, :, :].rearrange("p (a two s) n -> p a two (s n)", two=2, s=step)
                    s, t = halves(source), halves(target)
                    dve.tensor_tensor(t[:, :, 0], s[:, :, 0], s[:, :, 1], ALU.add).then_inc(mix_step, 1)
                    dve.tensor_tensor(t[:, :, 1], s[:, :, 0], s[:, :, 1], ALU.subtract).then_inc(mix_step, 1)
                    done += 2
                    dve.wait_ge(mix_step, done)

            def mixed_lows(b):
                for c in range(KD):
                    dve.wait_ge(mixed_high, b * KD + c + 1)
                    dve.tensor_tensor(mixed[LOW][:, b, c, :], turn_ps[c % 2][:, :],
                                      mixed[HIGH][:, b, c, :].bitcast(F32), ALU.subtract).then_inc(mixed_ready, 1)

            def hidden(g, i, b):
                s = g * B + b
                if b == 0:
                    now = scales[:, :, g:g + 1] if isinstance(g, int) else scales[:, :, bass.ds(g, 1)]
                    dve.wait_ge(scales_ready, g + 1)
                    dve.tensor_copy(scale_now[:, i, :], now.rearrange("p k a -> p (k a)")).then_inc(scales_ready, 1)
                    dve.wait_ge(scales_ready, g + 2)
                dve.wait_ge(silu_ready, s + 1 + 2)
                dve.wait_ge(up_filled, s + 1)
                dve.wait_ge(z_low, s + 1)
                dve.scalar_tensor_tensor(z[:, b % 2, :], up_ps[b % 2][:, :], scale_now[:, i, 1:2], silu[:, b % 2, :],
                                         ALU.mult, ALU.mult).then_inc(z_ready, 1)

            def update(g, b):
                s = g * B + b
                for t in range(NT):
                    dve.wait_ge(down_filled, s * NT + t + 1 + 2 * NT)
                    dve.tensor_tensor(x_res[:, b * NT + t, :], x_res[:, b * NT + t, :], down_ps[t % 2][:, :],
                                      ALU.add).then_inc(down_free, 1)

            normed(0)
            butterflies(0)
            normed(1)
            mixed_lows(0)
            butterflies(1)
            for b in range(B):
                if b + 2 < B:
                    normed(b + 2)
                if b + 1 < B:
                    mixed_lows(b + 1)
                hidden(0, 0, b)
                if b + 2 < B:
                    butterflies(b + 2)
                if b:
                    update(0, b - 1)

            def chunk(g, i):
                hidden(g, i, 0)
                update(g - 1, B - 1)
                for b in range(1, B):
                    hidden(g, i, b)
                    update(g, b - 1)

            with dve.Fori(0, LOOPS) as i:
                chunk(2 * i + 1, 1)
                chunk(2 * i + 2, 0)
            chunk(KF - 1, 1)
            update(KF - 1, B - 1)


def build(nc, a, out):
    with ExitStack() as ctx:
        sem = lambda name: ctx.enter_context(nc.semaphore(name))
        x_res = ctx.enter_context(nc.sbuf_tensor("x_res", [P, T, D], F32))
        ident = ctx.enter_context(nc.sbuf_tensor("ident", [P, P], F32))
        next_stats = ctx.enter_context(nc.sbuf_tensor("next_stats", [P, T, 6], F32))
        ident_ready = sem("ident_ready")
        down_turned = nc.dram_tensor("down_turned", (P, KF, D), F32, kind="Internal").ap()
        q_latent = nc.dram_tensor("q_latent", (P, XH, XR), F32, kind="Internal").ap()
        down_mixed = nc.dram_tensor("down_mixed", (P, KF, D), F32, kind="Internal").ap()
        with ExitStack() as ffn:
            ffn_w1 = ffn.enter_context(nc.sbuf_tensor("ffn_w1", [P, KD, DFF], F32))
            ffn_loaded = sem("ffn_loaded")
            with nc.Block() as block:
                @block.sync
                def _(sp):
                    sp.dma_start(ident[:, :], a["ident"]).then_inc(ident_ready, 16)

            gat_step(nc, sem, dict(x=a["x"], ctx_t=a["ctx_t"], W0=a["gat_w0"], W1=a["gat_w1"],
                                   a_self0=a["L0_xattn_a_self0"], a_neigh0=a["L0_xattn_a_neigh0"],
                                   a_self1=a["L0_xattn_a_self1"], a_neigh1=a["L0_xattn_a_neigh1"],
                                   b0=a["L0_xattn_b0"], b1=a["L0_xattn_b1"], ffn_w1=a["ffn_w1"],
                                   down_t=a["down_t"], down_turned=down_turned,
                                   kcq=a["kcq"], wqr=a["wqr"], q_latent=q_latent),
                     x_res, ident, ident_ready, ffn_w1, ffn_loaded)
            routed_ffn_step(nc, sem, dict(Wr=a["L0_ffn_Wr"], br=a["L0_ffn_br"], b1=a["ffn_b1"], b2=a["L0_ffn_b2"],
                                          before=a["before"], not_before=a["not_before"], slots=a["slots"],
                                          ones=a["ones"], hadamard=a["hadamard"], su_down=a["su_down"],
                                          ffn_w2=a["ffn_w2"], down_scale=a["L1_ffn_Wscale_dp"], down_turned=down_turned),
                            x_res, ident, ffn_w1, ffn_loaded, down_mixed)
        cross_attention_step(nc, sem, dict(wq=a["wq"], latent=q_latent,
                                           wo=a["wo"], kckv=a["kckv"], wkr=a["wkr"],
                                           ctx_t=a["ctx_t"],
                                           cos_t=a["cos_t"], sin_t=a["sin_t"]), x_res, ident, next_stats)
        gated_ffn_step(nc, sem, dict(up_gate=a["up_gate"], down=down_mixed, hadamard=a["hadamard"],
                                     su_up=a["su_up"], up_scale=a["up_scale"], gate_scale=a["gate_scale"]),
                       x_res, ident, next_stats, out)


def laid_out(i):
    import numpy as np

    def columns(v):
        return v.reshape(-1, P).T

    def swap(v, *axes):
        return i[v].transpose(axes)

    def chunked(m):
        return m.reshape(-1, P, *m.shape[1:]).swapaxes(0, 1)

    up_gate = np.stack([chunked(swap(n, 1, 0)).reshape(P, KD, KF, P) for n in ("L1_ffn_W_gate", "L1_ffn_W_up")])
    up_gate = up_gate.transpose(1, 3, 0, 2, 4).reshape(P, KF, 2 * KD * P)
    names = ["x", "L0_xattn_b0", "L0_xattn_b1", "L0_xattn_a_self0", "L0_xattn_a_neigh0", "L0_xattn_a_self1", "L0_xattn_a_neigh1",
             "L0_ffn_Wr", "L0_ffn_br", "L0_ffn_b2", "L1_ffn_Wscale_dp"]
    return {**{n: i[n] for n in names}, "ctx_t": swap("ctx_512", 0, 2, 1),
            "gat_w0": swap("L0_xattn_W0", 1, 0, 2).reshape(F_IN, -1),
            "gat_w1": chunked(swap("L0_xattn_W1", 1, 0, 2).reshape(D, -1)),
            "ffn_w1": chunked(i["L0_ffn_W1"]), "ffn_w2": chunked(i["L0_ffn_W2"]), "ffn_b1": columns(i["L0_ffn_b1"]),
            "kcq": chunked(swap("L1_xattn_w_kc_q", 2, 0, 1)), "wqr": chunked(swap("L1_xattn_W_qr", 1, 0, 2)),
            "wq": chunked(i["L1_xattn_Wq"]), "wo": chunked(swap("L1_xattn_Wo", 1, 0)),
            "kckv": swap("L1_xattn_w_kc_kv", 1, 0, 2), "wkr": swap("L1_xattn_W_kr", 1, 0, 2),
            "up_gate": up_gate,
            "down_t": chunked(swap("L1_ffn_W_down", 1, 0)),
            "su_up": columns(i["L1_ffn_SU_ug"]), "su_down": columns(i["L1_ffn_SU_dp"]),
            "up_scale": columns(i["L1_ffn_Wscale_ug"][:DFF]), "gate_scale": columns(i["L1_ffn_Wscale_ug"][DFF:])}


def constants():
    import numpy as np
    f32 = np.float32
    row, column = np.arange(N).reshape(NT, P).T[:, :, None], np.arange(N)[None, None, :]
    slots = np.full((P, 2, P), -1.0, f32)
    for g in range(2):
        slots[:, g, g * TOPK:(g + 1) * TOPK] = np.arange(TOPK)
    inv_freq = f32(1.0) / f32(10000.0) ** (np.arange(0, F_IN, 2, dtype=f32) / f32(F_IN))
    freqs = np.arange(N, dtype=f32)[:, None] * inv_freq[None, :]
    cos = np.repeat(np.cos(freqs), 2, axis=-1)
    sin = np.repeat(np.sin(freqs), 2, axis=-1)
    sin[:, :F_IN // 2] *= f32(-1.0)
    hadamard = np.ones((1, 1), f32)
    while hadamard.shape[0] < P:
        hadamard = np.block([[hadamard, hadamard], [hadamard, -hadamard]])
    return {"cos_t": np.ascontiguousarray(cos.T), "sin_t": np.ascontiguousarray(sin.T), "hadamard": hadamard,
            "ident": np.eye(P, dtype=f32), "ones": np.ones((P, P), f32), "slots": slots,
            "before": (column < row).astype(f32), "not_before": (column >= row).astype(f32)}


def kernel(**inputs):
    import numpy as np
    import concourse.bacc as bacc
    from concourse.bass_utils import run_bass_kernel_spmd as run

    nc = bacc.Bacc("TRN2", target_bir_lowering=False, num_devices=1)
    arrays = {name: np.ascontiguousarray(v) for name, v in laid_out(inputs).items()}
    arrays.update(constants())
    a = {name: nc.dram_tensor(f"in_{name}", v.shape, F32, kind="ExternalInput").ap() for name, v in arrays.items()}
    out = nc.dram_tensor("out", (B, N, D), F32, kind="ExternalOutput").ap()
    build(nc, a, out)
    r = run(nc, [{f"in_{name}": v for name, v in arrays.items()}], core_ids=[0])
    return r.results[0]["out"]
```
